# Optimizing a Trainium2 kernel written in Bass

```python
import numpy as np
import jax
import jax.numpy as jnp

def _softmax(x, axis=-1):
    return jax.nn.softmax(x, axis=axis)

def _gelu(x):
    return jax.nn.gelu(x, approximate=True)

def _silu(x):
    return jax.nn.silu(x)

def _sigmoid(x):
    return jax.nn.sigmoid(x)

def _layernorm(x, axis=-1, eps=1e-05):
    m = jnp.mean(x, axis=axis, keepdims=True)
    v = jnp.var(x, axis=axis, keepdims=True)
    return (x - m) / jnp.sqrt(v + eps)

def _scatter_add(tgt, idx, src, axis=0):
    return tgt.at[idx].add(src)

def _segment_sum(src, seg, n):
    return jax.ops.segment_sum(src, seg, n)
kernel_name = 'mk_gnn_preln_d2_gnn_r8_2c24c1'

def setup_inputs(seed: int=0):
    np.random.seed(seed)
    _w = jnp.asarray

    def _rec_inputs():
        import jax
        import jax.numpy as jnp
        _gk = jax.random.key(seed)
        x = -8.776e-05 + 1 * jax.random.normal(jax.random.fold_in(_gk, 1), (6250, 256), jnp.float32)
        _s = jax.random.randint(jax.random.fold_in(_gk, 2), (50000,), 0, 6250, jnp.int32)
        _d = jax.random.randint(jax.random.fold_in(_gk, 3), (50000,), 0, 6250, jnp.int32)
        _loop = jnp.arange(6250, dtype=jnp.int32)
        src = jnp.concatenate([_s, _d, _loop])
        dst = jnp.concatenate([_d, _s, _loop])
        _o = jnp.argsort(dst, stable=True)
        src = src[_o]
        dst = dst[_o]
        edge_attr_256 = 2.93046e-05 + 1.00006 * jax.random.normal(jax.random.fold_in(_gk, 11), (106250, 256), jnp.float32)
        edge_weight = jax.random.uniform(jax.random.fold_in(_gk, 13), (106250,), jnp.float32, 0.0, 0.999998)
        return (x, src, dst, edge_attr_256, edge_weight)
    x, src, dst, edge_attr_256, edge_weight = _rec_inputs()

    def _L0_gnn_setup():
        import jax, jax.numpy as jnp
        import numpy as np
        N, E, D = (2500, 40000, 256)
        H, C = (8, 32)
        key = jax.random.key(seed)
        ks = jax.random.split(key, 12)
        s = 1.0 / np.sqrt(D)
        return {'x': jax.random.normal(ks[0], (N, D), jnp.float32), 'edge_index': jax.random.randint(ks[1], (2, E), 0, N, jnp.int64), 'edge_attr': jax.random.normal(ks[2], (E, D), jnp.float32), 'Wq': jax.random.normal(ks[3], (D, H * C), jnp.float32) * s, 'bq': jnp.zeros((H * C,), jnp.float32), 'Wk': jax.random.normal(ks[4], (D, H * C), jnp.float32) * s, 'bk': jnp.zeros((H * C,), jnp.float32), 'Wv': jax.random.normal(ks[5], (D, H * C), jnp.float32) * s, 'bv': jnp.zeros((H * C,), jnp.float32), 'We': jax.random.normal(ks[6], (D, H * C), jnp.float32) * s, 'Ws': jax.random.normal(ks[7], (D, H * C), jnp.float32) * s, 'bs': jnp.zeros((H * C,), jnp.float32)}
    _L0_gnn_all = _L0_gnn_setup()
    _L0_gnn_in = {k: v for k, v in _L0_gnn_all.items() if k in ('Wq', 'bq', 'Wk', 'bk', 'Wv', 'bv', 'We', 'Ws', 'bs')}
    del _L0_gnn_all

    def _L1_gnn_setup():
        import jax, jax.numpy as jnp
        import numpy as np
        MIN_NORM = 1e-15
        BALL_EPS = 1e-05
        C = 1.0
        N_NODES, N_EDGES, D_IN, D_OUT = (5000, 40000, 256, 256)

        def _sqnorm(x):
            return jnp.sum(x * x, axis=-1, keepdims=True)

        def _norm(x):
            return jnp.maximum(jnp.sqrt(_sqnorm(x)), MIN_NORM)

        def _artanh(x):
            return jnp.arctanh(jnp.clip(x, -1.0 + 1e-07, 1.0 - 1e-07))

        def _lam(x, c):
            return jnp.maximum(2.0 / jnp.maximum(1.0 - c * _sqnorm(x), MIN_NORM), MIN_NORM)

        def mobius_add(x, y, c):
            x2, y2 = (_sqnorm(x), _sqnorm(y))
            xy = jnp.sum(x * y, axis=-1, keepdims=True)
            num = (1.0 + 2.0 * c * xy + c * y2) * x + (1.0 - c * x2) * y
            den = 1.0 + 2.0 * c * xy + c * c * x2 * y2
            return num / jnp.maximum(den, MIN_NORM)

        def expmap0(u, c):
            sc = jnp.sqrt(c)
            un = _norm(u)
            return jnp.tanh(sc * un) * u / (sc * un)

        def logmap0(p, c):
            sc = jnp.sqrt(c)
            pn = _norm(p)
            return _artanh(sc * pn) * p / (sc * pn)

        def expmap(u, base, c):
            sc = jnp.sqrt(c)
            un = _norm(u)
            second = jnp.tanh(sc * _lam(base, c) * un / 2.0) * u / (sc * un)
            return mobius_add(base, second, c)

        def logmap(p, base, c):
            sub = mobius_add(-base, p, c)
            sn = _norm(sub)
            sc = jnp.sqrt(c)
            return 2.0 / (sc * _lam(base, c)) * _artanh(sc * sn) * sub / sn

        def mobius_matvec(W, x, c):
            sc = jnp.sqrt(c)
            xn = _norm(x)
            mx = x @ W.T
            mxn = _norm(mx)
            res = jnp.tanh(mxn / xn * _artanh(sc * xn)) * mx / (mxn * sc)
            is_zero = jnp.all(mx == 0.0, axis=-1, keepdims=True)
            return jnp.where(is_zero, jnp.zeros_like(res), res)

        def project(x, c):
            n = _norm(x)
            maxn = (1.0 - BALL_EPS) / jnp.sqrt(c)
            return jnp.where(n > maxn, x / n * maxn, x)
        key = jax.random.key(seed)
        k1, k2, k3, k4, k5 = jax.random.split(key, 5)
        x_tan = 0.2 * jax.random.normal(k1, (N_NODES, D_IN), jnp.float32)
        x = project(expmap0(x_tan, C), C)
        bound = 0.05 * float(np.sqrt(6.0 / (D_IN + D_OUT)))
        weight = jax.random.uniform(k2, (D_OUT, D_IN), jnp.float32, -bound, bound)
        bias = 0.01 * jax.random.normal(k3, (D_OUT,), jnp.float32)
        edge_index = jax.random.randint(k4, (2, N_EDGES), 0, N_NODES, dtype=jnp.int32)
        edge_weight = jax.random.uniform(k5, (N_EDGES,), jnp.float32)
        return {'x': x, 'weight': weight, 'bias': bias, 'edge_index': edge_index, 'edge_weight': edge_weight}
    _L1_gnn_all = _L1_gnn_setup()
    _L1_gnn_in = {k: v for k, v in _L1_gnn_all.items() if k in ('weight', 'bias')}
    del _L1_gnn_all
    return {'x': x, 'src': src, 'dst': dst, 'edge_attr_256': edge_attr_256, 'edge_weight': edge_weight, 'L0_gnn_Wq': _L0_gnn_in['Wq'], 'L0_gnn_bq': _L0_gnn_in['bq'], 'L0_gnn_Wk': _L0_gnn_in['Wk'], 'L0_gnn_bk': _L0_gnn_in['bk'], 'L0_gnn_Wv': _L0_gnn_in['Wv'], 'L0_gnn_bv': _L0_gnn_in['bv'], 'L0_gnn_We': _L0_gnn_in['We'], 'L0_gnn_Ws': _L0_gnn_in['Ws'], 'L0_gnn_bs': _L0_gnn_in['bs'], 'L1_gnn_weight': _L1_gnn_in['weight'], 'L1_gnn_bias': _L1_gnn_in['bias']}

def reference(x, src, dst, edge_attr_256, edge_weight, L0_gnn_Wq, L0_gnn_bq, L0_gnn_Wk, L0_gnn_bk, L0_gnn_Wv, L0_gnn_bv, L0_gnn_We, L0_gnn_Ws, L0_gnn_bs, L1_gnn_weight, L1_gnn_bias):
    import jax
    import jax.numpy as jnp

    def _L0_gnn_ref(x, edge_index, edge_attr, Wq, bq, Wk, bk, Wv, bv, We, Ws, bs):
        import jax, jax.numpy as jnp
        import numpy as np
        N, E, D = (2500, 40000, 256)
        H, C = (8, 32)
        n = x.shape[0]
        src, dst = (edge_index[0], edge_index[1])
        q = (x @ Wq + bq).reshape(n, H, C)
        k = (x @ Wk + bk).reshape(n, H, C)
        v = (x @ Wv + bv).reshape(n, H, C)
        e = (edge_attr @ We).reshape(-1, H, C)
        kj = k[src] + e
        alpha = jnp.einsum('ehc,ehc->eh', q[dst], kj) / jnp.sqrt(jnp.float32(C))
        amax = jax.ops.segment_max(alpha, dst, num_segments=n)
        ea = jnp.exp(alpha - amax[dst])
        denom = jax.ops.segment_sum(ea, dst, num_segments=n)
        alpha = ea / (denom[dst] + 1e-16)
        msg = (v[src] + e) * alpha[:, :, None]
        out = jax.ops.segment_sum(msg, dst, num_segments=n)
        out = out.reshape(n, H * C) + (x @ Ws + bs)
        return out

    def _L1_gnn_ref(x, weight, bias, edge_index, edge_weight):
        import jax, jax.numpy as jnp
        import numpy as np
        MIN_NORM = 1e-15
        BALL_EPS = 1e-05
        C = 1.0
        N_NODES, N_EDGES, D_IN, D_OUT = (5000, 40000, 256, 256)

        def _sqnorm(x):
            return jnp.sum(x * x, axis=-1, keepdims=True)

        def _norm(x):
            return jnp.maximum(jnp.sqrt(_sqnorm(x)), MIN_NORM)

        def _artanh(x):
            return jnp.arctanh(jnp.clip(x, -1.0 + 1e-07, 1.0 - 1e-07))

        def _lam(x, c):
            return jnp.maximum(2.0 / jnp.maximum(1.0 - c * _sqnorm(x), MIN_NORM), MIN_NORM)

        def mobius_add(x, y, c):
            x2, y2 = (_sqnorm(x), _sqnorm(y))
            xy = jnp.sum(x * y, axis=-1, keepdims=True)
            num = (1.0 + 2.0 * c * xy + c * y2) * x + (1.0 - c * x2) * y
            den = 1.0 + 2.0 * c * xy + c * c * x2 * y2
            return num / jnp.maximum(den, MIN_NORM)

        def expmap0(u, c):
            sc = jnp.sqrt(c)
            un = _norm(u)
            return jnp.tanh(sc * un) * u / (sc * un)

        def logmap0(p, c):
            sc = jnp.sqrt(c)
            pn = _norm(p)
            return _artanh(sc * pn) * p / (sc * pn)

        def expmap(u, base, c):
            sc = jnp.sqrt(c)
            un = _norm(u)
            second = jnp.tanh(sc * _lam(base, c) * un / 2.0) * u / (sc * un)
            return mobius_add(base, second, c)

        def logmap(p, base, c):
            sub = mobius_add(-base, p, c)
            sn = _norm(sub)
            sc = jnp.sqrt(c)
            return 2.0 / (sc * _lam(base, c)) * _artanh(sc * sn) * sub / sn

        def mobius_matvec(W, x, c):
            sc = jnp.sqrt(c)
            xn = _norm(x)
            mx = x @ W.T
            mxn = _norm(mx)
            res = jnp.tanh(mxn / xn * _artanh(sc * xn)) * mx / (mxn * sc)
            is_zero = jnp.all(mx == 0.0, axis=-1, keepdims=True)
            return jnp.where(is_zero, jnp.zeros_like(res), res)

        def project(x, c):
            n = _norm(x)
            maxn = (1.0 - BALL_EPS) / jnp.sqrt(c)
            return jnp.where(n > maxn, x / n * maxn, x)
        c = jnp.float32(C)
        N = x.shape[0]
        src, dst = (edge_index[0], edge_index[1])
        x_src = x[src]
        x_dst = x[dst]
        msg = logmap(x_src, x_dst, c)
        msg = msg * edge_weight[:, None]
        agg = jax.ops.segment_sum(msg, dst, num_segments=N)
        u = expmap(agg, x, c)
        h = mobius_matvec(weight, u, c)
        b_ball = expmap0(jnp.broadcast_to(bias, h.shape), c)
        h = mobius_add(h, b_ball, c)
        h_tan = jax.nn.relu(logmap0(h, c))
        h = expmap0(h_tan, c)
        return project(h, c)
    edge_index = jnp.stack([src, dst])
    h = jnp.maximum(_layernorm(x, axis=-1), 0.0)
    x = x + _L0_gnn_ref(h, edge_index, edge_attr_256, L0_gnn_Wq, L0_gnn_bq, L0_gnn_Wk, L0_gnn_bk, L0_gnn_Wv, L0_gnn_bv, L0_gnn_We, L0_gnn_Ws, L0_gnn_bs)
    h = jnp.maximum(_layernorm(x, axis=-1), 0.0)
    x = x + _L1_gnn_ref(h, L1_gnn_weight, L1_gnn_bias, edge_index, edge_weight)
    return x

_drawn_inputs = setup_inputs


def setup_inputs(seed=0):
    import zlib

    import numpy as np

    out = dict(_drawn_inputs(seed))
    spreads = {'L0_gnn_bq': (0.0, 0.1),
     'L0_gnn_bk': (0.0, 0.8),
     'L0_gnn_bv': (0.0, 0.1),
     'L0_gnn_bs': (0.0, 0.1)}
    factors = {'edge_weight': 8.0, 'L1_gnn_weight': 5.125, 'L1_gnn_bias': 8.0}
    for name, (base, spread) in spreads.items():
        noise = np.random.default_rng([zlib.crc32(name.encode()), seed]).standard_normal(out[name].shape)
        drawn = base * np.exp(spread * noise) if base else spread * noise
        out[name] = jnp.asarray(drawn.astype(out[name].dtype))
    for name, factor in factors.items():
        out[name] = (out[name] * factor).astype(out[name].dtype)
    return out
```

```python
import concourse.bass as bass
import concourse.mybir as mybir
import numpy as np
from contextlib import ExitStack

F32 = mybir.dt.float32
I32 = mybir.dt.int32
ALU = mybir.AluOpType
ACT = mybir.ActivationFunctionType
AX = mybir.AxisListType

P = 128
N, E, D = 6250, 106250, 256
H, C = 8, 32
CE = C + 1
BLOCKS = -(-N // P)
TAIL = N - (BLOCKS - 1) * P
TILES = -(-E // P)
LAST = E - (TILES - 1) * P
S = 16
BATCHES = -(-(TILES + BLOCKS - 1) // S)
STEPS = BATCHES * S
COLS = -(-STEPS // P)
SPAD = COLS * P
NFLAG = 4 * P + 1
CH = 2 * S + 2
BIG = 1.0e30
HALF = D // P
EA_SLOTS = 4
KV_SLOTS = 8
LN_EPS = 1e-5
MIN_NORM = 1e-15
BALL_EPS = 1e-5
CLIP = float(np.float32(1.0 - 1e-7))
PACK = 4
GROUP = 7


class Round:

    def __init__(self, m, a):
        self.m, self.a = m, a

    def at(self, per, k=0):
        return per * self.a + k if self.m is None else self.m * (2 * per) + (per * self.a + k)


    def half(self, per, k=0):
        return per * (self.a // 2) + k if self.m is None else self.m * per + (per * (self.a // 2) + k)

    def before(self):
        return Round(self.m, self.a - 1)

    def has(self, back):
        return self.m is not None or self.a >= back


def rounds(eng, total, body):
    body(Round(None, 0), 0)
    body(Round(None, 1), 1)
    pairs = (total - 2) // 2
    with eng.Fori(0, pairs) as m:
        body(Round(m, 2), 0)
        body(Round(m, 3), 1)
    if total % 2:
        body(Round(None, total - 1), 0)


def edge_rounds(eng, body):
    body(Round(None, 0), 0, True, False)
    body(Round(None, 1), 1, True, True)
    with eng.Fori(0, (BATCHES - 2) // 2) as m:
        body(Round(m, 2), 0, True, True)
        body(Round(m, 3), 1, True, True)
    body(Round(None, BATCHES - 1), 0, True, True)
    body(Round(None, BATCHES), 1, False, True)


def bcast(ap, n):
    return ap.unsqueeze(2).to_broadcast([ap.shape[0], ap.shape[1], n])


class Line:

    def __init__(self, eng, sem, base=0):
        self.eng, self.sem, self.base, self.n = eng, sem, base, 0

    def __call__(self, ins):
        self.n += 1
        ins.then_inc(self.sem, 1)
        self.eng.wait_ge(self.sem, self.base + self.n)


class Build:
    def __init__(self, nc, a):
        self.nc, self.a = nc, a
        self.scratch()

    def scratch(self):
        nc = self.nc

        def dram(name, shape, dt=F32):
            return nc.dram_tensor(name, shape, dt, kind="Internal").ap()

        self.dstp = dram("dst_tiles", (TILES, P), I32)
        self.srcp = dram("src_tiles", (TILES, P), I32)
        self.wtp = dram("weight_tiles", (TILES, P))
        self.flags = dram("step_flags", (SPAD, H, NFLAG))
        self.ends = dram("step_ends", (SPAD, 5))
        self.kv = dram("kv_rows", (N, 2 * D))
        self.xs = dram("x_rows", (N, D))
        self.h2 = dram("h2_rows", (N, D))


def allocators(nc, ctx):
    def sb(name, shape, dt=F32):
        return ctx.enter_context(nc.sbuf_tensor(name, shape, dt))

    def ps(name, shape, dt=F32):
        return ctx.enter_context(nc.psum_tensor(name, shape, dt))

    def sem(name):
        return ctx.enter_context(nc.semaphore(name))

    return sb, ps, sem


def prep(nc, b, k):
    a = b.a
    with ExitStack() as ctx:
        sb, ps, sem = allocators(nc, ctx)
        tile_last = sb("tile_last", [1, TILES], I32)
        tile_block = sb("tile_block", [1, TILES], I32)
        tile_no = sb("tile_no", [1, TILES], I32)
        start_row = sb("start_row", [1, TILES], F32)
        block_row = sb("block_row", [1, TILES], F32)
        one_row = sb("one_row", [1, P], F32)
        starts = sb("starts", [P, TILES], F32)
        junk = sb("junk", [P, TILES], F32)
        step_no_i = sb("step_no_i", [P, COLS], I32)
        step_no = sb("step_no", [P, COLS], F32)
        tile_of = sb("tile_of", [P, COLS], F32)
        base_of = sb("base_of", [P, COLS], F32)
        dst_g = sb("dst_g", [P, COLS, P], I32)
        src_g = sb("src_g", [P, COLS, P], I32)
        loc = sb("loc", [P, COLS, P], F32)
        src_f = sb("src_f", [P, COLS, P], F32)
        seg = sb("seg", [P, COLS, P], F32)
        flag = sb("flag", [P, COLS, NFLAG], F32)
        dup_i = sb("dup_i", [P, 1], I32)
        dup = sb("dup", [P, 1])
        fill = sb("fill", [P, COLS])
        ends5 = sb("ends5", [P, COLS, 5], F32)
        ends8 = sb("ends8", [H, SPAD, 5], F32)
        neg = sb("neg", [1, P], I32)
        packf = sb("packf", [1, SPAD // PACK], F32)
        iota_i = sb("iota_i", [P, P], I32)
        part_i = sb("part_i", [P, 1], I32)
        part8_i = sb("part8_i", [P, 1], I32)
        partm_i = sb("partm_i", [P, 1], I32)
        part3 = sb("part3", [P, 3], F32)
        p_starts = ps("p_starts", [P, 1024], F32)
        p_tr = ps("p_tr", [P, 2, P], F32)
        tiles_in = sem("tiles_in")
        tables_out = sem("tables_out")
        iotas = sem("iotas")
        dve_line = sem("dve_line")
        row_ready = sem("row_ready")
        starts_up = sem("starts_up")
        tile_of_ready = sem("tile_of_ready")
        gathered = sem("gathered")
        loc_ready = sem("loc_ready")
        turned = sem("turned")
        turned_read = sem("turned_read")
        flags_ready = sem("flags_ready")
        flags_out = sem("flags_out")
        ends_in = sem("ends_in")
        block = ctx.enter_context(nc.Block())

        @block.sync
        def _(sp):
            with nc.allow_non_contiguous_dma(reason="the last edge of each tile"):
                sp.dma_start(tile_last[0:1, 0:TILES - 1],
                             a["dst"][0:(TILES - 1) * P].rearrange("(o t e) -> o t e", o=1, e=P)[:, :, P - 1])\
                    .then_inc(tiles_in, 16)
            sp.dma_start(tile_last[0:1, TILES - 1:TILES],
                         a["dst"][E - 1:E].rearrange("(o e) -> o e", o=1)).then_inc(tiles_in, 16)
            sp.dma_start(dup_i[:, :], a["dst"][E - LAST - 1:E - LAST].partition_broadcast(P)).then_inc(tiles_in, 16)
            for table, name in ((b.dstp, "dst"), (b.srcp, "src")):
                sp.dma_start(table[0:TILES - 1, :],
                             a[name][0:(TILES - 1) * P].rearrange("(t e) -> t e", e=P)).then_inc(tables_out, 16)
            sp.dma_start(b.srcp[TILES - 1:TILES, :],
                         a["src"][E - P:E].rearrange("(o e) -> o e", o=1)).then_inc(tables_out, 16)
            sp.dma_start(b.dstp[TILES - 1:TILES, P - LAST:P],
                         a["dst"][E - LAST:E].rearrange("(o e) -> o e", o=1)).then_inc(tables_out, 16)
            sp.wait_ge(iotas, 1)
            sp.dma_start(b.dstp[TILES - 1:TILES, 0:P - LAST], neg[0:1, 0:P - LAST]).then_inc(tables_out, 16)
            sp.wait_ge(flags_ready, 1)
            for h in range(H):
                sp.dma_start(b.flags[:, h, :].rearrange("(c p) f -> p c f", p=P), flag[:, :, :])\
                    .then_inc(flags_out, 16)
            with nc.allow_non_contiguous_dma(reason="five words for each step"):
                sp.dma_start(b.ends.rearrange("(c p) f -> p c f", p=P), ends5[:, :, :]).then_inc(flags_out, 16)
            sp.wait_ge(flags_out, 16 * (H + 1))
            sp.dma_start(ends8[:, :, :], b.ends.partition_broadcast(H)).then_inc(ends_in, 16)

        @block.gpsimd
        def _(pool):
            nc.gpsimd.memset(neg[:, :], -1).then_inc(iotas, 1)
            nc.gpsimd.iota(tile_no[:, :], [[1, TILES]], base=0, channel_multiplier=0).then_inc(iotas, 1)
            nc.gpsimd.iota(step_no_i[:, :], [[P, COLS]], base=0, channel_multiplier=1).then_inc(iotas, 1)
            nc.gpsimd.iota(iota_i[:, :], [[1, P]], base=0, channel_multiplier=0).then_inc(iotas, 1)
            nc.gpsimd.iota(part_i[:, :], [[0, 1]], base=0, channel_multiplier=1).then_inc(iotas, 1)
            pool.wait_ge(tables_out, 16 * 5)
            pool.wait_ge(tile_of_ready, 1)
            for c in range(COLS):
                for table, to in ((b.dstp, dst_g), (b.srcp, src_g)):
                    pool.indirect_dma_start(
                        out=to[:, c, :], out_offset=None, in_=table,
                        in_offset=bass.IndirectOffsetOnAxis(ap=k.tile_of[:, c:c + 1], axis=0))\
                        .then_inc(gathered, 16)

        @block.vector
        def _(dve):
            line = Line(dve, dve_line)
            dve.wait_ge(iotas, 5)
            line(nc.vector.tensor_copy(k.iota[:, :], iota_i[:, :]))
            line(nc.vector.tensor_copy(part3[:, 0:1], part_i[:, :]))
            line(nc.vector.tensor_single_scalar(part8_i[:, :], part_i[:, :], 3, ALU.arith_shift_right))
            line(nc.vector.tensor_single_scalar(partm_i[:, :], part_i[:, :], H - 1, ALU.bitwise_and))
            line(nc.vector.tensor_copy(part3[:, 1:2], part8_i[:, :]))
            line(nc.vector.tensor_copy(part3[:, 2:3], partm_i[:, :]))
            line(nc.vector.tensor_scalar(k.ident[:, :], k.iota[:, :], part3[:, 0:1], None, ALU.is_equal))
            line(nc.vector.tensor_scalar(k.of_step[:, :], k.iota[:, 0:S], part3[:, 1:2], None, ALU.is_equal))
            line(nc.vector.tensor_scalar(k.of_head[:, :], k.iota[:, 0:H], part3[:, 2:3], None, ALU.is_equal))
            for s in range(S):
                line(nc.vector.tensor_copy(k.head_of[:, s * H:(s + 1) * H], k.ident[0:H, 0:H]))
            line(nc.vector.memset(one_row[:, :], 1.0))
            dve.wait_ge(tiles_in, 48)
            line(nc.vector.tensor_single_scalar(tile_block[:, :], tile_last[:, :], 7, ALU.arith_shift_right))
            line(nc.vector.tensor_copy(block_row[:, :], tile_block[:, :]))
            line(nc.vector.tensor_copy(start_row[:, :], tile_no[:, :]))
            line(nc.vector.tensor_tensor(start_row[0:1, 1:TILES], start_row[0:1, 1:TILES],
                                         block_row[0:1, 0:TILES - 1], ALU.add))
            nc.vector.tensor_copy(step_no[:, :], step_no_i[:, :]).then_inc(row_ready, 1)
            dve.wait_ge(row_ready, 1)
            dve.wait_ge(starts_up, 1)
            line(nc.vector.tensor_copy(starts[:, :], p_starts[:, 0:TILES]))
            for c in range(COLS):
                line(nc.vector.tensor_scalar(junk[:, :], starts[:, :], step_no[:, c:c + 1], 0.0,
                                             ALU.is_le, ALU.add, accum_out=tile_of[:, c:c + 1]))
            line(nc.vector.tensor_scalar(tile_of[:, :], tile_of[:, :], -1.0, float(TILES - 1), ALU.add, ALU.min))
            nc.vector.tensor_copy(k.tile_of[:, :], tile_of[:, :]).then_inc(tile_of_ready, 1)
            line(nc.vector.tensor_tensor(base_of[:, :], step_no[:, :], tile_of[:, :], ALU.subtract))
            line(nc.vector.tensor_scalar(ends5[:, :, 3], base_of[:, :], float(BLOCKS - 1), None, ALU.min))
            line(nc.vector.tensor_scalar(ends5[:, :, 4], tile_of[:, :], float(P), float(E - P), ALU.mult, ALU.min))
            line(nc.vector.tensor_scalar(base_of[:, :], base_of[:, :], float(P), None, ALU.mult))
            dve.wait_ge(gathered, 16 * 2 * COLS)
            line(nc.vector.tensor_copy(loc[:, :, :], dst_g[:, :, :]))
            for c in range(COLS):
                line(nc.vector.tensor_scalar(loc[:, c, :], loc[:, c, :], base_of[:, c:c + 1], None, ALU.subtract))
            nc.vector.tensor_copy(src_f[:, :, :], src_g[:, :, :]).then_inc(loc_ready, 1)
            line(nc.vector.memset(flag[:, :, :], 0.0))
            line(nc.vector.tensor_scalar(seg[:, :, :], loc[:, :, :], -0.5, P - 0.5, ALU.max, ALU.min))
            line(nc.vector.tensor_tensor(flag[:, :, 3 * P + 1:NFLAG], seg[:, :, :], loc[:, :, :], ALU.is_equal))
            line(nc.vector.tensor_copy(dup[:, :], dup_i[:, :]))
            line(nc.vector.tensor_scalar(fill[:, :], tile_of[:, :], float(TILES - 1), dup[:, :], ALU.is_equal, ALU.mult))
            for c in range(COLS):
                line(nc.vector.tensor_copy(seg[:, c, :], dst_g[:, c, :]))
                line(nc.vector.tensor_scalar(seg[:, c, :], seg[:, c, :], fill[:, c:c + 1], base_of[:, c:c + 1],
                                             ALU.max, ALU.subtract))
            line(nc.vector.tensor_scalar(seg[:, :, :], seg[:, :, :], -0.5, P - 0.5, ALU.max, ALU.min))
            line(nc.vector.tensor_copy(ends5[:, :, 2], seg[:, :, 0]))
            for c in range(COLS):
                line(nc.vector.tensor_scalar(seg[:, c, :], seg[:, c, :], base_of[:, c:c + 1], None, ALU.add))
            line(nc.vector.tensor_copy(ends5[:, :, 0], seg[:, :, 0]))
            line(nc.vector.tensor_copy(ends5[:, :, 1], seg[:, :, P - 1]))
            line(nc.vector.tensor_tensor(flag[:, :, 1:P], seg[:, :, 1:P], seg[:, :, 0:P - 1], ALU.is_equal))
            for c in range(COLS):
                line(nc.vector.tensor_scalar(flag[:, c, P + 1:2 * P + 1], seg[:, c, :], seg[:, c, 0:1], None,
                                             ALU.is_equal))
                line(nc.vector.tensor_scalar(flag[:, c, 2 * P + 1:3 * P + 1], seg[:, c, :], seg[:, c, P - 1:P],
                                             None, ALU.is_equal))
            nc.vector.tensor_scalar(flag[:, :, :], flag[:, :, :], BIG, -BIG, ALU.mult, ALU.add)\
                .then_inc(flags_ready, 1)
            for c in range(COLS):
                dve.wait_ge(turned, c + 1)
                line(nc.vector.tensor_copy(k.loc[:, c * P:(c + 1) * P], p_tr[:, 0, :]))
                nc.vector.tensor_copy(k.src[:, c * P:(c + 1) * P], p_tr[:, 1, :]).then_inc(turned_read, 1)
            dve.wait_ge(ends_in, 16)
            chain = k.chain[:, :].rearrange("p (i c) -> p i c", c=CH)
            line(nc.vector.memset(k.chain[:, :], 0.0))
            e5 = ends8[:, 0:STEPS, :]
            line(nc.vector.tensor_tensor(
                chain[:, :, 2:CH - 1:2], e5[:, :, 0].rearrange("p (i s) -> p i s", s=S),
                e5[:, :, 1].rearrange("p (i s) -> p i s", s=S), ALU.is_equal))
            line(nc.vector.tensor_tensor(
                chain[:, :, 3:CH - 1:2], ends8[:, 1:STEPS + 1, 0].rearrange("p (i s) -> p i s", s=S)[:, :, 0:S - 1],
                e5[:, :, 1].rearrange("p (i s) -> p i s", s=S)[:, :, 0:S - 1], ALU.is_equal))
            line(nc.vector.tensor_tensor(
                chain[:, 1:BATCHES, 1], ends8[:, S:STEPS, 0].rearrange("p (i s) -> p i s", s=S)[:, :, 0],
                ends8[:, S - 1:STEPS - 1, 1].rearrange("p (i s) -> p i s", s=S)[:, :, 0], ALU.is_equal))
            line(nc.vector.tensor_scalar(k.chain[:, :], k.chain[:, :], BIG, -BIG, ALU.mult, ALU.add))
            line(nc.vector.tensor_copy(k.straddler[:, :], e5[:, :, 2].rearrange("p (i s) -> p i s", s=S)[:, :, 0]))
            line(nc.vector.tensor_copy(k.row[:, :], ends8[0:1, :, 4]))
            blocks = ends8[0:1, :, 3].rearrange("p (w j) -> p w j", j=PACK)
            line(nc.vector.tensor_copy(packf[:, :], blocks[:, :, PACK - 1]))
            for j in reversed(range(PACK - 1)):
                line(nc.vector.scalar_tensor_tensor(out=packf[:, :], in0=packf[:, :], scalar=64.0,
                                                    in1=blocks[:, :, j], op0=ALU.mult, op1=ALU.add))
            line(nc.vector.tensor_copy(k.packed[:, :], packf[:, :]))

        @block.tensor
        def _(pe):
            pe.wait_ge(row_ready, 1)
            for at in range(0, TILES, 512):
                n = min(512, TILES - at)
                last = nc.tensor.matmul(p_starts[:, at:at + n], one_row[:, :], start_row[0:1, at:at + n],
                                        start=True, stop=True)
            last.then_inc(starts_up, 1)
            pe.wait_ge(loc_ready, 1)
            for c in range(COLS):
                if c:
                    pe.wait_ge(turned_read, c)
                nc.tensor.transpose(p_tr[:, 0, :], loc[:, c, :], k.ident[:, :])
                nc.tensor.transpose(p_tr[:, 1, :], src_f[:, c, :], k.ident[:, :]).then_inc(turned, 1)


def rows_of(r):
    return TAIL if r.m is None and r.a == BLOCKS - 1 else P


def project_nodes(nc, b, k):
    a = b.a
    with ExitStack() as ctx:
        sb, ps, sem = allocators(nc, ctx)
        w = sb("w_qkvs", [P, HALF, 4 * D])
        bias = sb("bias_qkvs", [P, 4, D])
        x = sb("x_blk", [P, 2, D])
        carrier = sb("wait_carrier", [1, 2])
        six = sb("six", [P, 2, 6])
        mv = sb("mv", [P, 2, 2])
        sd = sb("sd", [P, 2, 1])
        rs = sb("rs", [P, 2, 1])
        nm = sb("nm", [P, 2, 1])
        h = sb("h_blk", [P, 2, D])
        ht = sb("ht_blk", [P, 2, D])
        kvs = sb("kv_stage", [P, 2, 2 * D])
        xo = sb("xo_stage", [P, 2, D])
        p_ht = ps("p_ht", [P, 2, D])
        p_qk = ps("p_qk", [P, 2, 2 * D])
        p_vs = ps("p_vs", [P, 2, 2 * D])
        w_in = sem("w_in")
        x_in = [sem(f"x_in{z}") for z in range(2)]
        out_done = [sem(f"kv_out{z}") for z in range(2)]
        line_sem = sem("proj_dve_line")
        var_ready, sd_ready, norm_ready = sem("var_ready"), sem("sd_ready"), sem("norm_ready")
        h_ready, turned, ht_ready = sem("h_ready"), sem("h_turned"), sem("ht_ready")
        projected, staged, setup = sem("projected"), sem("staged"), sem("proj_setup")
        block = ctx.enter_context(nc.Block())
        scale = 1.0 / float(np.sqrt(np.float32(C)))

        @block.sync
        def _(sp):
            for i, name in enumerate(("Wq", "Wk", "Wv", "Ws")):
                sp.dma_start(w[:, :, i * D:(i + 1) * D],
                             a[f"L0_gnn_{name}"].rearrange("(c p) n -> p c n", p=P)).then_inc(w_in, 16)
            for i, name in enumerate(("bq", "bk", "bv", "bs")):
                sp.dma_start(bias[:, i, :], a[f"L0_gnn_{name}"].partition_broadcast(P)).then_inc(w_in, 16)

            def store(r, z):
                n = rows_of(r)
                sp.wait_ge(staged, r.at(1, 1))
                sp.dma_start(b.kv[bass.ds(r.at(P), n), :], kvs[0:n, z, :]).then_inc(out_done[z], 16)
                sp.dma_start(b.xs[bass.ds(r.at(P), n), :], xo[0:n, z, :]).then_inc(out_done[z], 16)

            def body(r, z):
                n = rows_of(r)
                if r.has(2):
                    sp.wait_ge(staged, r.at(1, -1))
                sp.dma_start(x[0:n, z, :], a["x"][bass.ds(r.at(P), n), :]).then_inc(x_in[z], 16)
                if r.has(1):
                    store(r.before(), 1 - z)

            rounds(sp, BLOCKS, body)
            store(Round(None, BLOCKS - 1), 0)
            sp.wait_ge(out_done[0], 32 * 25)
            sp.wait_ge(out_done[1], 32 * 24)

        @block.vector
        def _(dve):
            per = 7
            dve.wait_ge(w_in, 16 * 8)
            nc.vector.tensor_scalar(bias[:, 0, :], bias[:, 0, :], scale, None, ALU.mult).then_inc(setup, 1)
            dve.wait_ge(setup, 1)
            lines = {}

            def evacuate(r, z):
                line = lines["line"]
                dve.wait_ge(projected, r.at(1, 1))
                q = k.big2[:, bass.ds(r.at(D + 1), D)]
                nc.vector.scalar_tensor_tensor(out=q, in0=p_qk[:, z, 0:D], scalar=scale, in1=bias[:, 0, :],
                                               op0=ALU.mult, op1=ALU.add)
                if r.has(2):
                    dve.wait_ge(out_done[z], r.half(32, 0))
                nc.vector.tensor_tensor(kvs[:, z, 0:D], p_qk[:, z, D:2 * D], bias[:, 1, :], ALU.add)
                nc.vector.tensor_tensor(kvs[:, z, D:2 * D], p_vs[:, z, 0:D], bias[:, 2, :], ALU.add)
                line(nc.vector.tensor_tensor(xo[:, z, :], p_vs[:, z, D:2 * D], bias[:, 3, :], ALU.add))
                nc.vector.tensor_tensor(xo[:, z, :], xo[:, z, :], x[:, z, :], ALU.add).then_inc(staged, 1)

            def body(r, z):
                lines["line"] = line = Line(dve, line_sem, r.at(per))
                dve.wait_ge(x_in[z], r.half(16, 16))
                line(nc.vector.bn_stats(six[:, z, :], x[:, z, :]))
                nc.vector.memset(carrier[:, z:z + 1], 0.0)
                line(nc.vector.bn_aggr(mv[:, z, :], six[:, z, :]))
                nc.vector.tensor_scalar(mv[:, z, 1:2], mv[:, z, 1:2], LN_EPS, None, ALU.add).then_inc(var_ready, 1)
                if r.has(1):
                    evacuate(r.before(), 1 - z)
                else:
                    line(nc.vector.memset(sd[:, 1, :], 1.0))
                dve.wait_ge(sd_ready, r.at(1, 1))
                line(nc.vector.reciprocal(rs[:, z, :], sd[:, z, :]))
                nc.vector.scalar_tensor_tensor(out=nm[:, z, :], in0=mv[:, z, 0:1], scalar=-1.0, in1=rs[:, z, :],
                                               op0=ALU.mult, op1=ALU.mult).then_inc(norm_ready, 1)
                while line.n < per:
                    line(nc.vector.memset(six[:, z, 0:1], 0.0))

            rounds(dve, BLOCKS, body)
            lines["line"] = Line(dve, line_sem, BLOCKS * per)
            evacuate(Round(None, BLOCKS - 1), 0)

        @block.scalar
        def _(act):
            def body(r, z):
                act.wait_ge(var_ready, r.at(1, 1))
                nc.scalar.activation(sd[:, z, :], mv[:, z, 1:2], ACT.Sqrt).then_inc(sd_ready, 1)
                act.wait_ge(norm_ready, r.at(1, 1))
                if r.has(2):
                    act.wait_ge(turned, r.at(1, -1))
                nc.scalar.activation(h[:, z, :], x[:, z, :], ACT.Relu, bias=nm[:, z, :], scale=rs[:, z, :])\
                    .then_inc(h_ready, 1)
                act.wait_ge(turned, r.at(1, 1))
                if r.has(2):
                    act.wait_ge(projected, r.at(1, -1))
                nc.scalar.copy(ht[:, z, :], p_ht[:, z, :]).then_inc(ht_ready, 1)

            rounds(act, BLOCKS, body)

        @block.tensor
        def _(pe):
            pe.wait_ge(w_in, 16 * 8)

            def body(r, z):
                pe.wait_ge(h_ready, r.at(1, 1))
                if r.has(2):
                    pe.wait_ge(ht_ready, r.at(1, -1))
                for c in range(HALF):
                    last = nc.tensor.transpose(p_ht[:, z, c * P:(c + 1) * P], h[:, z, c * P:(c + 1) * P],
                                               k.ident[:, :])
                last.then_inc(turned, 1)
                if r.has(2):
                    pe.wait_ge(staged, r.at(1, -1))
                pe.wait_ge(ht_ready, r.at(1, 1))
                for to, at in ((p_qk, 0), (p_vs, 2 * D)):
                    for c in range(HALF):
                        last = nc.tensor.matmul(to[:, z, :], ht[:, z, c * P:(c + 1) * P], w[:, c, at:at + 2 * D],
                                                start=c == 0, stop=c == HALF - 1)
                last.then_inc(projected, 1)

            rounds(pe, BLOCKS, body)


MSG_AT = {j: [2 * (j - 6), 2 * (j - 6) + 1] for j in range(6, 14)}
SUM_AT = {j + 1: m for j, m in MSG_AT.items()}
ADD_AT = {j + 2: m for j, m in MSG_AT.items()}


def block_no(eng, k, r, j, word):
    if j % PACK == 0:
        word[0] = eng.value_load(k.packed[0:1, bass.ds(r.at(S // PACK, j // PACK), 1)], min_val=0,
                                 max_val=(1 << (6 * PACK)) - 1)
    return eng.bass.s_assert_within(
        eng.snap((word[0] >> (6 * (j % PACK))) & 63), 0, BLOCKS - 1,
        skip_runtime_bounds_check_because="the table's blocks are clamped to the last one")


def attend(nc, b, k):
    a = b.a
    with ExitStack() as ctx:
        sb, ps, sem = allocators(nc, ctx)
        we = sb("we", [P, HALF, D])
        ea = sb("ea", [P, EA_SLOTS, D])
        kv = sb("kv", [P, KV_SLOTS, 2 * D])
        idx = sb("idx", [P, 2, S], I32)
        carrier = sb("wait_carrier3", [1, S])
        loc = sb("loc_b", [P, 2, S])
        oh = sb("oh", [P, 2, S, P])
        xt = sb("xt", [P, 2, D + P])
        kj = sb("kj", [P, 2, D])
        score = sb("score", [P, 2, S * H])
        ve = sb("ve", [P, 2, S, H * CE])
        msg = sb("msg", [P, 4, H * CE])
        fl = sb("fl", [P, NFLAG])
        run = sb("run", [P, P])
        top = sb("top", [P, P])
        sc = sb("sc", [P, P])
        u = sb("u", [P, 2 * S])
        cin = sb("cin", [H, CH - 1])
        cfl = sb("chain_flags", [H, 2, CH])
        cf = sb("cf", [H, CH - 1])
        cb = sb("cb", [H, CH - 1])
        carry = sb("carry", [H, 1])
        fd = sb("fd", [H, 1])
        fe = sb("fe", [H, 1])
        oh8 = sb("oh8", [H, P])
        sel8 = sb("sel8", [H, H])
        own = sb("own", [P, S])
        mf = sb("mf", [P, 2])
        p_x = ps("p_x", [P, 2, 512])
        p_y = ps("p_y", [P, 2, 2 * D])
        p_ch = ps("p_ch", [P, 512])
        p_p = ps("p_p", [P, 512])
        p_sum = ps("p_sum", [P, 2, 512])
        p_st, p_top, p_f, p_u = p_ch[:, 0:P], p_ch[:, 128:128 + CH - 1], p_ch[:, 192:192 + H], p_ch[0:H, 256:256 + 2 * S]
        we_in, setup = sem("we_in"), sem("att_setup")
        ea_in = [sem(f"ea_in{i}") for i in range(EA_SLOTS)]
        kv_in = [sem(f"kv_in{i}") for i in range(KV_SLOTS)]
        fl_in = sem("fl_in")
        idx_ready, oh_ready = sem("idx_ready"), sem("oh_ready")
        turned, xt_ready, y_done = sem("turned"), sem("xt_ready"), sem("y_done")
        kj_done, ve_done, prod_done, score_done = sem("kj_done"), sem("ve_done"), sem("prod_done"), sem("score_done")
        st_done, u_ready, u_done, c_ready, fd_ready, fe_ready, sel_ready, top_done = (
            sem(n) for n in ("st_done", "u_ready", "u_done", "c_ready", "fd_ready", "fe_ready", "sel_ready", "top_done"))
        dd_ready, pt_ready, p_ready, scaled = sem("dd_ready"), sem("pt_ready"), sem("p_ready"), sem("scaled")
        msg_done, sum_done, add_done, chain_line = sem("msg_done"), sem("sum_done"), sem("add_done"), sem("chain_line")
        block = ctx.enter_context(nc.Block())
        NLINE = 16

        @block.sync
        def _(sp):
            sp.dma_start(we[:, :, :], a["L0_gnn_We"].rearrange("(c p) n -> p c n", p=P)).then_inc(we_in, 16)
            flag_rows = b.flags.rearrange("s h f -> (s h) f")

            def body(r, z, here, prev):
                if not here:
                    return
                for j in range(S):
                    row = sp.value_load(k.row[0:1, bass.ds(r.at(S, j), 1)], min_val=0, max_val=E - P)
                    if r.has(1) or j >= EA_SLOTS:
                        sp.wait_ge(turned, r.at(S, j + 1 - EA_SLOTS))
                    slot = j % EA_SLOTS
                    sp.dma_start(ea[:, slot, :], a["edge_attr_256"][bass.ds(row, P), :]).then_inc(ea_in[slot], 16)
                if r.has(1):
                    sp.wait_ge(dd_ready, r.at(1, 0))
                sp.dma_start(fl[:, :], flag_rows[bass.ds(r.at(S * H), S * H), :]).then_inc(fl_in, 16)

            edge_rounds(sp, body)

        @block.gpsimd
        def _(pool):
            def body(r, z, here, prev):
                if not here:
                    return
                nc.gpsimd.tensor_copy(idx[:, z, :], k.src[:, bass.ds(r.at(S), S)]).then_inc(idx_ready, 1)
                nc.gpsimd.tensor_copy(loc[:, z, :], k.loc[:, bass.ds(r.at(S), S)]).then_inc(idx_ready, 1)
                nc.gpsimd.tensor_copy(cfl[:, z, :], k.chain[:, bass.ds(r.at(CH), CH)]).then_inc(idx_ready, 1)
                pool.wait_ge(idx_ready, r.at(3, 3))
                for j in range(S):
                    slot = j % KV_SLOTS
                    if r.has(1) or j >= KV_SLOTS:
                        pool.wait_ge(ve_done, r.at(S, j + 1 - KV_SLOTS))
                    if r.has(2):
                        pool.wait_ge(sum_done, r.at(S, j + 1 - 2 * S))
                    nc.gpsimd.tensor_tensor(carrier[:, j:j + 1], k.iota[0:1, 0:1], k.iota[0:1, 0:1], ALU.add)
                    nc.gpsimd.tensor_scalar(oh[:, z, j, :], k.iota[:, :], loc[:, z, j:j + 1], None, ALU.is_equal)\
                        .then_inc(oh_ready, 1)
                    pool.indirect_dma_start(
                        out=kv[:, slot, :], out_offset=None, in_=b.kv,
                        in_offset=bass.IndirectOffsetOnAxis(ap=idx[:, z, j:j + 1], axis=0)).then_inc(kv_in[slot], 16)

            edge_rounds(pool, body)

        @block.tensor
        def _(pe):
            pe.wait_ge(we_in, 16)
            word = [None]

            def turn(r, z, j):
                g = j % 2
                pe.wait_ge(ea_in[j % EA_SLOTS], r.at(16 * (S // EA_SLOTS), 16 * (j // EA_SLOTS + 1)))
                if r.has(1) or j >= 2:
                    pe.wait_ge(xt_ready, r.at(S, j - 1))
                for c in range(HALF):
                    nc.tensor.transpose(p_x[:, g, c * P:(c + 1) * P], ea[:, j % EA_SLOTS, c * P:(c + 1) * P],
                                        k.ident[:, :])
                pe.wait_ge(oh_ready, r.at(S, j + 1))
                nc.tensor.transpose(p_x[:, g, D:D + P], oh[:, z, j, :], k.ident[:, :]).then_inc(turned, 1)

            def product(r, z, j):
                g = j % 2
                block_of = block_no(pe, k, r, j, word)
                if r.has(1) or j >= 2:
                    pe.wait_ge(prod_done, r.at(S, j - 1))
                pe.wait_ge(xt_ready, r.at(S, j + 1))
                for c in range(HALF):
                    nc.tensor.matmul(p_y[:, g, 0:D], xt[:, g, c * P:(c + 1) * P], we[:, c, :],
                                     start=c == 0, stop=c == HALF - 1)
                nc.tensor.matmul(p_y[:, g, D:2 * D], xt[:, g, D:D + P], k.big2[:, bass.ds(block_of * (D + 1), D)],
                                 start=True, stop=True).then_inc(y_done, 1)

            def body(r, z, here, prev):
                p, y = r.before(), 1 - z
                for j in range(S):
                    if here and j == 0:
                        turn(r, z, 0)
                    if here and j + 1 < S:
                        turn(r, z, j + 1)
                    if here:
                        product(r, z, j)
                    if not prev:
                        continue
                    if j == 0:
                        pe.wait_ge(score_done, p.at(S, S))
                        nc.tensor.transpose(p_st, score[:, y, :], k.ident[:, :]).then_inc(st_done, 1)
                    if j == 1:
                        pe.wait_ge(u_ready, p.at(1, 1))
                        nc.tensor.matmul(p_u, k.of_head[:, :], u[:, :], start=True, stop=True).then_inc(u_done, 1)
                    if j == 3:
                        pe.wait_ge(c_ready, p.at(1, 1))
                        nc.tensor.matmul(p_top, k.head_of[:, :], cb[:, :], start=True, stop=True)
                        pe.wait_ge(sel_ready, p.at(1, 1))
                        nc.tensor.matmul(p_f, oh8[:, :], sel8[:, :], start=True, stop=True).then_inc(top_done, 1)
                    if j == 5:
                        pe.wait_ge(pt_ready, p.at(1, 1))
                        nc.tensor.transpose(p_p[:, 0:P], run[:, :], k.ident[:, :]).then_inc(p_ready, 1)
                    for i in SUM_AT.get(j, ()):
                        if p.has(1) or i >= 2:
                            pe.wait_ge(add_done, p.at(S, i - 1))
                        pe.wait_ge(msg_done, p.at(S, i + 1))
                        nc.tensor.matmul(p_sum[:, i % 2, 0:H * CE], oh[:, y, i, :], msg[:, i % 4, :],
                                         start=True, stop=True).then_inc(sum_done, 1)

            edge_rounds(pe, body)

        @block.scalar
        def _(act):
            def body(r, z, here, prev):
                p = r.before()
                for j in range(S):
                    g = j % 2
                    for i in ([0, 1] if j == 0 else [j + 1] if j + 1 < S else []):
                        if not here:
                            break
                        g = i % 2
                        act.wait_ge(turned, r.at(S, i + 1))
                        if r.has(1) or i >= 2:
                            act.wait_ge(y_done, r.at(S, i - 1))
                        nc.scalar.copy(xt[:, g, :], p_x[:, g, 0:D + P]).then_inc(xt_ready, 1)
                    if prev and j == 1:
                        act.wait_ge(fd_ready, p.at(1, 1))
                        nc.scalar.activation(fe[:, :], fd[:, :], ACT.Exp).then_inc(fe_ready, 1)
                    if prev and j == 4:
                        act.wait_ge(dd_ready, p.at(1, 1))
                        nc.scalar.activation(run[:, :], run[:, :], ACT.Exp).then_inc(pt_ready, 1)

            edge_rounds(act, body)

        @block.vector
        def _(dve):
            nc.vector.memset(k.big1[:, :], 0.0).then_inc(setup, 1)
            nc.vector.memset(ve[:, :, :, :], 1.0).then_inc(setup, 1)
            nc.vector.memset(carry[:, :], -BIG).then_inc(setup, 1)
            dve.wait_ge(setup, 3)
            word = [None]

            def edge_rows(r, z, j):
                g, slot = j % 2, j % KV_SLOTS
                dve.wait_ge(y_done, r.at(S, j + 1))
                dve.wait_ge(kv_in[slot], r.at(16 * (S // KV_SLOTS), 16 * (j // KV_SLOTS + 1)))
                nc.vector.tensor_tensor(kj[:, g, :], p_y[:, g, 0:D], kv[:, slot, 0:D], ALU.add).then_inc(kj_done, 1)
                nc.vector.tensor_tensor(
                    ve[:, z, j, :].rearrange("p (h c) -> p h c", c=CE)[:, :, 0:C],
                    p_y[:, g, 0:D].rearrange("p (h c) -> p h c", c=C),
                    kv[:, slot, D:2 * D].rearrange("p (h c) -> p h c", c=C), ALU.add).then_inc(ve_done, 1)

            def multiply(r, z, j):
                g = j % 2
                dve.wait_ge(kj_done, r.at(S, j + 1))
                nc.vector.tensor_tensor(kj[:, g, :], p_y[:, g, D:2 * D], kj[:, g, :], ALU.mult).then_inc(prod_done, 1)

            def reduce(r, z, j):
                g = j % 2
                if j == 0 and r.has(2):
                    dve.wait_ge(st_done, r.at(1, -1))
                dve.wait_ge(prod_done, r.at(S, j + 1))
                nc.vector.tensor_reduce(score[:, z, j * H:(j + 1) * H],
                                        kj[:, g, :].rearrange("p (h c) -> p h c", c=C), AX.X, ALU.add)\
                    .then_inc(score_done, 1)

            def add(p, i):
                block_of = block_no(dve, k, p, i, word)
                to = k.big1[:, bass.ds(block_of * (H * CE), H * CE)]
                dve.wait_ge(sum_done, p.at(S, i + 1))
                if p.has(1) or i:
                    dve.wait_ge(add_done, p.at(S, i))
                if i == 0:
                    dve.wait_ge(scaled, p.at(1, 1))
                nc.vector.tensor_tensor(to, p_sum[:, i % 2, 0:H * CE], to, ALU.add).then_inc(add_done, 1)

            def message(p, y, i):
                dve.wait_ge(p_ready, p.at(1, 1))
                if p.has(1) or i >= 4:
                    dve.wait_ge(sum_done, p.at(S, i - 3))
                nc.vector.tensor_tensor(msg[:, i % 4, :].rearrange("p (h c) -> p h c", c=CE),
                                        ve[:, y, i, :].rearrange("p (h c) -> p h c", c=CE),
                                        bcast(p_p[:, i * H:(i + 1) * H], CE), ALU.mult).then_inc(msg_done, 1)

            def chain(p, y, j, line):
                if j == 0:
                    dve.wait_ge(st_done, p.at(1, 1))
                    dve.wait_ge(fl_in, p.at(16, 16))
                    if p.has(1):
                        dve.wait_ge(p_ready, p.at(1, 0))
                    line(nc.vector.tensor_tensor(sc[:, :], p_st, fl[:, 3 * P + 1:NFLAG], ALU.add))
                    line(nc.vector.tensor_tensor_scan(run[:, :], fl[:, 0:P], sc[:, :], -BIG, ALU.add, ALU.max))
                    line(nc.vector.tensor_tensor_scan(top[:, ::-1], fl[:, 1:P + 1][:, ::-1], run[:, ::-1], -BIG,
                                                      ALU.add, ALU.max))
                    line(nc.vector.tensor_scalar(u[:, 0:2 * S:2], k.of_step[:, :], top[:, 0:1], None, ALU.mult))
                    nc.vector.tensor_scalar(u[:, 1:2 * S:2], k.of_step[:, :], top[:, P - 1:P], None, ALU.mult)\
                        .then_inc(u_ready, 1)
                if j == 1:
                    dve.wait_ge(u_done, p.at(1, 1))
                    line(nc.vector.tensor_copy(cin[:, 0:1], carry[:, :]))
                    line(nc.vector.tensor_copy(cin[:, 1:CH - 1], p_u))
                    flags = cfl[:, y, :]
                    line(nc.vector.tensor_tensor_scan(cf[:, :], flags[:, 0:CH - 1], cin[:, :], -BIG, ALU.add, ALU.max))
                    nc.vector.tensor_tensor_scan(cb[:, ::-1], flags[:, 1:CH][:, ::-1], cf[:, ::-1], -BIG,
                                                 ALU.add, ALU.max).then_inc(c_ready, 1)
                    dve.wait_ge(c_ready, p.at(1, 1))
                    line(nc.vector.tensor_copy(carry[:, :], cb[:, CH - 2:CH - 1]))
                    nc.vector.tensor_tensor(fd[:, :], cin[:, 0:1], cb[:, 0:1], ALU.subtract).then_inc(fd_ready, 1)
                if j == 2:
                    dve.wait_ge(fe_ready, p.at(1, 1))
                    line(nc.vector.tensor_scalar(oh8[:, :], k.iota[0:H, :], k.straddler[:, bass.ds(p.at(1), 1)], None,
                                                 ALU.is_equal))
                    line(nc.vector.tensor_scalar(fe[:, :], fe[:, :], -1.0, None, ALU.add))
                    nc.vector.tensor_scalar(sel8[:, :], k.ident[0:H, 0:H], fe[:, :], None, ALU.mult).then_inc(sel_ready, 1)
                if j == 4:
                    dve.wait_ge(top_done, p.at(1, 1))
                    for c in range(2):
                        line(nc.vector.tensor_tensor(own[:, :], p_top[:, 1 + c:CH - 1:2], k.of_step[:, :], ALU.mult))
                        line(nc.vector.tensor_reduce(mf[:, c:c + 1], own[:, :], AX.X, ALU.add))
                    for c in range(2):
                        line(nc.vector.scalar_tensor_tensor(
                            out=top[:, :], in0=fl[:, (c + 1) * P + 1:(c + 2) * P + 1], scalar=mf[:, c:c + 1],
                            in1=top[:, :], op0=ALU.add, op1=ALU.max))
                    nc.vector.tensor_tensor(run[:, :], sc[:, :], top[:, :], ALU.subtract).then_inc(dd_ready, 1)
                if j == 6:
                    to = k.big1[:, bass.ds(block_no(dve, k, p, 0, word) * (H * CE), H * CE)]\
                        .rearrange("p (h c) -> p h c", c=CE)
                    if p.has(1):
                        dve.wait_ge(add_done, p.at(S, 0))
                    nc.vector.scalar_tensor_tensor(out=to, in0=bcast(p_f, CE), scalar=1.0, in1=to, op0=ALU.add,
                                                   op1=ALU.mult).then_inc(scaled, 1)

            def body(r, z, here, prev):
                p, y = r.before(), 1 - z
                line = Line(dve, chain_line, p.at(NLINE) if prev else 0)
                for j in range(S):
                    if here:
                        if r.has(1) or j >= 2:
                            dve.wait_ge(score_done, r.at(S, j - 1))
                        edge_rows(r, z, j)
                    if prev:
                        for i in ADD_AT.get(j, ()):
                            add(p, i)
                    if here:
                        multiply(r, z, j)
                    if prev:
                        chain(p, y, j, line)
                        for i in MSG_AT.get(j, ()):
                            message(p, y, i)
                    if here:
                        reduce(r, z, j)
                assert not prev or line.n == NLINE, line.n

            edge_rounds(dve, body)


def finish_attention(nc, b, k):
    with ExitStack() as ctx:
        sb, ps, sem = allocators(nc, ctx)
        x = sb("x1_blk", [P, 2, D])
        carrier = sb("wait_carrier2", [1, 2])
        den = sb("den", [P, 2, H])
        out = sb("att_out", [P, 2, D])
        six = sb("six2", [P, 2, 6])
        mv = sb("mv2", [P, 2, 2])
        sd = sb("sd2", [P, 2, 1])
        rs = sb("rs2", [P, 2, 1])
        nm = sb("nm2", [P, 2, 1])
        junk = sb("sq_junk", [P, 2, D])
        x_in = [sem(f"xr_in{z}") for z in range(2)]
        out_done = [sem(f"x1_out{z}") for z in range(2)]
        x1_ready, var_ready, sd_ready, norm_ready = sem("x1_ready"), sem("var2_ready"), sem("sd2_ready"), sem("norm2_ready")
        h_ready, sq_ready, line_sem = sem("h2_ready"), sem("sq_ready"), sem("fin_dve_line")
        block = ctx.enter_context(nc.Block())

        @block.sync
        def _(sp):
            def store(r, z):
                n = rows_of(r)
                sp.wait_ge(x1_ready, r.at(1, 1))
                sp.dma_start(b.xs[bass.ds(r.at(P), n), :], x[0:n, z, :]).then_inc(out_done[z], 16)
                sp.wait_ge(h_ready, r.at(1, 1))
                sp.dma_start(b.h2[bass.ds(r.at(P), n), :], k.big2[0:n, bass.ds(r.at(D + 1), D)])\
                    .then_inc(out_done[z], 16)

            def body(r, z):
                n = rows_of(r)
                if r.has(2):
                    sp.wait_ge(out_done[z], r.half(32, 0))
                    sp.wait_ge(h_ready, r.at(1, -1))
                sp.dma_start(x[0:n, z, :], b.xs[bass.ds(r.at(P), n), :]).then_inc(x_in[z], 16)
                if r.has(1):
                    store(r.before(), 1 - z)

            rounds(sp, BLOCKS, body)
            store(Round(None, BLOCKS - 1), 0)
            sp.wait_ge(out_done[0], 32 * 25)
            sp.wait_ge(out_done[1], 32 * 24)

        @block.vector
        def _(dve):
            per = 6

            def body(r, z):
                line = Line(dve, line_sem, r.at(per))
                sums = k.big1[:, bass.ds(r.at(H * CE), H * CE)].rearrange("p (h c) -> p h c", c=CE)
                line(nc.vector.tensor_scalar(den[:, z, :], sums[:, :, C], 1e-16, None, ALU.add))
                line(nc.vector.reciprocal(den[:, z, :], den[:, z, :]))
                line(nc.vector.tensor_tensor(out[:, z, :].rearrange("p (h c) -> p h c", c=C), sums[:, :, 0:C],
                                             bcast(den[:, z, :], C), ALU.mult))
                dve.wait_ge(x_in[z], r.half(16, 16))
                nc.vector.tensor_tensor(x[:, z, :], out[:, z, :], x[:, z, :], ALU.add).then_inc(x1_ready, 1)
                dve.wait_ge(x1_ready, r.at(1, 1))
                line(nc.vector.bn_stats(six[:, z, :], x[:, z, :]))
                nc.vector.memset(carrier[:, z:z + 1], 0.0)
                line(nc.vector.bn_aggr(mv[:, z, :], six[:, z, :]))
                nc.vector.tensor_scalar(mv[:, z, 1:2], mv[:, z, 1:2], LN_EPS, None, ALU.add).then_inc(var_ready, 1)
                dve.wait_ge(sd_ready, r.at(1, 1))
                line(nc.vector.reciprocal(rs[:, z, :], sd[:, z, :]))
                nc.vector.scalar_tensor_tensor(out=nm[:, z, :], in0=mv[:, z, 0:1], scalar=-1.0, in1=rs[:, z, :],
                                               op0=ALU.mult, op1=ALU.mult).then_inc(norm_ready, 1)
                assert line.n == per, line.n

            rounds(dve, BLOCKS, body)

        @block.scalar
        def _(act):
            def body(r, z):
                act.wait_ge(var_ready, r.at(1, 1))
                nc.scalar.activation(sd[:, z, :], mv[:, z, 1:2], ACT.Sqrt).then_inc(sd_ready, 1)
                act.wait_ge(norm_ready, r.at(1, 1))
                rows = k.big2[:, bass.ds(r.at(D + 1), D)]
                nc.scalar.activation(rows, x[:, z, :], ACT.Relu, bias=nm[:, z, :], scale=rs[:, z, :]).then_inc(h_ready, 1)
                act.wait_ge(h_ready, r.at(1, 1))
                if r.has(2):
                    act.wait_ge(sq_ready, r.at(1, -1))
                nc.scalar.activation(junk[:, z, :], rows, ACT.Square,
                                     accum_out=k.big2[:, bass.ds(r.at(D + 1, D), 1)]).then_inc(sq_ready, 1)

            rounds(act, BLOCKS, body)


def weights_by_step(nc, b, k):
    a = b.a
    with ExitStack() as ctx:
        sb, ps, sem = allocators(nc, ctx)
        wg = sb("w_gathered", [P, COLS, P])
        p_tr = ps("p_wtr", [P, P])
        table_out, gathered, turned, copied = sem("w_table_out"), sem("w_gathered_sem"), sem("w_turned"), sem("w_copied")
        block = ctx.enter_context(nc.Block())

        @block.sync
        def _(sp):
            sp.dma_start(b.wtp[0:TILES - 1, :],
                         a["edge_weight"][0:(TILES - 1) * P].rearrange("(t e) -> t e", e=P)).then_inc(table_out, 16)
            sp.dma_start(b.wtp[TILES - 1:TILES, :],
                         a["edge_weight"][E - P:E].rearrange("(o e) -> o e", o=1)).then_inc(table_out, 16)

        @block.gpsimd
        def _(pool):
            pool.wait_ge(table_out, 32)
            for c in range(COLS):
                pool.indirect_dma_start(out=wg[:, c, :], out_offset=None, in_=b.wtp,
                                        in_offset=bass.IndirectOffsetOnAxis(ap=k.tile_of[:, c:c + 1], axis=0))\
                    .then_inc(gathered, 16)

        @block.tensor
        def _(pe):
            pe.wait_ge(gathered, 16 * COLS)
            for c in range(COLS):
                if c:
                    pe.wait_ge(copied, c)
                nc.tensor.transpose(p_tr[:, :], wg[:, c, :], k.ident[:, :]).then_inc(turned, 1)

        @block.vector
        def _(dve):
            nc.vector.memset(k.big1[:, :], 0.0)
            for c in range(COLS):
                dve.wait_ge(turned, c + 1)
                nc.vector.tensor_copy(k.wt[:, c * P:(c + 1) * P], p_tr[:, :]).then_inc(copied, 1)


def artanh_ratio_tail(nc, line, out, ln, sn, z, t, mask):
    line(nc.vector.reciprocal(out, sn))
    line(nc.vector.scalar_tensor_tensor(out=out, in0=ln, scalar=0.5, in1=out, op0=ALU.mult, op1=ALU.mult))
    line(nc.vector.tensor_tensor(z, z, z, ALU.mult))
    line(nc.vector.tensor_scalar(t, z, 1.0 / 7, 1.0 / 5, ALU.mult, ALU.add))
    line(nc.vector.tensor_tensor(t, t, z, ALU.mult))
    line(nc.vector.tensor_scalar(t, t, 1.0 / 3, None, ALU.add))
    line(nc.vector.tensor_tensor(t, t, z, ALU.mult))
    line(nc.vector.tensor_scalar(mask, z, 1e-3, None, ALU.is_lt))
    line(nc.vector.scalar_tensor_tensor(out=t, in0=t, scalar=1.0, in1=out, op0=ALU.add, op1=ALU.subtract))
    line(nc.vector.tensor_tensor(t, t, mask, ALU.mult))
    line(nc.vector.tensor_tensor(out, out, t, ALU.add))


def aggregate(nc, b, k):
    with ExitStack() as ctx:
        sb, ps, sem = allocators(nc, ctx)
        xs = sb("xs", [P, 2, S, D])
        idx = sb("idx2", [P, 2, S], I32)
        carrier = sb("wait_carrier4", [1, S])
        loc = sb("loc_b2", [P, 2, S])
        wt = sb("wt_b", [P, 2, S])
        oh = sb("oh2", [P, 2, S, P])
        oht = sb("oht2", [P, 2, P])
        junk = sb("dot_junk", [P, 2, D])
        sqj = sb("sqj", [P, 2, D])
        xy = sb("xy", [P, 2, S])
        x2 = sb("x2", [P, 2, S])
        y2 = sb("y2", [P, 2, S])
        wide = sb("oh_c2", [P, 4, P])
        tmp = [sb(f"edge_t{i}", [P, S]) for i in range(12)]
        ca, cb_, dn, bc, sn, zc, rat, ln, c1, c2, t, mask = [v[:, :] for v in tmp]
        p_x = ps("p_x2", [P, 2, 512])
        p_y = ps("p_y2", [P, 2, 512])
        p_sum = ps("p_sum2", [P, 2, 512])
        xs_in = [sem(f"xs_in{i}") for i in range(KV_SLOTS)]
        idx_ready, oh_ready = sem("idx2_ready"), sem("oh2_ready")
        turned, oht_ready, y_done, dot_done, x2_done, y2_done = (
            sem(n) for n in ("turned2", "oht2_ready", "y2_mm", "dot_done", "x2_done", "y2_done"))
        sq_ready, sn_ready, rat_ready, ln_ready, c_ready = (
            sem(n) for n in ("n2_ready", "sn_ready", "rat_ready", "ln_ready", "c12_ready"))
        wide_done, sum_done, add_done, line_sem = sem("wide_done"), sem("sum2_done"), sem("add2_done"), sem("edge_line")
        block = ctx.enter_context(nc.Block())
        NLINE = 39

        @block.gpsimd
        def _(pool):
            def body(r, z, here, prev):
                if not here:
                    return
                nc.gpsimd.tensor_copy(idx[:, z, :], k.src[:, bass.ds(r.at(S), S)]).then_inc(idx_ready, 1)
                nc.gpsimd.tensor_copy(loc[:, z, :], k.loc[:, bass.ds(r.at(S), S)]).then_inc(idx_ready, 1)
                nc.gpsimd.tensor_copy(wt[:, z, :], k.wt[:, bass.ds(r.at(S), S)]).then_inc(idx_ready, 1)
                pool.wait_ge(idx_ready, r.at(3, 3))
                for j in range(S):
                    slot = j % KV_SLOTS
                    if r.has(1) or j >= KV_SLOTS:
                        pool.wait_ge(dot_done, r.at(S, j + 1 - KV_SLOTS))
                        pool.wait_ge(y2_done, r.at(S, j + 1 - KV_SLOTS))
                    if r.has(2):
                        pool.wait_ge(sum_done, r.at(S, j + 1 - 2 * S))
                    nc.gpsimd.tensor_tensor(carrier[:, j:j + 1], k.iota[0:1, 0:1], k.iota[0:1, 0:1], ALU.add)
                    nc.gpsimd.tensor_scalar(oh[:, z, j, :], k.iota[:, :], loc[:, z, j:j + 1], None, ALU.is_equal)\
                        .then_inc(oh_ready, 1)
                    pool.indirect_dma_start(
                        out=xs[:, z, j, :], out_offset=None, in_=b.h2,
                        in_offset=bass.IndirectOffsetOnAxis(ap=idx[:, z, j:j + 1], axis=0)).then_inc(xs_in[slot], 16)

            edge_rounds(pool, body)

        @block.tensor
        def _(pe):
            word = [None]

            def turn(r, z, j):
                pe.wait_ge(oh_ready, r.at(S, j + 1))
                if r.has(1) or j >= 2:
                    pe.wait_ge(oht_ready, r.at(S, j - 1))
                nc.tensor.transpose(p_x[:, j % 2, 0:P], oh[:, z, j, :], k.ident[:, :]).then_inc(turned, 1)

            def product(r, z, j):
                block_of = block_no(pe, k, r, j, word)
                if r.has(1) or j >= 2:
                    pe.wait_ge(x2_done, r.at(S, j - 1))
                pe.wait_ge(oht_ready, r.at(S, j + 1))
                nc.tensor.matmul(p_y[:, j % 2, 0:D + 1], oht[:, j % 2, :], k.big2[:, bass.ds(block_of * (D + 1), D + 1)],
                                 start=True, stop=True).then_inc(y_done, 1)

            def body(r, z, here, prev):
                p, y = r.before(), 1 - z
                for j in range(S):
                    if here and j == 0:
                        turn(r, z, 0)
                    if here and j + 1 < S:
                        turn(r, z, j + 1)
                    if here:
                        product(r, z, j)
                    for i in SUM_AT.get(j, ()) if prev else ():
                        if p.has(1) or i >= 2:
                            pe.wait_ge(add_done, p.at(S, i - 1))
                        pe.wait_ge(wide_done, p.at(S, i + 1))
                        nc.tensor.matmul(p_sum[:, i % 2, 0:D], wide[:, i % 4, :], xs[:, y, i, :],
                                         start=True, stop=True)
                        nc.tensor.matmul(p_sum[:, i % 2, D:D + 1], oh[:, y, i, :], c1[:, i:i + 1],
                                         start=True, stop=True).then_inc(sum_done, 1)

            edge_rounds(pe, body)

        @block.scalar
        def _(act):
            def body(r, z, here, prev):
                p = r.before()
                for j in range(S):
                    for i in ([0, 1] if j == 0 else [j + 1] if j + 1 < S else []) if here else ():
                        act.wait_ge(turned, r.at(S, i + 1))
                        if r.has(1) or i >= 2:
                            act.wait_ge(y_done, r.at(S, i - 1))
                        nc.scalar.copy(oht[:, i % 2, :], p_x[:, i % 2, 0:P]).then_inc(oht_ready, 1)
                    if here:
                        if r.has(1) or j >= 2:
                            act.wait_ge(y2_done, r.at(S, j - 1))
                        if j == 0 and r.has(2):
                            act.wait_ge(c_ready, r.at(1, -1))
                        act.wait_ge(xs_in[j % KV_SLOTS], r.at(16 * (S // KV_SLOTS), 16 * (j // KV_SLOTS + 1)))
                        nc.scalar.activation(sqj[:, j % 2, :], xs[:, z, j, :], ACT.Square,
                                             accum_out=y2[:, z, j:j + 1]).then_inc(y2_done, 1)
                    if prev and j == 1:
                        act.wait_ge(sq_ready, p.at(1, 1))
                        nc.scalar.activation(sn, sn, ACT.Sqrt).then_inc(sn_ready, 1)
                    if prev and j == 3:
                        act.wait_ge(rat_ready, p.at(1, 1))
                        nc.scalar.activation(ln, rat, ACT.Ln).then_inc(ln_ready, 1)

            edge_rounds(act, body)

        @block.vector
        def _(dve):
            word = [None]
            V = nc.vector

            def dot(r, z, j):
                if r.has(1) or j >= 2:
                    dve.wait_ge(dot_done, r.at(S, j - 1))
                dve.wait_ge(xs_in[j % KV_SLOTS], r.at(16 * (S // KV_SLOTS), 16 * (j // KV_SLOTS + 1)))
                dve.wait_ge(y_done, r.at(S, j + 1))
                V.tensor_tensor_reduce(out=junk[:, j % 2, :], in0=p_y[:, j % 2, 0:D], in1=xs[:, z, j, :], scale=1.0,
                                       scalar=0.0, op0=ALU.mult, op1=ALU.add, accum_out=xy[:, z, j:j + 1])\
                    .then_inc(dot_done, 1)
                V.tensor_copy(x2[:, z, j:j + 1], p_y[:, j % 2, D:D + 1]).then_inc(x2_done, 1)

            def coefficients(p, y, j, line):
                w = wt[:, y, :]
                X2, Y2, XY = x2[:, y, :], y2[:, y, :], xy[:, y, :]
                if j == 0:
                    dve.wait_ge(x2_done, p.at(S, S))
                    dve.wait_ge(dot_done, p.at(S, S))
                    dve.wait_ge(y2_done, p.at(S, S))
                    if p.has(1):
                        dve.wait_ge(sum_done, p.at(S, 0))
                    line(V.tensor_scalar(t, XY, -2.0, 1.0, ALU.mult, ALU.add))
                    line(V.tensor_tensor(ca, t, Y2, ALU.add))
                    line(V.tensor_scalar(bc, X2, -1.0, 1.0, ALU.mult, ALU.add))
                    line(V.tensor_tensor(dn, X2, Y2, ALU.mult))
                    line(V.tensor_tensor(dn, dn, t, ALU.add))
                    line(V.tensor_scalar(dn, dn, MIN_NORM, None, ALU.max))
                    line(V.reciprocal(dn, dn))
                    line(V.tensor_tensor(cb_, bc, XY, ALU.mult))
                    line(V.tensor_tensor(sn, ca, X2, ALU.mult))
                    line(V.scalar_tensor_tensor(out=sn, in0=cb_, scalar=-2.0, in1=sn, op0=ALU.mult, op1=ALU.add))
                    line(V.tensor_tensor(sn, sn, ca, ALU.mult))
                    line(V.tensor_tensor(cb_, bc, Y2, ALU.mult))
                    line(V.tensor_tensor(cb_, bc, cb_, ALU.mult))
                    line(V.tensor_tensor(sn, sn, cb_, ALU.add))
                    line(V.tensor_tensor(sn, sn, dn, ALU.mult))
                    line(V.tensor_tensor(sn, sn, dn, ALU.mult))
                    V.tensor_scalar(sn, sn, 0.0, None, ALU.max).then_inc(sq_ready, 1)
                if j == 2:
                    dve.wait_ge(sn_ready, p.at(1, 1))
                    line(V.tensor_scalar(sn, sn, MIN_NORM, None, ALU.max))
                    line(V.tensor_scalar(zc, sn, CLIP, None, ALU.min))
                    line(V.tensor_scalar(t, zc, -1.0, 1.0, ALU.mult, ALU.add))
                    line(V.reciprocal(t, t))
                    V.scalar_tensor_tensor(out=rat, in0=zc, scalar=1.0, in1=t, op0=ALU.add, op1=ALU.mult)\
                        .then_inc(rat_ready, 1)
                if j == 4:
                    dve.wait_ge(ln_ready, p.at(1, 1))
                    artanh_ratio_tail(nc, line, rat, ln, sn, zc, t, mask)
                    line(V.tensor_scalar(t, bc, MIN_NORM, None, ALU.max))
                    line(V.reciprocal(t, t))
                    line(V.tensor_scalar(t, t, 2.0, MIN_NORM, ALU.mult, ALU.max))
                    line(V.reciprocal(t, t))
                    line(V.scalar_tensor_tensor(out=t, in0=t, scalar=2.0, in1=rat, op0=ALU.mult, op1=ALU.mult))
                    line(V.tensor_tensor(t, t, w, ALU.mult))
                    line(V.tensor_tensor(t, t, dn, ALU.mult))
                    line(V.scalar_tensor_tensor(out=c1, in0=t, scalar=-1.0, in1=ca, op0=ALU.mult, op1=ALU.mult))
                    V.tensor_tensor(c2, t, bc, ALU.mult).then_inc(c_ready, 1)

            def widen(p, y, i):
                dve.wait_ge(c_ready, p.at(1, 1))
                if p.has(1) or i >= 4:
                    dve.wait_ge(sum_done, p.at(S, i - 3))
                V.tensor_scalar(wide[:, i % 4, :], oh[:, y, i, :], c2[:, i:i + 1], None, ALU.mult).then_inc(wide_done, 1)

            def add(p, i):
                block_of = block_no(dve, k, p, i, word)
                to = k.big1[:, bass.ds(block_of * (D + 1), D + 1)]
                dve.wait_ge(sum_done, p.at(S, i + 1))
                if p.has(1) or i:
                    dve.wait_ge(add_done, p.at(S, i))
                V.tensor_tensor(to, p_sum[:, i % 2, 0:D + 1], to, ALU.add).then_inc(add_done, 1)

            def body(r, z, here, prev):
                p, y = r.before(), 1 - z
                line = Line(dve, line_sem, p.at(NLINE) if prev else 0)
                for j in range(S):
                    if here:
                        dot(r, z, j)
                    if prev:
                        for i in ADD_AT.get(j, ()):
                            add(p, i)
                        coefficients(p, y, j, line)
                        for i in MSG_AT.get(j, ()):
                            widen(p, y, i)
                assert not prev or line.n == NLINE, line.n

            edge_rounds(dve, body)


def hyperbolic_layer(nc, b, k, out):
    a = b.a
    with ExitStack() as ctx:
        sb, ps, sem = allocators(nc, ctx)
        w_rows = sb("w_rows", [P, HALF, D])
        wT = sb("w_turned_t", [P, HALF, D])
        bias = sb("bias1", [P, D])
        ball = sb("ball", [P, D])
        junk = sb("junk5", [P, 2, D])
        junk2 = sb("junk6", [P, 2, D])
        part = sb("part", [P, 2, D])
        u = sb("u_blk", [P, 2, D])
        ut = sb("ut_blk", [P, 2, D])
        xr = sb("xr_blk", [P, 2, D])
        tabs = {n: sb(f"t_{n}", [P, BLOCKS])[:, :] for n in
                ("n2", "xa", "u2", "m2", "mb", "h2", "t2", "a", "b", "c", "d", "e", "f", "g", "w", "v", "x2")}
        one = {n: sb(f"o_{n}", [P, 1])[:, :] for n in ("n2", "n", "th", "b2", "r")}
        p_w = ps("p_w", [P, 2, 512])
        p_ut = ps("p_ut", [P, 2, 512])
        p_m = ps("p_m", [P, 2, 512])
        V, A = nc.vector, nc.scalar
        sums = k.big1[:, 0:BLOCKS * (D + 1)].rearrange("p (b c) -> p b c", c=D + 1)
        rows_x2 = k.big2[:, :].rearrange("p (b c) -> p b c", c=D + 1)[:, :, D]

        def sums_of(r):
            return k.big1[:, bass.ds(r.at(D + 1), D)]

        def rows_of_block(r):
            return k.big2[:, bass.ds(r.at(D + 1), D)]

        def col(name, r):
            return tabs[name][:, bass.ds(r.at(1), 1)]

        def phase(name, engines):
            with ExitStack() as c:
                sems = {}

                def s(n):
                    if n not in sems:
                        sems[n] = c.enter_context(nc.semaphore(f"{name}_{n}"))
                    return sems[n]

                block = c.enter_context(nc.Block())
                for e, fn in engines.items():
                    engine = {"sync": block.sync, "vector": block.vector, "scalar": block.scalar,
                              "tensor": block.tensor}[e]
                    engine(lambda eng, fn=fn: fn(eng, s))

        def p1_dve(dve, s):
            def body(r, z):
                to = sums_of(r)
                V.scalar_tensor_tensor(out=to, in0=rows_of_block(r), scalar=k.big1[:, bass.ds(r.at(D + 1, D), 1)],
                                       in1=to, op0=ALU.mult, op1=ALU.add).then_inc(s("first"), 1)
                dve.wait_ge(s("first"), r.at(1, 1))
                if r.has(2):
                    dve.wait_ge(s("fourth"), r.at(1, -1))
                V.tensor_tensor(junk[:, z, :], to, rows_of_block(r), ALU.mult).then_inc(s("second"), 1)
            rounds(dve, BLOCKS, body)

        def p1_act(act, s):
            def body(r, z):
                act.wait_ge(s("first"), r.at(1, 1))
                if r.has(2):
                    act.wait_ge(s("third"), r.at(1, -1))
                A.activation(junk2[:, z, :], sums_of(r), ACT.Square, accum_out=col("n2", r)).then_inc(s("third"), 1)
                act.wait_ge(s("second"), r.at(1, 1))
                A.activation(junk[:, z, :], junk[:, z, :], ACT.Copy, accum_out=col("xa", r)).then_inc(s("fourth"), 1)
            rounds(act, BLOCKS, body)

        def p1_sp(sp, s):
            sp.dma_start(w_rows[:, :, :], a["L1_gnn_weight"].rearrange("(c p) n -> p c n", p=P)).then_inc(s("in0"), 16)
            sp.dma_start(bias[:, :], a["L1_gnn_bias"].partition_broadcast(P)).then_inc(s("in0"), 16)
            sp.wait_ge(s("in0"), 32)

        phase("sum_pass", {"sync": p1_sp, "vector": p1_dve, "scalar": p1_act})

        def q1_dve(dve, s):
            line = Line(dve, s("line"))
            T = tabs
            line(V.tensor_copy(T["x2"], rows_x2))
            dve.wait_ge(s("first"), 1)
            line(V.tensor_scalar(T["a"], T["a"], MIN_NORM, None, ALU.max))
            line(V.tensor_scalar(T["b"], T["x2"], -1.0, 1.0, ALU.mult, ALU.add))
            line(V.tensor_scalar(T["c"], T["b"], MIN_NORM, None, ALU.max))
            line(V.reciprocal(T["c"], T["c"]))
            line(V.tensor_scalar(T["c"], T["c"], 2.0, MIN_NORM, ALU.mult, ALU.max))
            line(V.scalar_tensor_tensor(out=T["d"], in0=T["a"], scalar=0.5, in1=T["c"], op0=ALU.mult, op1=ALU.mult))
            V.reciprocal(T["c"], T["a"]).then_inc(s("second"), 1)
            dve.wait_ge(s("third"), 1)
            dve.wait_ge(s("second"), 1)
            line(V.tensor_tensor(T["d"], T["d"], T["c"], ALU.mult))
            line(V.tensor_tensor(T["e"], T["d"], T["xa"], ALU.mult))
            line(V.tensor_tensor(T["f"], T["n2"], T["d"], ALU.mult))
            line(V.tensor_tensor(T["f"], T["f"], T["d"], ALU.mult))
            line(V.tensor_scalar(T["e"], T["e"], 2.0, 1.0, ALU.mult, ALU.add))
            line(V.tensor_tensor(T["g"], T["x2"], T["f"], ALU.mult))
            line(V.tensor_tensor(T["g"], T["g"], T["e"], ALU.add))
            line(V.tensor_scalar(T["g"], T["g"], MIN_NORM, None, ALU.max))
            line(V.reciprocal(T["g"], T["g"]))
            line(V.tensor_tensor(T["e"], T["e"], T["f"], ALU.add))
            line(V.tensor_tensor(T["v"], T["e"], T["g"], ALU.mult))
            line(V.tensor_tensor(T["b"], T["b"], T["g"], ALU.mult))
            line(V.tensor_tensor(T["w"], T["b"], T["d"], ALU.mult))
            dve.wait_ge(s("fourth"), 1)
            line(V.tensor_scalar(one["n"], one["n"], MIN_NORM, None, ALU.max))
            V.reciprocal(one["r"], one["n"]).then_inc(s("fifth"), 1)
            dve.wait_ge(s("sixth"), 1)
            dve.wait_ge(s("fifth"), 1)
            line(V.tensor_tensor(one["r"], one["r"], one["th"], ALU.mult))
            line(V.tensor_scalar(ball[:, :], bias[:, :], one["r"], None, ALU.mult))
            line(V.tensor_tensor_reduce(out=junk[:, 0, :], in0=ball[:, :], in1=ball[:, :], scale=1.0, scalar=0.0,
                                        op0=ALU.mult, op1=ALU.add, accum_out=one["b2"]))
            for c in range(HALF):
                dve.wait_ge(s("ready"), c + 1)
                line(V.tensor_copy(wT[:, c, :], p_w[:, c, 0:D]))

        def q1_act(act, s):
            line = Line(act, s("act_line"))
            line(A.activation(tabs["a"], tabs["n2"], ACT.Sqrt))
            A.activation(junk2[:, 0, :], bias[:, :], ACT.Square, accum_out=one["n2"]).then_inc(s("first"), 1)
            act.wait_ge(s("first"), 1)
            A.activation(one["n"], one["n2"], ACT.Sqrt).then_inc(s("fourth"), 1)
            act.wait_ge(s("second"), 1)
            A.activation(tabs["d"], tabs["d"], ACT.Tanh).then_inc(s("third"), 1)
            act.wait_ge(s("fifth"), 1)
            A.activation(one["th"], one["n"], ACT.Tanh).then_inc(s("sixth"), 1)

        def q1_pe(pe, s):
            for c in range(HALF):
                for o in range(HALF):
                    last = nc.tensor.transpose(p_w[:, c, o * P:(o + 1) * P], w_rows[:, o, c * P:(c + 1) * P],
                                               k.ident[:, :])
                last.then_inc(s("ready"), 1)

        phase("expmap", {"vector": q1_dve, "scalar": q1_act, "tensor": q1_pe})

        def p2_act(act, s):
            def multiply(r, z):
                if r.has(2):
                    act.wait_ge(s("second"), r.at(1, -1))
                A.activation(part[:, z, :], rows_of_block(r), ACT.Copy, scale=col("v", r)).then_inc(s("first"), 1)

            def body(r, z):
                multiply(r, z)
                act.wait_ge(s("second"), r.at(1, 1))
                if r.has(2):
                    act.wait_ge(s("act_line"), r.at(2, -2))
                A.activation(junk2[:, z, :], u[:, z, :], ACT.Square, accum_out=col("u2", r)).then_inc(s("act_line"), 1)
                act.wait_ge(s("third"), r.at(1, 1))
                A.copy(ut[:, z, :], p_ut[:, z, 0:D]).then_inc(s("fourth"), 1)
                act.wait_ge(s("sixth"), r.at(1, 1))
                act.wait_ge(s("act_line"), r.at(2, 1))
                A.activation(junk2[:, z, :], sums_of(r), ACT.Square, accum_out=col("m2", r)).then_inc(s("act_line"), 1)
                act.wait_ge(s("ready"), r.at(1, 1))
                A.activation(junk[:, z, :], junk[:, z, :], ACT.Copy, accum_out=col("mb", r)).then_inc(s("dotted"), 1)
            rounds(act, BLOCKS, body)

        def p2_dve(dve, s):
            def body(r, z):
                dve.wait_ge(s("first"), r.at(1, 1))
                if r.has(2):
                    dve.wait_ge(s("third"), r.at(1, -1))
                    dve.wait_ge(s("act_line"), r.at(2, -2))
                V.scalar_tensor_tensor(out=u[:, z, :], in0=sums_of(r), scalar=col("w", r), in1=part[:, z, :],
                                       op0=ALU.mult, op1=ALU.add).then_inc(s("second"), 1)
                dve.wait_ge(s("fifth"), r.at(1, 1))
                dve.wait_ge(s("second"), r.at(1, 1))
                V.tensor_scalar(sums_of(r), p_m[:, z, 0:D], 1.0, None, ALU.mult).then_inc(s("sixth"), 1)
                if r.has(2):
                    dve.wait_ge(s("dotted"), r.at(1, -1))
                V.tensor_tensor(junk[:, z, :], p_m[:, z, 0:D], ball[:, :], ALU.mult).then_inc(s("ready"), 1)
            rounds(dve, BLOCKS, body)

        def p2_pe(pe, s):
            def body(r, z):
                pe.wait_ge(s("second"), r.at(1, 1))
                if r.has(2):
                    pe.wait_ge(s("fourth"), r.at(1, -1))
                for c in range(HALF):
                    last = nc.tensor.transpose(p_ut[:, z, c * P:(c + 1) * P], u[:, z, c * P:(c + 1) * P], k.ident[:, :])
                last.then_inc(s("third"), 1)
                pe.wait_ge(s("fourth"), r.at(1, 1))
                if r.has(2):
                    pe.wait_ge(s("ready"), r.at(1, -1))
                for c in range(HALF):
                    last = nc.tensor.matmul(p_m[:, z, 0:D], ut[:, z, c * P:(c + 1) * P], wT[:, c, :],
                                            start=c == 0, stop=c == HALF - 1)
                last.then_inc(s("fifth"), 1)
            rounds(pe, BLOCKS, body)

        phase("matvec", {"vector": p2_dve, "scalar": p2_act, "tensor": p2_pe})

        def q2_dve(dve, s):
            line = Line(dve, s("line"))
            T = tabs
            dve.wait_ge(s("first"), 1)
            line(V.tensor_scalar(T["a"], T["a"], MIN_NORM, None, ALU.max))
            line(V.tensor_scalar(T["b"], T["b"], MIN_NORM, None, ALU.max))
            line(V.tensor_scalar(T["c"], T["a"], CLIP, None, ALU.min))
            line(V.tensor_scalar(T["d"], T["c"], -1.0, 1.0, ALU.mult, ALU.add))
            line(V.reciprocal(T["d"], T["d"]))
            V.scalar_tensor_tensor(out=T["d"], in0=T["c"], scalar=1.0, in1=T["d"], op0=ALU.add, op1=ALU.mult)\
                .then_inc(s("second"), 1)
            dve.wait_ge(s("third"), 1)
            artanh_ratio_tail(nc, line, T["f"], T["d"], T["a"], T["c"], T["e"], T["g"])
            V.tensor_tensor(T["f"], T["f"], T["b"], ALU.mult).then_inc(s("fourth"), 1)
            dve.wait_ge(s("fifth"), 1)
            line(V.reciprocal(T["b"], T["b"]))
            line(V.tensor_tensor(T["f"], T["f"], T["b"], ALU.mult))
            line(V.tensor_tensor(T["c"], T["f"], T["m2"], ALU.mult))
            line(V.tensor_tensor(T["c"], T["f"], T["c"], ALU.mult))
            line(V.tensor_tensor(T["d"], T["f"], T["mb"], ALU.mult))
            line(V.tensor_scalar(T["d"], T["d"], 2.0, 1.0, ALU.mult, ALU.add))
            line(V.tensor_scalar(T["e"], T["c"], one["b2"], None, ALU.mult))
            line(V.tensor_tensor(T["e"], T["e"], T["d"], ALU.add))
            line(V.tensor_scalar(T["e"], T["e"], MIN_NORM, None, ALU.max))
            line(V.reciprocal(T["e"], T["e"]))
            line(V.tensor_scalar(T["d"], T["d"], one["b2"], None, ALU.add))
            line(V.tensor_tensor(T["d"], T["d"], T["f"], ALU.mult))
            line(V.tensor_tensor(T["v"], T["d"], T["e"], ALU.mult))
            line(V.tensor_scalar(T["c"], T["c"], -1.0, 1.0, ALU.mult, ALU.add))
            line(V.tensor_tensor(T["w"], T["c"], T["e"], ALU.mult))

        def q2_act(act, s):
            line = Line(act, s("act_line"))
            line(A.activation(tabs["a"], tabs["u2"], ACT.Sqrt))
            A.activation(tabs["b"], tabs["m2"], ACT.Sqrt).then_inc(s("first"), 1)
            act.wait_ge(s("second"), 1)
            A.activation(tabs["d"], tabs["d"], ACT.Ln).then_inc(s("third"), 1)
            act.wait_ge(s("fourth"), 1)
            A.activation(tabs["f"], tabs["f"], ACT.Tanh).then_inc(s("fifth"), 1)

        phase("matvec_norms", {"vector": q2_dve, "scalar": q2_act})

        def p3_dve(dve, s):
            def body(r, z):
                if r.has(2):
                    dve.wait_ge(s("second"), r.at(1, -1))
                V.tensor_scalar(part[:, z, :], ball[:, :], col("w", r), None, ALU.mult).then_inc(s("first"), 1)
                dve.wait_ge(s("first"), r.at(1, 1))
                V.scalar_tensor_tensor(out=sums_of(r), in0=sums_of(r), scalar=col("v", r), in1=part[:, z, :],
                                       op0=ALU.mult, op1=ALU.add).then_inc(s("second"), 1)
            rounds(dve, BLOCKS, body)

        def p3_act(act, s):
            def body(r, z):
                act.wait_ge(s("second"), r.at(1, 1))
                if r.has(2):
                    act.wait_ge(s("third"), r.at(1, -1))
                A.activation(junk2[:, z, :], sums_of(r), ACT.Square, accum_out=col("h2", r)).then_inc(s("third"), 1)
            rounds(act, BLOCKS, body)

        phase("ball_add", {"vector": p3_dve, "scalar": p3_act})

        def q3_dve(dve, s):
            line = Line(dve, s("line"))
            T = tabs
            dve.wait_ge(s("first"), 1)
            line(V.tensor_scalar(T["a"], T["a"], MIN_NORM, None, ALU.max))
            line(V.tensor_scalar(T["c"], T["a"], CLIP, None, ALU.min))
            line(V.tensor_scalar(T["d"], T["c"], -1.0, 1.0, ALU.mult, ALU.add))
            line(V.reciprocal(T["d"], T["d"]))
            V.scalar_tensor_tensor(out=T["d"], in0=T["c"], scalar=1.0, in1=T["d"], op0=ALU.add, op1=ALU.mult)\
                .then_inc(s("second"), 1)
            dve.wait_ge(s("third"), 1)
            artanh_ratio_tail(nc, line, T["f"], T["d"], T["a"], T["c"], T["e"], T["g"])

        def q3_act(act, s):
            A.activation(tabs["a"], tabs["h2"], ACT.Sqrt).then_inc(s("first"), 1)
            act.wait_ge(s("second"), 1)
            A.activation(tabs["d"], tabs["d"], ACT.Ln).then_inc(s("third"), 1)

        phase("logmap", {"vector": q3_dve, "scalar": q3_act})

        def p4_act(act, s):
            def body(r, z):
                A.activation(sums_of(r), sums_of(r), ACT.Relu, scale=col("f", r)).then_inc(s("first"), 1)
                act.wait_ge(s("first"), r.at(1, 1))
                if r.has(2):
                    act.wait_ge(s("second"), r.at(1, -1))
                A.activation(junk2[:, z, :], sums_of(r), ACT.Square, accum_out=col("t2", r)).then_inc(s("second"), 1)
            rounds(act, BLOCKS, body)

        phase("tangent", {"scalar": p4_act})

        def q4_dve(dve, s):
            line = Line(dve, s("line"))
            T = tabs
            top = 1.0 - BALL_EPS
            dve.wait_ge(s("first"), 1)
            line(V.tensor_scalar(T["a"], T["a"], MIN_NORM, None, ALU.max))
            V.reciprocal(T["b"], T["a"]).then_inc(s("second"), 1)
            dve.wait_ge(s("third"), 1)
            dve.wait_ge(s("second"), 1)
            line(V.tensor_tensor(T["v"], T["c"], T["b"], ALU.mult))
            line(V.tensor_scalar(T["d"], T["t2"], 0.0, None, ALU.is_gt))
            line(V.tensor_tensor(T["c"], T["c"], T["d"], ALU.mult))
            line(V.tensor_scalar(T["c"], T["c"], top, None, ALU.max))
            line(V.reciprocal(T["c"], T["c"]))
            line(V.tensor_scalar(T["c"], T["c"], top, None, ALU.mult))
            line(V.tensor_tensor(T["v"], T["v"], T["c"], ALU.mult))

        def q4_act(act, s):
            A.activation(tabs["a"], tabs["t2"], ACT.Sqrt).then_inc(s("first"), 1)
            act.wait_ge(s("second"), 1)
            A.activation(tabs["c"], tabs["a"], ACT.Tanh).then_inc(s("third"), 1)

        phase("project", {"vector": q4_dve, "scalar": q4_act})

        def p5_sp(sp, s):
            def store(r, z):
                n = rows_of(r)
                sp.wait_ge(s("first"), r.at(1, 1))
                sp.dma_start(out[bass.ds(r.at(P), n), :], xr[0:n, z, :]).then_inc(s(f"out{z}"), 16)

            def body(r, z):
                n = rows_of(r)
                if r.has(2):
                    sp.wait_ge(s(f"out{z}"), r.half(16, 0))
                sp.dma_start(xr[0:n, z, :], b.xs[bass.ds(r.at(P), n), :]).then_inc(s(f"in{z}"), 16)
                if r.has(1):
                    store(r.before(), 1 - z)
            rounds(sp, BLOCKS, body)
            store(Round(None, BLOCKS - 1), 0)
            sp.wait_ge(s("out0"), 16 * 25)
            sp.wait_ge(s("out1"), 16 * 24)

        def p5_dve(dve, s):
            def body(r, z):
                dve.wait_ge(s(f"in{z}"), r.half(16, 16))
                V.scalar_tensor_tensor(out=xr[:, z, :], in0=sums_of(r), scalar=col("v", r), in1=xr[:, z, :],
                                       op0=ALU.mult, op1=ALU.add).then_inc(s("first"), 1)
            rounds(dve, BLOCKS, body)

        phase("result", {"sync": p5_sp, "vector": p5_dve})


class Keep:
    pass


def program(nc, a, out):
    b = Build(nc, a)
    k = Keep()
    with ExitStack() as ctx:
        sb, _, _ = allocators(nc, ctx)
        k.iota = sb("iota", [P, P])
        k.ident = sb("ident", [P, P])
        k.of_step = sb("of_step", [P, S])
        k.of_head = sb("of_head", [P, H])
        k.head_of = sb("head_of", [H, P])
        k.loc = sb("loc_tab", [P, SPAD])
        k.tile_of = sb("tile_of_i", [P, COLS], I32)
        k.src = sb("src_tab", [P, SPAD], I32)
        k.chain = sb("chain_tab", [H, BATCHES * CH])
        k.straddler = sb("straddler", [H, BATCHES])
        k.row = sb("row_tab", [1, SPAD], I32)
        k.packed = sb("packed_tab", [1, SPAD // PACK], I32)
        k.big1 = sb("node_sums", [P, BLOCKS * H * CE])
        k.big2 = sb("node_rows", [P, BLOCKS * (D + 1)])
        prep(nc, b, k)
        if PHASES >= 2:
            project_nodes(nc, b, k)
        if PHASES >= 3:
            attend(nc, b, k)
        if PHASES >= 4:
            finish_attention(nc, b, k)
        if PHASES >= 5:
            k.wt = sb("wt_tab", [P, SPAD])
            weights_by_step(nc, b, k)
            aggregate(nc, b, k)
        if PHASES >= 6:
            hyperbolic_layer(nc, b, k, out)


PHASES = 6


_INS = ["x", "src", "dst", "edge_attr_256", "edge_weight",
        "L0_gnn_Wq", "L0_gnn_bq", "L0_gnn_Wk", "L0_gnn_bk", "L0_gnn_Wv", "L0_gnn_bv", "L0_gnn_We",
        "L0_gnn_Ws", "L0_gnn_bs", "L1_gnn_weight", "L1_gnn_bias"]


def kernel(**inputs):
    import numpy as _np
    import concourse.bacc as _bacc
    from concourse import mybir as _mybir
    from concourse.bass_utils import run_bass_kernel_spmd as _run

    nc = _bacc.Bacc("TRN2", target_bir_lowering=False, num_devices=1)
    arrays, args = {}, {}
    for name in _INS:
        x = _np.ascontiguousarray(inputs[name])
        arrays[f"in_{name}"] = x
        args[name] = nc.dram_tensor(f"in_{name}", x.shape, _mybir.dt.from_np(x.dtype), kind="ExternalInput").ap()
    out = nc.dram_tensor("out_rows", (N, D), F32, kind="ExternalOutput").ap()
    program(nc, args, out)
    r = _run(nc, [arrays], core_ids=[0])
    return r.results[0]["out_rows"]
```

```python
import concourse.bass as bass
import concourse.mybir as mybir
import numpy as np
from contextlib import ExitStack

F32 = mybir.dt.float32
I32 = mybir.dt.int32
ALU = mybir.AluOpType
ACT = mybir.ActivationFunctionType
AX = mybir.AxisListType

P = 128
N, E, D = 6250, 106250, 256
H, C = 8, 32
CE = C + 1
BLOCKS = -(-N // P)
TAIL = N - (BLOCKS - 1) * P
TILES = -(-E // P)
LAST = E - (TILES - 1) * P
S = 16
BATCHES = -(-(TILES + BLOCKS - 1) // S)
STEPS = BATCHES * S
COLS = -(-STEPS // P)
SPAD = COLS * P
NFLAG = 4 * P + 1
CH = 2 * S + 2
BIG = 1.0e30
HALF = D // P
EA_SLOTS = 4
KV_SLOTS = 8
LN_EPS = 1e-5
MIN_NORM = 1e-15
BALL_EPS = 1e-5
CLIP = float(np.float32(1.0 - 1e-7))
CHUNK = 4
PACK = 4
GROUP = 7


class Round:

    def __init__(self, m, a):
        self.m, self.a = m, a

    def at(self, per, k=0):
        return per * self.a + k if self.m is None else self.m * (2 * per) + (per * self.a + k)


    def half(self, per, k=0):
        return per * (self.a // 2) + k if self.m is None else self.m * per + (per * (self.a // 2) + k)

    def after(self):
        return Round(self.m, self.a + 1)

    def before(self):
        return Round(self.m, self.a - 1)

    def has(self, back):
        return self.m is not None or self.a >= back


def rounds(eng, total, body):
    body(Round(None, 0), 0)
    body(Round(None, 1), 1)
    pairs = (total - 2) // 2
    with eng.Fori(0, pairs) as m:
        body(Round(m, 2), 0)
        body(Round(m, 3), 1)
    if total % 2:
        body(Round(None, total - 1), 0)


def edge_rounds(eng, body):
    body(Round(None, 0), 0, True, False, False)
    body(Round(None, 1), 1, True, True, False)
    with eng.Fori(0, (BATCHES - 2) // 2) as m:
        body(Round(m, 2), 0, True, True, True)
        body(Round(m, 3), 1, True, True, True)
    body(Round(None, BATCHES - 1), 0, True, True, True)
    body(Round(None, BATCHES), 1, False, True, True)
    body(Round(None, BATCHES + 1), 0, False, False, True)


def bcast(ap, n):
    return ap.unsqueeze(2).to_broadcast([ap.shape[0], ap.shape[1], n])


class Line:

    def __init__(self, eng, sem, base=0):
        self.eng, self.sem, self.base, self.n = eng, sem, base, 0

    def __call__(self, ins):
        self.n += 1
        ins.then_inc(self.sem, 1)
        self.eng.wait_ge(self.sem, self.base + self.n)

    def on(self, ins):
        self.n += 1
        ins.then_inc(self.sem, 1)


class Build:
    def __init__(self, nc, a):
        self.nc, self.a = nc, a
        self.scratch()

    def scratch(self):
        nc = self.nc

        def dram(name, shape, dt=F32):
            return nc.dram_tensor(name, shape, dt, kind="Internal").ap()

        self.dstp = dram("dst_tiles", (TILES, P), I32)
        self.srcp = dram("src_tiles", (TILES, P), I32)
        self.wtp = dram("weight_tiles", (TILES, P))
        self.flags = dram("step_flags", (SPAD, H, NFLAG))
        self.ends = dram("step_ends", (SPAD, 5))
        self.kv = dram("kv_rows", (N, 2 * D))
        self.xs = dram("x_rows", (N, D))
        self.h2 = dram("h2_rows", (N, D))


def allocators(nc, ctx):
    def sb(name, shape, dt=F32):
        return ctx.enter_context(nc.sbuf_tensor(name, shape, dt))

    def ps(name, shape, dt=F32):
        return ctx.enter_context(nc.psum_tensor(name, shape, dt))

    def sem(name):
        return ctx.enter_context(nc.semaphore(name))

    return sb, ps, sem


def prep(nc, b, k):
    a = b.a
    with ExitStack() as ctx:
        sb, ps, sem = allocators(nc, ctx)
        tile_last = sb("tile_last", [1, TILES], I32)
        tile_block = sb("tile_block", [1, TILES], I32)
        tile_no = sb("tile_no", [1, TILES], I32)
        start_row = sb("start_row", [1, TILES], F32)
        block_row = sb("block_row", [1, TILES], F32)
        one_row = sb("one_row", [1, P], F32)
        starts = sb("starts", [P, TILES], F32)
        junk = sb("junk", [P, TILES], F32)
        step_no_i = sb("step_no_i", [P, COLS], I32)
        step_no = sb("step_no", [P, COLS], F32)
        tile_of = sb("tile_of", [P, COLS], F32)
        base_of = sb("base_of", [P, COLS], F32)
        dst_g = sb("dst_g", [P, COLS, P], I32)
        src_g = sb("src_g", [P, COLS, P], I32)
        loc = sb("loc", [P, COLS, P], F32)
        src_f = sb("src_f", [P, COLS, P], F32)
        seg = sb("seg", [P, COLS, P], F32)
        flag = sb("flag", [P, COLS, NFLAG], F32)
        dup_i = sb("dup_i", [P, 1], I32)
        dup = sb("dup", [P, 1])
        fill = sb("fill", [P, COLS])
        ends5 = sb("ends5", [P, COLS, 5], F32)
        ends8 = sb("ends8", [H, SPAD, 5], F32)
        neg = sb("neg", [1, P], I32)
        packf = sb("packf", [1, SPAD // PACK], F32)
        iota_i = sb("iota_i", [P, P], I32)
        part_i = sb("part_i", [P, 1], I32)
        part8_i = sb("part8_i", [P, 1], I32)
        partm_i = sb("partm_i", [P, 1], I32)
        part3 = sb("part3", [P, 3], F32)
        p_starts = ps("p_starts", [P, 1024], F32)
        p_tr = ps("p_tr", [P, 2, P], F32)
        tiles_in = sem("tiles_in")
        tables_out = sem("tables_out")
        iotas = sem("iotas")
        dve_line = sem("dve_line")
        row_ready = sem("row_ready")
        starts_up = sem("starts_up")
        tile_of_ready = sem("tile_of_ready")
        gathered = sem("gathered")
        loc_ready = sem("loc_ready")
        turned = sem("turned")
        turned_read = sem("turned_read")
        flags_ready = sem("flags_ready")
        flags_out = sem("flags_out")
        block = ctx.enter_context(nc.Block())

        @block.sync
        def _(sp):
            with nc.allow_non_contiguous_dma(reason="the last edge of each tile"):
                sp.dma_start(tile_last[0:1, 0:TILES - 1],
                             a["dst"][0:(TILES - 1) * P].rearrange("(o t e) -> o t e", o=1, e=P)[:, :, P - 1])\
                    .then_inc(tiles_in, 16)
            sp.dma_start(tile_last[0:1, TILES - 1:TILES],
                         a["dst"][E - 1:E].rearrange("(o e) -> o e", o=1)).then_inc(tiles_in, 16)
            sp.dma_start(dup_i[:, :], a["dst"][E - LAST - 1:E - LAST].partition_broadcast(P)).then_inc(tiles_in, 16)
            for table, name in ((b.dstp, "dst"), (b.srcp, "src")):
                sp.dma_start(table[0:TILES - 1, :],
                             a[name][0:(TILES - 1) * P].rearrange("(t e) -> t e", e=P)).then_inc(tables_out, 16)
            sp.dma_start(b.srcp[TILES - 1:TILES, :],
                         a["src"][E - P:E].rearrange("(o e) -> o e", o=1)).then_inc(tables_out, 16)
            sp.dma_start(b.dstp[TILES - 1:TILES, P - LAST:P],
                         a["dst"][E - LAST:E].rearrange("(o e) -> o e", o=1)).then_inc(tables_out, 16)
            sp.wait_ge(iotas, 1)
            sp.dma_start(b.dstp[TILES - 1:TILES, 0:P - LAST], neg[0:1, 0:P - LAST]).then_inc(tables_out, 16)
            sp.wait_ge(flags_ready, 1)
            for h in range(H):
                sp.dma_start(b.flags[:, h, :].rearrange("(c p) f -> p c f", p=P), flag[:, :, :])\
                    .then_inc(flags_out, 16)
            with nc.allow_non_contiguous_dma(reason="five words for each step"):
                sp.dma_start(b.ends.rearrange("(c p) f -> p c f", p=P), ends5[:, :, :]).then_inc(flags_out, 16)
            sp.wait_ge(flags_out, 16 * (H + 1))
            sp.dma_start(ends8[:, :, :], b.ends.partition_broadcast(H)).then_inc(flags_out, 16)

        @block.gpsimd
        def _(pool):
            nc.gpsimd.memset(neg[:, :], -1).then_inc(iotas, 1)
            nc.gpsimd.iota(tile_no[:, :], [[1, TILES]], base=0, channel_multiplier=0).then_inc(iotas, 1)
            nc.gpsimd.iota(step_no_i[:, :], [[P, COLS]], base=0, channel_multiplier=1).then_inc(iotas, 1)
            nc.gpsimd.iota(iota_i[:, :], [[1, P]], base=0, channel_multiplier=0).then_inc(iotas, 1)
            nc.gpsimd.iota(part_i[:, :], [[0, 1]], base=0, channel_multiplier=1).then_inc(iotas, 1)
            pool.wait_ge(tables_out, 16 * 5)
            pool.wait_ge(tile_of_ready, 1)
            for c in range(COLS):
                for table, to in ((b.dstp, dst_g), (b.srcp, src_g)):
                    pool.indirect_dma_start(
                        out=to[:, c, :], out_offset=None, in_=table,
                        in_offset=bass.IndirectOffsetOnAxis(ap=k.tile_of[:, c:c + 1], axis=0))\
                        .then_inc(gathered, 16)

        @block.vector
        def _(dve):
            line = Line(dve, dve_line)
            dve.wait_ge(iotas, 5)
            line(nc.vector.tensor_copy(k.iota[:, :], iota_i[:, :]))
            line(nc.vector.tensor_copy(part3[:, 0:1], part_i[:, :]))
            line(nc.vector.tensor_single_scalar(part8_i[:, :], part_i[:, :], 3, ALU.arith_shift_right))
            line(nc.vector.tensor_single_scalar(partm_i[:, :], part_i[:, :], H - 1, ALU.bitwise_and))
            line(nc.vector.tensor_copy(part3[:, 1:2], part8_i[:, :]))
            line(nc.vector.tensor_copy(part3[:, 2:3], partm_i[:, :]))
            line(nc.vector.tensor_scalar(k.ident[:, :], k.iota[:, :], part3[:, 0:1], None, ALU.is_equal))
            line(nc.vector.tensor_scalar(k.of_step[:, :], k.iota[:, 0:S], part3[:, 1:2], None, ALU.is_equal))
            line(nc.vector.tensor_scalar(k.of_head[:, :], k.iota[:, 0:H], part3[:, 2:3], None, ALU.is_equal))
            for s in range(S):
                line(nc.vector.tensor_copy(k.head_of[:, s * H:(s + 1) * H], k.ident[0:H, 0:H]))
            line(nc.vector.memset(one_row[:, :], 1.0))
            dve.wait_ge(tiles_in, 48)
            line(nc.vector.tensor_single_scalar(tile_block[:, :], tile_last[:, :], 7, ALU.arith_shift_right))
            line(nc.vector.tensor_copy(block_row[:, :], tile_block[:, :]))
            line(nc.vector.tensor_copy(start_row[:, :], tile_no[:, :]))
            line(nc.vector.tensor_tensor(start_row[0:1, 1:TILES], start_row[0:1, 1:TILES],
                                         block_row[0:1, 0:TILES - 1], ALU.add))
            nc.vector.tensor_copy(step_no[:, :], step_no_i[:, :]).then_inc(row_ready, 1)
            dve.wait_ge(row_ready, 1)
            dve.wait_ge(starts_up, 1)
            line(nc.vector.tensor_copy(starts[:, :], p_starts[:, 0:TILES]))
            for c in range(COLS):
                line(nc.vector.tensor_scalar(junk[:, :], starts[:, :], step_no[:, c:c + 1], 0.0,
                                             ALU.is_le, ALU.add, accum_out=tile_of[:, c:c + 1]))
            line(nc.vector.tensor_scalar(tile_of[:, :], tile_of[:, :], -1.0, float(TILES - 1), ALU.add, ALU.min))
            nc.vector.tensor_copy(k.tile_of[:, :], tile_of[:, :]).then_inc(tile_of_ready, 1)
            line(nc.vector.tensor_tensor(base_of[:, :], step_no[:, :], tile_of[:, :], ALU.subtract))
            line(nc.vector.tensor_scalar(ends5[:, :, 3], base_of[:, :], float(BLOCKS - 1), None, ALU.min))
            line(nc.vector.tensor_scalar(ends5[:, :, 4], tile_of[:, :], float(P), float(E - P), ALU.mult, ALU.min))
            line(nc.vector.tensor_scalar(base_of[:, :], base_of[:, :], float(P), None, ALU.mult))
            dve.wait_ge(gathered, 16 * 2 * COLS)
            line(nc.vector.tensor_copy(loc[:, :, :], dst_g[:, :, :]))
            for c in range(COLS):
                line(nc.vector.tensor_scalar(loc[:, c, :], loc[:, c, :], base_of[:, c:c + 1], None, ALU.subtract))
            nc.vector.tensor_copy(src_f[:, :, :], src_g[:, :, :]).then_inc(loc_ready, 1)
            line(nc.vector.memset(flag[:, :, :], 0.0))
            line(nc.vector.tensor_scalar(seg[:, :, :], loc[:, :, :], -0.5, P - 0.5, ALU.max, ALU.min))
            line(nc.vector.tensor_tensor(flag[:, :, 3 * P + 1:NFLAG], seg[:, :, :], loc[:, :, :], ALU.is_equal))
            line(nc.vector.tensor_copy(dup[:, :], dup_i[:, :]))
            line(nc.vector.tensor_scalar(fill[:, :], tile_of[:, :], float(TILES - 1), dup[:, :], ALU.is_equal, ALU.mult))
            for c in range(COLS):
                line(nc.vector.tensor_copy(seg[:, c, :], dst_g[:, c, :]))
                line(nc.vector.tensor_scalar(seg[:, c, :], seg[:, c, :], fill[:, c:c + 1], base_of[:, c:c + 1],
                                             ALU.max, ALU.subtract))
            line(nc.vector.tensor_scalar(seg[:, :, :], seg[:, :, :], -0.5, P - 0.5, ALU.max, ALU.min))
            line(nc.vector.tensor_copy(ends5[:, :, 2], seg[:, :, 0]))
            for c in range(COLS):
                line(nc.vector.tensor_scalar(seg[:, c, :], seg[:, c, :], base_of[:, c:c + 1], None, ALU.add))
            line(nc.vector.tensor_copy(ends5[:, :, 0], seg[:, :, 0]))
            line(nc.vector.tensor_copy(ends5[:, :, 1], seg[:, :, P - 1]))
            line(nc.vector.tensor_tensor(flag[:, :, 1:P], seg[:, :, 1:P], seg[:, :, 0:P - 1], ALU.is_equal))
            for c in range(COLS):
                line(nc.vector.tensor_scalar(flag[:, c, P + 1:2 * P + 1], seg[:, c, :], seg[:, c, 0:1], None,
                                             ALU.is_equal))
                line(nc.vector.tensor_scalar(flag[:, c, 2 * P + 1:3 * P + 1], seg[:, c, :], seg[:, c, P - 1:P],
                                             None, ALU.is_equal))
            nc.vector.tensor_scalar(flag[:, :, :], flag[:, :, :], BIG, -BIG, ALU.mult, ALU.add)\
                .then_inc(flags_ready, 1)
            for c in range(COLS):
                dve.wait_ge(turned, c + 1)
                line(nc.vector.tensor_copy(k.loc[:, c * P:(c + 1) * P], p_tr[:, 0, :]))
                nc.vector.tensor_copy(k.src[:, c * P:(c + 1) * P], p_tr[:, 1, :]).then_inc(turned_read, 1)
            dve.wait_ge(flags_out, 16 * (H + 2))
            chain = k.chain[:, :].rearrange("p (i c) -> p i c", c=CH)
            line(nc.vector.memset(k.chain[:, :], 0.0))
            e5 = ends8[:, 0:STEPS, :]
            line(nc.vector.tensor_tensor(
                chain[:, :, 2:CH - 1:2], e5[:, :, 0].rearrange("p (i s) -> p i s", s=S),
                e5[:, :, 1].rearrange("p (i s) -> p i s", s=S), ALU.is_equal))
            line(nc.vector.tensor_tensor(
                chain[:, :, 3:CH - 1:2], ends8[:, 1:STEPS + 1, 0].rearrange("p (i s) -> p i s", s=S)[:, :, 0:S - 1],
                e5[:, :, 1].rearrange("p (i s) -> p i s", s=S)[:, :, 0:S - 1], ALU.is_equal))
            line(nc.vector.tensor_tensor(
                chain[:, 1:BATCHES, 1], ends8[:, S:STEPS, 0].rearrange("p (i s) -> p i s", s=S)[:, :, 0],
                ends8[:, S - 1:STEPS - 1, 1].rearrange("p (i s) -> p i s", s=S)[:, :, 0], ALU.is_equal))
            line(nc.vector.tensor_scalar(k.chain[:, :], k.chain[:, :], BIG, -BIG, ALU.mult, ALU.add))
            line(nc.vector.tensor_copy(k.straddler[:, :], e5[:, :, 2].rearrange("p (i s) -> p i s", s=S)[:, :, 0]))
            line(nc.vector.tensor_copy(k.row[:, :], ends8[0:1, :, 4]))
            blocks = ends8[0:1, :, 3].rearrange("p (w j) -> p w j", j=PACK)
            line(nc.vector.tensor_copy(packf[:, :], blocks[:, :, PACK - 1]))
            for j in reversed(range(PACK - 1)):
                line(nc.vector.scalar_tensor_tensor(out=packf[:, :], in0=packf[:, :], scalar=64.0,
                                                    in1=blocks[:, :, j], op0=ALU.mult, op1=ALU.add))
            line(nc.vector.tensor_copy(k.packed[:, :], packf[:, :]))

        @block.tensor
        def _(pe):
            pe.wait_ge(row_ready, 1)
            for at in range(0, TILES, 512):
                n = min(512, TILES - at)
                last = nc.tensor.matmul(p_starts[:, at:at + n], one_row[:, :], start_row[0:1, at:at + n],
                                        start=True, stop=True)
            last.then_inc(starts_up, 1)
            pe.wait_ge(loc_ready, 1)
            for c in range(COLS):
                if c:
                    pe.wait_ge(turned_read, c)
                nc.tensor.transpose(p_tr[:, 0, :], loc[:, c, :], k.ident[:, :])
                nc.tensor.transpose(p_tr[:, 1, :], src_f[:, c, :], k.ident[:, :]).then_inc(turned, 1)


def rows_of(r):
    return TAIL if r.m is None and r.a == BLOCKS - 1 else P


def project_nodes(nc, b, k):
    a = b.a
    with ExitStack() as ctx:
        sb, ps, sem = allocators(nc, ctx)
        w = sb("w_qkvs", [P, HALF, 4 * D])
        bias = sb("bias_qkvs", [P, 4, D])
        x = sb("x_blk", [P, 2, D])
        carrier = sb("wait_carrier", [1, 2])
        six = sb("six", [P, 2, 6])
        mv = sb("mv", [P, 2, 2])
        sd = sb("sd", [P, 2, 1])
        rs = sb("rs", [P, 2, 1])
        nm = sb("nm", [P, 2, 1])
        xb = sb("x_bs", [P, 2, D])
        h = sb("h_blk", [P, 2, D])
        ht = sb("ht_blk", [P, 2, D])
        kvs = sb("kv_stage", [P, 2, 2 * D])
        xo = sb("xo_stage", [P, 2, D])
        p_ht = ps("p_ht", [P, 2, D])
        p_qk = ps("p_qk", [P, 2, 2 * D])
        p_vs = ps("p_vs", [P, 2, 2 * D])
        w_in = sem("w_in")
        x_in = [sem(f"x_in{z}") for z in range(2)]
        out_done = [sem(f"kv_out{z}") for z in range(2)]
        line_sem = sem("proj_dve_line")
        var_ready, sd_ready, norm_ready = sem("var_ready"), sem("sd_ready"), sem("norm_ready")
        h_ready, turned, ht_ready = sem("h_ready"), sem("h_turned"), sem("ht_ready")
        projected, staged, xb_ready = sem("projected"), sem("staged"), sem("xb_ready")
        block = ctx.enter_context(nc.Block())
        scale = 1.0 / float(np.sqrt(np.float32(C)))

        @block.sync
        def _(sp):
            for i, name in enumerate(("Wq", "Wk", "Wv", "Ws")):
                sp.dma_start(w[:, :, i * D:(i + 1) * D],
                             a[f"L0_gnn_{name}"].rearrange("(c p) n -> p c n", p=P)).then_inc(w_in, 16)
            for i, name in enumerate(("bq", "bk", "bv", "bs")):
                sp.dma_start(bias[:, i, :], a[f"L0_gnn_{name}"].partition_broadcast(P)).then_inc(w_in, 16)

            def store(r, z):
                n = rows_of(r)
                sp.wait_ge(staged, r.at(1, 1))
                sp.dma_start(b.kv[bass.ds(r.at(P), n), :], kvs[0:n, z, :]).then_inc(out_done[z], 16)
                sp.dma_start(b.xs[bass.ds(r.at(P), n), :], xo[0:n, z, :]).then_inc(out_done[z], 16)

            def body(r, z):
                n = rows_of(r)
                if r.has(2):
                    sp.wait_ge(h_ready, r.at(1, -1))
                    sp.wait_ge(xb_ready, r.at(1, -1))
                sp.dma_start(x[0:n, z, :], a["x"][bass.ds(r.at(P), n), :]).then_inc(x_in[z], 16)
                if r.has(2):
                    store(r.before().before(), z)

            rounds(sp, BLOCKS, body)
            store(Round(None, BLOCKS - 2), 1)
            store(Round(None, BLOCKS - 1), 0)
            sp.wait_ge(out_done[0], 32 * 25)
            sp.wait_ge(out_done[1], 32 * 24)

        @block.gpsimd
        def _(pool):
            pool.wait_ge(w_in, 16 * 8)

            def body(r, z):
                pool.wait_ge(x_in[z], r.half(16, 16))
                if r.has(2):
                    pool.wait_ge(staged, r.at(1, -1))
                nc.gpsimd.tensor_tensor(xb[:, z, :], x[:, z, :], bias[:, 3, :], ALU.add).then_inc(xb_ready, 1)

            rounds(pool, BLOCKS, body)

        @block.vector
        def _(dve):
            dve.wait_ge(w_in, 16 * 8)
            nc.vector.tensor_scalar(bias[:, 0, :], bias[:, 0, :], scale, None, ALU.mult).then_inc(line_sem, 1)
            dve.wait_ge(line_sem, 1)

            def evacuate(r, z):
                dve.wait_ge(projected, r.at(1, 1))
                q = k.big2[:, bass.ds(r.at(D + 1), D)]
                nc.vector.scalar_tensor_tensor(out=q, in0=p_qk[:, z, 0:D], scalar=scale, in1=bias[:, 0, :],
                                               op0=ALU.mult, op1=ALU.add)
                if r.has(2):
                    dve.wait_ge(out_done[z], r.half(32, 0))
                nc.vector.tensor_tensor(kvs[:, z, 0:D], p_qk[:, z, D:2 * D], bias[:, 1, :], ALU.add)
                nc.vector.tensor_tensor(kvs[:, z, D:2 * D], p_vs[:, z, 0:D], bias[:, 2, :], ALU.add)
                dve.wait_ge(xb_ready, r.at(1, 1))
                nc.vector.tensor_tensor(xo[:, z, :], p_vs[:, z, D:2 * D], xb[:, z, :], ALU.add).then_inc(staged, 1)

            def stats(r, z):
                line = Line(dve, line_sem, r.at(3, 1))
                dve.wait_ge(x_in[z], r.half(16, 16))
                line(nc.vector.bn_stats(six[:, z, :], x[:, z, :]))
                nc.vector.memset(carrier[:, z:z + 1], 0.0)
                line(nc.vector.bn_aggr(mv[:, z, :], six[:, z, :]))
                nc.vector.tensor_scalar(mv[:, z, 1:2], mv[:, z, 1:2], LN_EPS, None, ALU.add).then_inc(var_ready, 1)

            def norm(r, z):
                line = Line(dve, line_sem, r.at(3, 3))
                dve.wait_ge(sd_ready, r.at(1, 1))
                line(nc.vector.reciprocal(rs[:, z, :], sd[:, z, :]))
                nc.vector.scalar_tensor_tensor(out=nm[:, z, :], in0=mv[:, z, 0:1], scalar=-1.0, in1=rs[:, z, :],
                                               op0=ALU.mult, op1=ALU.mult).then_inc(norm_ready, 1)

            def body(r, z):
                norm(r, z)
                if r.has(1):
                    evacuate(r.before(), 1 - z)
                if r.m is not None or r.a + 1 < BLOCKS:
                    stats(r.after(), 1 - z)

            stats(Round(None, 0), 0)
            rounds(dve, BLOCKS, body)
            evacuate(Round(None, BLOCKS - 1), 0)

        @block.scalar
        def _(act):
            def deviation(r, z):
                act.wait_ge(var_ready, r.at(1, 1))
                nc.scalar.activation(sd[:, z, :], mv[:, z, 1:2], ACT.Sqrt).then_inc(sd_ready, 1)

            def body(r, z):
                act.wait_ge(norm_ready, r.at(1, 1))
                if r.has(2):
                    act.wait_ge(turned, r.at(1, -1))
                nc.scalar.activation(h[:, z, :], x[:, z, :], ACT.Relu, bias=nm[:, z, :], scale=rs[:, z, :])\
                    .then_inc(h_ready, 1)
                act.wait_ge(turned, r.at(1, 1))
                if r.has(2):
                    act.wait_ge(projected, r.at(1, -1))
                nc.scalar.copy(ht[:, z, :], p_ht[:, z, :]).then_inc(ht_ready, 1)
                if r.m is not None or r.a + 1 < BLOCKS:
                    deviation(r.after(), 1 - z)

            deviation(Round(None, 0), 0)
            rounds(act, BLOCKS, body)

        @block.tensor
        def _(pe):
            pe.wait_ge(w_in, 16 * 8)

            def body(r, z):
                pe.wait_ge(h_ready, r.at(1, 1))
                if r.has(2):
                    pe.wait_ge(ht_ready, r.at(1, -1))
                for c in range(HALF):
                    last = nc.tensor.transpose(p_ht[:, z, c * P:(c + 1) * P], h[:, z, c * P:(c + 1) * P],
                                               k.ident[:, :])
                last.then_inc(turned, 1)
                if r.has(2):
                    pe.wait_ge(staged, r.at(1, -1))
                pe.wait_ge(ht_ready, r.at(1, 1))
                for to, at in ((p_qk, 0), (p_vs, 2 * D)):
                    for c in range(HALF):
                        last = nc.tensor.matmul(to[:, z, :], ht[:, z, c * P:(c + 1) * P], w[:, c, at:at + 2 * D],
                                                start=c == 0, stop=c == HALF - 1)
                last.then_inc(projected, 1)

            rounds(pe, BLOCKS, body)


MSG_FROM = S // 2
LAG = 2
MSG_AT = {j: [2 * (j - MSG_FROM), 2 * (j - MSG_FROM) + 1] for j in range(MSG_FROM, S)}
SUM_AT = {j + LAG: m for j, m in MSG_AT.items() if j + LAG < S}
LATE_AT = {j + LAG - S: m for j, m in MSG_AT.items() if j + LAG >= S}


def block_no(eng, k, r, j, word, known=False):
    if j % PACK == 0 and not known:
        word[0] = eng.value_load(k.packed[0:1, bass.ds(r.at(S // PACK, j // PACK), 1)], min_val=0,
                                 max_val=(1 << (6 * PACK)) - 1)
    return eng.bass.s_assert_within(
        eng.snap((word[0] >> (6 * (j % PACK))) & 63), 0, BLOCKS - 1,
        skip_runtime_bounds_check_because="the table's blocks are clamped to the last one")


def attend(nc, b, k):
    a = b.a
    with ExitStack() as ctx:
        sb, ps, sem = allocators(nc, ctx)
        we = sb("we", [P, HALF, D])
        ea = sb("ea", [P, EA_SLOTS, D])
        kv = sb("kv", [P, KV_SLOTS, 2 * D])
        idx = sb("idx", [P, 2, S], I32)
        carrier = sb("wait_carrier3", [1, S])
        loc = sb("loc_b", [P, 2, S])
        oh = sb("oh", [P, 2, S, P])
        xt = sb("xt", [P, 2, D + P])
        kj = sb("kj", [P, 4, D])
        score = sb("score", [P, S * H])
        ve = sb("ve", [P, 2, S, H * CE])
        msg = sb("msg", [P, 4, H * CE])
        fl = sb("fl", [P, NFLAG])
        run = sb("run", [P, P])
        top = sb("top", [P, P])
        sc = sb("sc", [P, P])
        u = sb("u", [P, 2 * S])
        cin = sb("cin", [H, CH - 1])
        cfl = sb("chain_flags", [H, 2, CH])
        cf = sb("cf", [H, CH - 1])
        cb = sb("cb", [H, CH - 1])
        carry = sb("carry", [H, 1])
        fd = sb("fd", [H, 1])
        fe = sb("fe", [H, 1])
        sel8 = sb("sel8", [H, H])
        oh8 = top[0:H, :]
        mf = sb("mf", [P, 2])
        p_x = ps("p_x", [P, 2, 512])
        p_y = ps("p_y", [P, 2, 2 * D])
        p_ch = ps("p_ch", [P, 512])
        p_p = ps("p_p", [P, 512])
        p_sum = ps("p_sum", [P, 2, 512])
        p_st, p_top, p_f, p_u = p_ch[:, 0:P], p_ch[:, 128:128 + CH - 1], p_ch[:, 192:192 + H], p_ch[0:H, 256:256 + 2 * S]
        we_in, setup = sem("we_in"), sem("att_setup")
        ea_in = [sem(f"ea_in{i}") for i in range(EA_SLOTS)]
        kv_in = [sem(f"kv_in{i}") for i in range(KV_SLOTS)]
        fl_in = sem("fl_in")
        idx_ready, oh_ready = sem("idx_ready"), sem("oh_ready")
        turned, xt_ready, y_done = sem("turned"), sem("xt_ready"), sem("y_done")
        kj_done, ve_done, prod_done, score_done = sem("kj_done"), sem("ve_done"), sem("prod_done"), sem("score_done")
        st_done, u_ready, u_done, c_ready, fd_ready, fe_ready, sel_ready, top_done, f_done = (
            sem(n) for n in ("st_done", "u_ready", "u_done", "c_ready", "fd_ready", "fe_ready", "sel_ready", "top_done",
                             "f_done"))
        dd_ready, pt_ready, p_ready = sem("dd_ready"), sem("pt_ready"), sem("p_ready")
        msg_done, sum_done, add_done, chain_line = sem("msg_done"), sem("sum_done"), sem("add_done"), sem("chain_line")
        block = ctx.enter_context(nc.Block())
        NLINE = 15

        @block.sync
        def _(sp):
            sp.dma_start(we[:, :, :], a["L0_gnn_We"].rearrange("(c p) n -> p c n", p=P)).then_inc(we_in, 16)
            flag_rows = b.flags.rearrange("s h f -> (s h) f")

            def body(r, z, here, prev, late):
                if not here:
                    return
                for j in range(S):
                    row = sp.value_load(k.row[0:1, bass.ds(r.at(S, j), 1)], min_val=0, max_val=E - P)
                    if r.has(1) or j >= EA_SLOTS:
                        sp.wait_ge(turned, r.at(S, j + 1 - EA_SLOTS))
                    slot = j % EA_SLOTS
                    sp.dma_start(ea[:, slot, :], a["edge_attr_256"][bass.ds(row, P), :]).then_inc(ea_in[slot], 16)
                if r.has(1):
                    sp.wait_ge(dd_ready, r.at(1, 0))
                sp.dma_start(fl[:, :], flag_rows[bass.ds(r.at(S * H), S * H), :]).then_inc(fl_in, 16)

            edge_rounds(sp, body)

        @block.gpsimd
        def _(pool):
            def body(r, z, here, prev, late):
                if not here:
                    return
                nc.gpsimd.tensor_copy(idx[:, z, :], k.src[:, bass.ds(r.at(S), S)]).then_inc(idx_ready, 1)
                nc.gpsimd.tensor_copy(loc[:, z, :], k.loc[:, bass.ds(r.at(S), S)]).then_inc(idx_ready, 1)
                nc.gpsimd.tensor_copy(cfl[:, z, :], k.chain[:, bass.ds(r.at(CH), CH)]).then_inc(idx_ready, 1)
                pool.wait_ge(idx_ready, r.at(3, 3))
                for j in range(S):
                    slot = j % KV_SLOTS
                    if r.has(1) or j >= KV_SLOTS:
                        pool.wait_ge(ve_done, r.at(S, j + 1 - KV_SLOTS))
                    if r.has(2):
                        pool.wait_ge(sum_done, r.at(S, j + 1 - 2 * S))
                    nc.gpsimd.tensor_tensor(carrier[:, j:j + 1], k.iota[0:1, 0:1], k.iota[0:1, 0:1], ALU.add)
                    nc.gpsimd.tensor_scalar(oh[:, z, j, :], k.iota[:, :], loc[:, z, j:j + 1], None, ALU.is_equal)\
                        .then_inc(oh_ready, 1)
                    pool.indirect_dma_start(
                        out=kv[:, slot, :], out_offset=None, in_=b.kv,
                        in_offset=bass.IndirectOffsetOnAxis(ap=idx[:, z, j:j + 1], axis=0)).then_inc(kv_in[slot], 16)

            edge_rounds(pool, body)

        @block.tensor
        def _(pe):
            pe.wait_ge(we_in, 16)
            word = [None]

            def turn(r, z, j):
                g = j % 2
                pe.wait_ge(ea_in[j % EA_SLOTS], r.at(16 * (S // EA_SLOTS), 16 * (j // EA_SLOTS + 1)))
                for c in range(HALF):
                    nc.tensor.transpose(p_x[:, g, c * P:(c + 1) * P], ea[:, j % EA_SLOTS, c * P:(c + 1) * P],
                                        k.ident[:, :])
                pe.wait_ge(oh_ready, r.at(S, j + 1))
                nc.tensor.transpose(p_x[:, g, D:D + P], oh[:, z, j, :], k.ident[:, :]).then_inc(turned, 1)

            def product(r, z, j):
                g = j % 2
                block_of = block_no(pe, k, r, j, word)
                if r.has(1) or j >= 2:
                    pe.wait_ge(prod_done, r.at(S, j - 1))
                pe.wait_ge(xt_ready, r.at(S, j + 1))
                for c in range(HALF):
                    nc.tensor.matmul(p_y[:, g, 0:D], xt[:, g, c * P:(c + 1) * P], we[:, c, :],
                                     start=c == 0, stop=c == HALF - 1)
                nc.tensor.matmul(p_y[:, g, D:2 * D], xt[:, g, D:D + P], k.big2[:, bass.ds(block_of * (D + 1), D)],
                                 start=True, stop=True).then_inc(y_done, 1)

            def sums(p, y, i):
                if i % 2 == 0:
                    if p.has(1) or i >= 2:
                        pe.wait_ge(add_done, p.at(S, i))
                    pe.wait_ge(msg_done, p.at(S, i + 2))
                nc.tensor.matmul(p_sum[:, i % 2, 0:H * CE], oh[:, y, i, :], msg[:, i % 4, :],
                                 start=True, stop=True).then_inc(sum_done, 1)

            def chain(p, y, j):
                if j == 1:
                    pe.wait_ge(score_done, p.at(S, S))
                    nc.tensor.transpose(p_st, score[:, :], k.ident[:, :]).then_inc(st_done, 1)
                if j == 3:
                    pe.wait_ge(u_ready, p.at(1, 1))
                    nc.tensor.matmul(p_u, k.of_head[:, :], u[:, :], start=True, stop=True).then_inc(u_done, 1)
                if j == 5:
                    pe.wait_ge(c_ready, p.at(1, 1))
                    nc.tensor.matmul(p_top, k.head_of[:, :], cb[:, :], start=True, stop=True).then_inc(top_done, 1)
                if j == 7:
                    pe.wait_ge(pt_ready, p.at(1, 1))
                    nc.tensor.transpose(p_p[:, 0:P], run[:, :], k.ident[:, :]).then_inc(p_ready, 1)
                if j == 8:
                    pe.wait_ge(sel_ready, p.at(1, 1))
                    nc.tensor.matmul(p_f, oh8, sel8[:, :], start=True, stop=True).then_inc(f_done, 1)

            def body(r, z, here, prev, late):
                p, y = r.before(), 1 - z
                for j in range(S):
                    if here and j == 0:
                        turn(r, z, 0)
                    if here and j + 1 < S:
                        turn(r, z, j + 1)
                    if here:
                        product(r, z, j)
                    if late:
                        for i in LATE_AT.get(j, ()):
                            sums(p.before(), z, i)
                    if prev:
                        chain(p, y, j)
                        for i in SUM_AT.get(j, ()):
                            sums(p, y, i)

            edge_rounds(pe, body)

        @block.scalar
        def _(act):
            def body(r, z, here, prev, late):
                p = r.before()
                for j in range(S):
                    g = j % 2
                    for i in ([0, 1] if j == 0 else [j + 1] if j + 1 < S else []):
                        if not here:
                            break
                        g = i % 2
                        act.wait_ge(kv_in[i % KV_SLOTS], r.at(16 * (S // KV_SLOTS), 16 * (i // KV_SLOTS + 1)))
                        act.wait_ge(turned, r.at(S, i + 1))
                        if r.has(1) or i >= 2:
                            act.wait_ge(y_done, r.at(S, i - 1))
                        nc.scalar.copy(xt[:, g, :], p_x[:, g, 0:D + P]).then_inc(xt_ready, 1)
                    if prev and j == 5:
                        act.wait_ge(fd_ready, p.at(1, 1))
                        nc.scalar.activation(fe[:, :], fd[:, :], ACT.Exp).then_inc(fe_ready, 1)
                    if prev and j == 7:
                        act.wait_ge(dd_ready, p.at(1, 1))
                        nc.scalar.activation(run[:, :], run[:, :], ACT.Exp).then_inc(pt_ready, 1)

            edge_rounds(act, body)

        @block.vector
        def _(dve):
            nc.vector.memset(k.big1[:, :], 0.0).then_inc(setup, 1)
            nc.vector.memset(ve[:, :, :, :], 1.0).then_inc(setup, 1)
            nc.vector.memset(carry[:, :], -BIG).then_inc(setup, 1)
            dve.wait_ge(setup, 3)
            word = [None]

            def keys(r, z, j):
                g, slot = j % 2, j % KV_SLOTS
                dve.wait_ge(y_done, r.at(S, j + 1))
                nc.vector.tensor_tensor(kj[:, j % 4, :], p_y[:, g, 0:D], kv[:, slot, 0:D], ALU.add).then_inc(kj_done, 1)

            def values(r, z, j):
                g, slot = j % 2, j % KV_SLOTS
                nc.vector.tensor_tensor(
                    ve[:, z, j, :].rearrange("p (h c) -> p h c", c=CE)[:, :, 0:C],
                    p_y[:, g, 0:D].rearrange("p (h c) -> p h c", c=C),
                    kv[:, slot, D:2 * D].rearrange("p (h c) -> p h c", c=C), ALU.add).then_inc(ve_done, 1)

            def multiply(r, z, j):
                dve.wait_ge(kj_done, r.at(S, j + 1))
                nc.vector.tensor_tensor(kj[:, j % 4, :], p_y[:, j % 2, D:2 * D], kj[:, j % 4, :], ALU.mult)\
                    .then_inc(prod_done, 1)

            def reduce(r, z, j, waits=False):
                if j == 0 and r.has(1):
                    dve.wait_ge(st_done, r.at(1, 0))
                if waits:
                    dve.wait_ge(prod_done, r.at(S, j + 1))
                nc.vector.tensor_reduce(score[:, j * H:(j + 1) * H],
                                        kj[:, j % 4, :].rearrange("p (h c) -> p h c", c=C), AX.X, ALU.add)\
                    .then_inc(score_done, 1)

            def add(p, i):
                block_of = block_no(dve, k, p, i, word, known=i == 0)
                to = k.big1[:, bass.ds(block_of * (H * CE), H * CE)]
                dve.wait_ge(sum_done, p.at(S, i + 1))
                if i:
                    dve.wait_ge(add_done, p.at(S, i))
                nc.vector.tensor_tensor(to, p_sum[:, i % 2, 0:H * CE], to, ALU.add).then_inc(add_done, 1)

            def message(p, y, i):
                if i == 0:
                    dve.wait_ge(p_ready, p.at(1, 1))
                nc.vector.tensor_tensor(msg[:, i % 4, :].rearrange("p (h c) -> p h c", c=CE),
                                        ve[:, y, i, :].rearrange("p (h c) -> p h c", c=CE),
                                        bcast(p_p[:, i * H:(i + 1) * H], CE), ALU.mult).then_inc(msg_done, 1)

            def chain(p, y, j, line):
                if j == 1:
                    dve.wait_ge(st_done, p.at(1, 1))
                    dve.wait_ge(fl_in, p.at(16, 16))
                    if p.has(1):
                        dve.wait_ge(p_ready, p.at(1, 0))
                    line(nc.vector.tensor_tensor(sc[:, :], p_st, fl[:, 3 * P + 1:NFLAG], ALU.add))
                    line(nc.vector.tensor_tensor_scan(run[:, :], fl[:, 0:P], sc[:, :], -BIG, ALU.add, ALU.max))
                    line(nc.vector.tensor_tensor_scan(top[:, ::-1], fl[:, 1:P + 1][:, ::-1], run[:, ::-1], -BIG,
                                                      ALU.add, ALU.max))
                    line.on(nc.vector.tensor_scalar(u[:, 0:2 * S:2], k.of_step[:, :], top[:, 0:1], None, ALU.mult))
                    nc.vector.tensor_scalar(u[:, 1:2 * S:2], k.of_step[:, :], top[:, P - 1:P], None, ALU.mult)\
                        .then_inc(u_ready, 1)
                if j == 3:
                    dve.wait_ge(u_done, p.at(1, 1))
                    line.on(nc.vector.tensor_copy(cin[:, 0:1], carry[:, :]))
                    line(nc.vector.tensor_copy(cin[:, 1:CH - 1], p_u))
                    flags = cfl[:, y, :]
                    line(nc.vector.tensor_tensor_scan(cf[:, :], flags[:, 0:CH - 1], cin[:, :], -BIG, ALU.add, ALU.max))
                    nc.vector.tensor_tensor_scan(cb[:, ::-1], flags[:, 1:CH][:, ::-1], cf[:, ::-1], -BIG,
                                                 ALU.add, ALU.max).then_inc(c_ready, 1)
                    dve.wait_ge(c_ready, p.at(1, 1))
                    line.on(nc.vector.tensor_copy(carry[:, :], cb[:, CH - 2:CH - 1]))
                    nc.vector.tensor_tensor(fd[:, :], cin[:, 0:1], cb[:, 0:1], ALU.subtract).then_inc(fd_ready, 1)
                if j == 6:
                    dve.wait_ge(fe_ready, p.at(1, 1))
                    dve.wait_ge(dd_ready, p.at(1, 1))
                    line.on(nc.vector.tensor_scalar(oh8, k.iota[0:H, :], k.straddler[:, bass.ds(p.at(1), 1)], None,
                                                 ALU.is_equal))
                    line(nc.vector.tensor_scalar(fe[:, :], fe[:, :], -1.0, None, ALU.add))
                    nc.vector.tensor_scalar(sel8[:, :], k.ident[0:H, 0:H], fe[:, :], None, ALU.mult).then_inc(sel_ready, 1)
                if j == 5:
                    dve.wait_ge(top_done, p.at(1, 1))
                    for c, step in enumerate((line.on, line)):
                        step(nc.vector.tensor_tensor_reduce(
                            out=u[:, c * S:(c + 1) * S], in0=p_top[:, 1 + c:CH - 1:2], in1=k.of_step[:, :], scale=1.0, scalar=0.0,
                            op0=ALU.mult, op1=ALU.add, accum_out=mf[:, c:c + 1]))
                    for c in range(2):
                        line(nc.vector.scalar_tensor_tensor(
                            out=top[:, :], in0=fl[:, (c + 1) * P + 1:(c + 2) * P + 1], scalar=mf[:, c:c + 1],
                            in1=top[:, :], op0=ALU.add, op1=ALU.max))
                    nc.vector.tensor_tensor(run[:, :], sc[:, :], top[:, :], ALU.subtract).then_inc(dd_ready, 1)
                if j == 9:
                    dve.wait_ge(f_done, p.at(1, 1))
                    to = k.big1[:, bass.ds(block_no(dve, k, p, 0, word) * (H * CE), H * CE)]\
                        .rearrange("p (h c) -> p h c", c=CE)
                    if p.has(1):
                        dve.wait_ge(add_done, p.at(S, 0))
                    line(nc.vector.scalar_tensor_tensor(out=to, in0=bcast(p_f, CE), scalar=1.0, in1=to, op0=ALU.add,
                                                        op1=ALU.mult))

            def body(r, z, here, prev, late):
                p, y = r.before(), 1 - z
                line = Line(dve, chain_line, p.at(NLINE) if prev else 0)
                for j in range(S):
                    adds = [(p, i) for i in SUM_AT.get(j, ()) if prev] + [(p.before(), i) for i in LATE_AT.get(j, ()) if late]
                    for q, i in adds[:1]:
                        add(q, i)
                    if here:
                        keys(r, z, j)
                    for q, i in adds[1:]:
                        add(q, i)
                    if here:
                        values(r, z, j)
                        multiply(r, z, j)
                    if here and j:
                        reduce(r, z, j - 1)
                    if prev:
                        chain(p, y, j, line)
                        for i in MSG_AT.get(j, ()):
                            message(p, y, i)
                if here:
                    reduce(r, z, S - 1, waits=True)
                assert not prev or line.n == NLINE, line.n

            edge_rounds(dve, body)


def finish_attention(nc, b, k):
    with ExitStack() as ctx:
        sb, ps, sem = allocators(nc, ctx)
        xr = sb("x_skip_blk", [P, 2, D])
        x = sb("x1_blk", [P, 2, D])
        carrier = sb("wait_carrier2", [1, 2])
        den = sb("den", [P, 2, H])
        out = sb("att_out", [P, 2, D])
        six = sb("six2", [P, 2, 6])
        mv = sb("mv2", [P, 2, 2])
        sd = sb("sd2", [P, 2, 1])
        rs = sb("rs2", [P, 2, 1])
        nm = sb("nm2", [P, 2, 1])
        junk = sb("sq_junk", [P, 2, D])
        x_in = [sem(f"xr_in{z}") for z in range(2)]
        out_done = [sem(f"x1_out{z}") for z in range(2)]
        x1_ready, var_ready, sd_ready, norm_ready = sem("x1_ready"), sem("var2_ready"), sem("sd2_ready"), sem("norm2_ready")
        h_ready, sq_ready, line_sem = sem("h2_ready"), sem("sq_ready"), sem("fin_dve_line")
        norm_line, h2_out = sem("fin_norm_line"), sem("h2_out")
        block = ctx.enter_context(nc.Block())

        @block.sync
        def _(sp):
            def store(r, z):
                n = rows_of(r)
                sp.wait_ge(x1_ready, r.at(1, 1))
                sp.dma_start(b.xs[bass.ds(r.at(P), n), :], x[0:n, z, :]).then_inc(out_done[z], 16)

            def store_h2(r):
                n = rows_of(r)
                sp.wait_ge(h_ready, r.at(1, 1))
                sp.dma_start(b.h2[bass.ds(r.at(P), n), :], k.big2[0:n, bass.ds(r.at(D + 1), D)])\
                    .then_inc(h2_out, 16)

            def body(r, z):
                n = rows_of(r)
                if r.has(2):
                    sp.wait_ge(x1_ready, r.at(1, -1))
                sp.dma_start(xr[0:n, z, :], b.xs[bass.ds(r.at(P), n), :]).then_inc(x_in[z], 16)
                if r.has(1):
                    store(r.before(), 1 - z)
                if r.has(2):
                    store_h2(r.before().before())

            rounds(sp, BLOCKS, body)
            store(Round(None, BLOCKS - 1), 0)
            store_h2(Round(None, BLOCKS - 2))
            store_h2(Round(None, BLOCKS - 1))
            sp.wait_ge(out_done[0], 16 * 25)
            sp.wait_ge(out_done[1], 16 * 24)
            sp.wait_ge(h2_out, 16 * BLOCKS)

        @block.vector
        def _(dve):
            per = 5

            def front(r, z):
                line = Line(dve, line_sem, r.at(per))
                sums = k.big1[:, bass.ds(r.at(H * CE), H * CE)].rearrange("p (h c) -> p h c", c=CE)
                line(nc.vector.tensor_scalar(den[:, z, :], sums[:, :, C], 1e-16, None, ALU.add))
                line(nc.vector.reciprocal(den[:, z, :], den[:, z, :]))
                line(nc.vector.tensor_tensor(out[:, z, :].rearrange("p (h c) -> p h c", c=C), sums[:, :, 0:C],
                                             bcast(den[:, z, :], C), ALU.mult))
                dve.wait_ge(x_in[z], r.half(16, 16))
                if r.has(2):
                    dve.wait_ge(out_done[z], r.half(16, 0))
                    dve.wait_ge(h_ready, r.at(1, -1))
                nc.vector.tensor_tensor(x[:, z, :], out[:, z, :], xr[:, z, :], ALU.add).then_inc(x1_ready, 1)
                dve.wait_ge(x1_ready, r.at(1, 1))
                line(nc.vector.bn_stats(six[:, z, :], x[:, z, :]))
                nc.vector.memset(carrier[:, z:z + 1], 0.0)
                line(nc.vector.bn_aggr(mv[:, z, :], six[:, z, :]))
                nc.vector.tensor_scalar(mv[:, z, 1:2], mv[:, z, 1:2], LN_EPS, None, ALU.add).then_inc(var_ready, 1)

            def norm(r, z):
                line = Line(dve, norm_line, r.at(1))
                dve.wait_ge(sd_ready, r.at(1, 1))
                line(nc.vector.reciprocal(rs[:, z, :], sd[:, z, :]))
                nc.vector.scalar_tensor_tensor(out=nm[:, z, :], in0=mv[:, z, 0:1], scalar=-1.0, in1=rs[:, z, :],
                                               op0=ALU.mult, op1=ALU.mult).then_inc(norm_ready, 1)

            def body(r, z):
                if r.m is not None or r.a + 1 < BLOCKS:
                    front(r.after(), 1 - z)
                norm(r, z)

            front(Round(None, 0), 0)
            rounds(dve, BLOCKS, body)

        @block.scalar
        def _(act):
            def deviation(r, z):
                act.wait_ge(var_ready, r.at(1, 1))
                nc.scalar.activation(sd[:, z, :], mv[:, z, 1:2], ACT.Sqrt).then_inc(sd_ready, 1)

            def body(r, z):
                if r.m is not None or r.a + 1 < BLOCKS:
                    deviation(r.after(), 1 - z)
                act.wait_ge(norm_ready, r.at(1, 1))
                rows = k.big2[:, bass.ds(r.at(D + 1), D)]
                nc.scalar.activation(rows, x[:, z, :], ACT.Relu, bias=nm[:, z, :], scale=rs[:, z, :]).then_inc(h_ready, 1)
                act.wait_ge(h_ready, r.at(1, 1))
                if r.has(2):
                    act.wait_ge(sq_ready, r.at(1, -1))
                nc.scalar.activation(junk[:, z, :], rows, ACT.Square,
                                     accum_out=k.big2[:, bass.ds(r.at(D + 1, D), 1)]).then_inc(sq_ready, 1)

            deviation(Round(None, 0), 0)
            rounds(act, BLOCKS, body)


def weights_by_step(nc, b, k):
    a = b.a
    with ExitStack() as ctx:
        sb, ps, sem = allocators(nc, ctx)
        wg = sb("w_gathered", [P, COLS, P])
        p_tr = ps("p_wtr", [P, P])
        table_out, gathered, turned, copied = sem("w_table_out"), sem("w_gathered_sem"), sem("w_turned"), sem("w_copied")
        block = ctx.enter_context(nc.Block())

        @block.sync
        def _(sp):
            sp.dma_start(b.wtp[0:TILES - 1, :],
                         a["edge_weight"][0:(TILES - 1) * P].rearrange("(t e) -> t e", e=P)).then_inc(table_out, 16)
            sp.dma_start(b.wtp[TILES - 1:TILES, :],
                         a["edge_weight"][E - P:E].rearrange("(o e) -> o e", o=1)).then_inc(table_out, 16)

        @block.gpsimd
        def _(pool):
            pool.wait_ge(table_out, 32)
            for c in range(COLS):
                pool.indirect_dma_start(out=wg[:, c, :], out_offset=None, in_=b.wtp,
                                        in_offset=bass.IndirectOffsetOnAxis(ap=k.tile_of[:, c:c + 1], axis=0))\
                    .then_inc(gathered, 16)

        @block.tensor
        def _(pe):
            pe.wait_ge(gathered, 16 * COLS)
            for c in range(COLS):
                if c:
                    pe.wait_ge(copied, c)
                nc.tensor.transpose(p_tr[:, :], wg[:, c, :], k.ident[:, :]).then_inc(turned, 1)

        @block.vector
        def _(dve):
            nc.vector.memset(k.big1[:, :], 0.0)
            for c in range(COLS):
                dve.wait_ge(turned, c + 1)
                nc.vector.tensor_copy(k.wt[:, c * P:(c + 1) * P], p_tr[:, :]).then_inc(copied, 1)


def artanh_ratio_tail(nc, line, out, ln, isn, z, t, mask):
    V = nc.vector
    line.on(V.scalar_tensor_tensor(out=out, in0=ln, scalar=0.5, in1=isn, op0=ALU.mult, op1=ALU.mult))
    line(V.tensor_tensor(z, z, z, ALU.mult))
    line.on(V.tensor_scalar(mask, z, 1e-3, None, ALU.is_lt))
    line(V.tensor_scalar(t, z, 1.0 / 7, 1.0 / 5, ALU.mult, ALU.add))
    line(V.tensor_tensor(t, t, z, ALU.mult))
    line(V.scalar_tensor_tensor(out=t, in0=t, scalar=1.0 / 3, in1=z, op0=ALU.add, op1=ALU.mult))
    line(V.scalar_tensor_tensor(out=t, in0=t, scalar=1.0, in1=out, op0=ALU.add, op1=ALU.subtract))
    line(V.tensor_tensor(t, t, mask, ALU.mult))
    line(V.tensor_tensor(out, out, t, ALU.add))


def aggregate(nc, b, k):
    with ExitStack() as ctx:
        sb, ps, sem = allocators(nc, ctx)
        xs = sb("xs", [P, 2, S, D + 1])
        idx = sb("idx2", [P, 2, S], I32)
        carrier = sb("wait_carrier4", [1, S])
        wt = sb("wt_b", [P, 2, S])
        oh = sb("oh2", [P, 2, S, P])
        oht = sb("oht2", [P, 2, P])
        junk = sb("dot_junk", [P, 2, D])
        sqj = sb("sqj", [P, 2, D])
        xy = sb("xy", [P, 2, S])
        x2 = sb("x2", [P, 2, S])
        y2 = sb("y2", [P, 2, S])
        tmp = [sb(f"edge_t{i}", [P, S]) for i in range(13)]
        ca, cb_, dn, bc, sn, zc, rat, ln, c2, t, mask, lam, isn = [v[:, :] for v in tmp]
        p_x = ps("p_x2", [P, 2, 512])
        p_y = ps("p_y2", [P, 2, 512])
        p_sum = ps("p_sum2", [P, 4, 512])
        xs_in = [sem(f"xs_in{i}") for i in range(KV_SLOTS)]
        idx_ready, oh_ready = sem("idx2_ready"), sem("oh2_ready")
        turned, oht_ready, y_done, x2_done, y2_done = (
            sem(n) for n in ("turned2", "oht2_ready", "y2_mm", "x2_done", "y2_done"))
        sq_ready, sn_ready, rat_ready, ln_ready, c_ready = (
            sem(n) for n in ("n2_ready", "sn_ready", "rat_ready", "ln_ready", "c12_ready"))
        scaled_done, sum_done, add_done, line_sem = sem("rows_scaled"), sem("sum2_done"), sem("add2_done"), sem("edge_line")
        block = ctx.enter_context(nc.Block())
        NLINE = 38

        @block.gpsimd
        def _(pool):
            def body(r, z, here, prev, late):
                if not here:
                    return
                nc.gpsimd.tensor_copy(idx[:, z, :], k.src[:, bass.ds(r.at(S), S)]).then_inc(idx_ready, 1)
                nc.gpsimd.tensor_copy(wt[:, z, :], k.wt[:, bass.ds(r.at(S), S)]).then_inc(idx_ready, 1)
                pool.wait_ge(idx_ready, r.at(2, 2))
                for j in range(S):
                    slot = j % KV_SLOTS
                    if r.has(1) or j >= KV_SLOTS:
                        pool.wait_ge(x2_done, r.at(S, j + 1 - KV_SLOTS))
                        pool.wait_ge(y2_done, r.at(S, j + 1 - KV_SLOTS))
                    if r.has(2):
                        pool.wait_ge(sum_done, r.at(S, j + 1 - 2 * S))
                    nc.gpsimd.tensor_tensor(carrier[:, j:j + 1], k.iota[0:1, 0:1], k.iota[0:1, 0:1], ALU.add)
                    pool.indirect_dma_start(
                        out=xs[:, z, j, 0:D], out_offset=None, in_=b.h2,
                        in_offset=bass.IndirectOffsetOnAxis(ap=idx[:, z, j:j + 1], axis=0)).then_inc(xs_in[slot], 16)

            edge_rounds(pool, body)

        @block.tensor
        def _(pe):
            word = [None]

            def turn(r, z, j):
                if j % CHUNK == 0:
                    pe.wait_ge(oh_ready, r.at(S // CHUNK, j // CHUNK + 1))
                nc.tensor.transpose(p_x[:, j % 2, 0:P], oh[:, z, j, :], k.ident[:, :]).then_inc(turned, 1)

            def product(r, z, j):
                block_of = block_no(pe, k, r, j, word)
                if r.has(1) or j >= 2:
                    pe.wait_ge(x2_done, r.at(S, j - 1))
                pe.wait_ge(oht_ready, r.at(S, j + 1))
                nc.tensor.matmul(p_y[:, j % 2, 0:D + 1], oht[:, j % 2, :], k.big2[:, bass.ds(block_of * (D + 1), D + 1)],
                                 start=True, stop=True).then_inc(y_done, 1)

            def sums(p, y, i):
                if i % 2 == 0:
                    if p.has(1) or i >= 4:
                        pe.wait_ge(add_done, p.at(S, i - 2))
                    pe.wait_ge(scaled_done, p.at(S, i + 2))
                nc.tensor.matmul(p_sum[:, i % 4, 0:D + 1], oh[:, y, i, :], xs[:, y, i, :],
                                 start=True, stop=True).then_inc(sum_done, 1)

            def body(r, z, here, prev, late):
                p, y = r.before(), 1 - z
                for j in range(S):
                    if here and j == 0:
                        turn(r, z, 0)
                    if here and j + 1 < S:
                        turn(r, z, j + 1)
                    if here:
                        product(r, z, j)
                    if late:
                        for i in LATE_AT.get(j, ()):
                            sums(p.before(), z, i)
                    if prev:
                        for i in SUM_AT.get(j, ()):
                            sums(p, y, i)

            edge_rounds(pe, body)

        @block.scalar
        def _(act):
            def scale_row(p, y, i):
                if i == 0:
                    act.wait_ge(c_ready, p.at(1, 1))
                nc.scalar.activation(xs[:, y, i, 0:D], xs[:, y, i, 0:D], ACT.Copy, scale=c2[:, i:i + 1])\
                    .then_inc(scaled_done, 1)

            def body(r, z, here, prev, late):
                p, y = r.before(), 1 - z
                for j in range(S):
                    for i in ([0, 1] if j == 0 else [j + 1] if j + 1 < S else []) if here else ():
                        act.wait_ge(turned, r.at(S, i + 1))
                        if r.has(1) or i >= 2:
                            act.wait_ge(y_done, r.at(S, i - 1))
                        nc.scalar.copy(oht[:, i % 2, :], p_x[:, i % 2, 0:P]).then_inc(oht_ready, 1)
                    if here:
                        if r.has(1) or j >= 2:
                            act.wait_ge(y2_done, r.at(S, j - 1))
                        if j == 0 and r.has(2):
                            act.wait_ge(c_ready, r.at(1, -1))
                        act.wait_ge(xs_in[j % KV_SLOTS], r.at(16 * (S // KV_SLOTS), 16 * (j // KV_SLOTS + 1)))
                        nc.scalar.activation(sqj[:, j % 2, :], xs[:, z, j, 0:D], ACT.Square,
                                             accum_out=y2[:, z, j:j + 1]).then_inc(y2_done, 1)
                    if prev and j == 3:
                        act.wait_ge(sq_ready, p.at(1, 1))
                        nc.scalar.activation(sn, sn, ACT.Sqrt).then_inc(sn_ready, 1)
                    if prev and j == 5:
                        act.wait_ge(rat_ready, p.at(1, 1))
                        nc.scalar.activation(ln, rat, ACT.Ln).then_inc(ln_ready, 1)
                    if prev:
                        for i in MSG_AT.get(j, ()):
                            scale_row(p, y, i)

            edge_rounds(act, body)

        @block.vector
        def _(dve):
            word = [None]
            V = nc.vector

            def dot(r, z, j):
                dve.wait_ge(xs_in[j % KV_SLOTS], r.at(16 * (S // KV_SLOTS), 16 * (j // KV_SLOTS + 1)))
                dve.wait_ge(y_done, r.at(S, j + 1))
                V.tensor_tensor_reduce(out=junk[:, j % 2, :], in0=p_y[:, j % 2, 0:D], in1=xs[:, z, j, 0:D], scale=1.0,
                                       scalar=0.0, op0=ALU.mult, op1=ALU.add, accum_out=xy[:, z, j:j + 1])
                V.tensor_copy(x2[:, z, j:j + 1], p_y[:, j % 2, D:D + 1]).then_inc(x2_done, 1)

            def coefficients(p, y, j, line):
                w = wt[:, y, :]
                X2, Y2, XY = x2[:, y, :], y2[:, y, :], xy[:, y, :]
                if j == 0:
                    dve.wait_ge(x2_done, p.at(S, S))
                    dve.wait_ge(y2_done, p.at(S, S))
                    line.on(V.tensor_scalar(t, XY, -2.0, 1.0, ALU.mult, ALU.add))
                    line.on(V.tensor_scalar(bc, X2, -1.0, 1.0, ALU.mult, ALU.add))
                    line(V.tensor_tensor(dn, X2, Y2, ALU.mult))
                    line.on(V.tensor_tensor(ca, t, Y2, ALU.add))
                    line.on(V.tensor_tensor(cb_, bc, XY, ALU.mult))
                    line(V.tensor_tensor(dn, dn, t, ALU.add))
                if j == 1:
                    line.on(V.tensor_tensor(sn, ca, X2, ALU.mult))
                    line(V.tensor_scalar(dn, dn, MIN_NORM, None, ALU.max))
                    line.on(V.scalar_tensor_tensor(out=sn, in0=cb_, scalar=-2.0, in1=sn, op0=ALU.mult, op1=ALU.add))
                    line(V.reciprocal(dn, dn))
                    line.on(V.tensor_tensor(sn, sn, ca, ALU.mult))
                    line(V.tensor_tensor(cb_, bc, Y2, ALU.mult))
                    line.on(V.tensor_scalar(lam, bc, MIN_NORM, None, ALU.max))
                    line(V.tensor_tensor(cb_, bc, cb_, ALU.mult))
                    line.on(V.reciprocal(lam, lam))
                    line(V.tensor_tensor(sn, sn, cb_, ALU.add))
                    line.on(V.tensor_scalar(lam, lam, 2.0, MIN_NORM, ALU.mult, ALU.max))
                    line(V.tensor_tensor(sn, sn, dn, ALU.mult))
                    line(V.tensor_tensor(sn, sn, dn, ALU.mult))
                    V.tensor_scalar(sn, sn, 0.0, None, ALU.max).then_inc(sq_ready, 1)
                if j == 3:
                    dve.wait_ge(sn_ready, p.at(1, 1))
                    line.on(V.reciprocal(lam, lam))
                    line(V.tensor_scalar(sn, sn, MIN_NORM, None, ALU.max))
                    line(V.tensor_scalar(zc, sn, CLIP, None, ALU.min))
                    line(V.tensor_scalar(t, zc, -1.0, 1.0, ALU.mult, ALU.add))
                    line(V.reciprocal(t, t))
                    V.scalar_tensor_tensor(out=rat, in0=zc, scalar=1.0, in1=t, op0=ALU.add, op1=ALU.mult)\
                        .then_inc(rat_ready, 1)
                if j == 4:
                    line.on(V.scalar_tensor_tensor(out=lam, in0=lam, scalar=2.0, in1=w, op0=ALU.mult, op1=ALU.mult))
                    line(V.reciprocal(isn, sn))
                    line(V.tensor_tensor(lam, lam, dn, ALU.mult))
                if j == 5:
                    dve.wait_ge(ln_ready, p.at(1, 1))
                    artanh_ratio_tail(nc, line, rat, ln, isn, zc, t, mask)
                if j == 6:
                    line(V.tensor_tensor(t, lam, rat, ALU.mult))
                    line(V.scalar_tensor_tensor(out=xs[:, y, :, D], in0=t, scalar=-1.0, in1=ca, op0=ALU.mult, op1=ALU.mult))
                    V.tensor_tensor(c2, t, bc, ALU.mult).then_inc(c_ready, 1)

            def one_hots(r, z, c):
                V.tensor_tensor(oh[:, z, c * CHUNK:(c + 1) * CHUNK, :],
                                k.iota[:, :].unsqueeze(1).to_broadcast([P, CHUNK, P]),
                                bcast(k.loc[:, bass.ds(r.at(S, c * CHUNK), CHUNK)], P), ALU.is_equal).then_inc(oh_ready, 1)

            def add(p, i):
                block_of = block_no(dve, k, p, i, word)
                to = k.big1[:, bass.ds(block_of * (D + 1), D + 1)]
                dve.wait_ge(sum_done, p.at(S, i + 1))
                if p.has(1) or i:
                    dve.wait_ge(add_done, p.at(S, i))
                V.tensor_tensor(to, p_sum[:, i % 4, 0:D + 1], to, ALU.add).then_inc(add_done, 1)

            def body(r, z, here, prev, late):
                p, y = r.before(), 1 - z
                line = Line(dve, line_sem, p.at(NLINE) if prev else 0)
                if here and not r.has(1):
                    one_hots(r, z, 0)
                for j in range(S):
                    adds = [(p, i) for i in SUM_AT.get(j, ()) if prev] + [(p.before(), i) for i in LATE_AT.get(j, ()) if late]
                    for q, i in adds[:1]:
                        add(q, i)
                    if here:
                        dot(r, z, j)
                    for q, i in adds[1:]:
                        add(q, i)
                    if here and j % CHUNK == 0 and j + CHUNK < S:
                        one_hots(r, z, j // CHUNK + 1)
                    if here and j + CHUNK == S and (r.m is not None or r.a + 1 < BATCHES):
                        one_hots(r.after(), 1 - z, 0)
                    if prev:
                        coefficients(p, y, j, line)
                assert not prev or line.n == NLINE, line.n

            edge_rounds(dve, body)


def hyperbolic_layer(nc, b, k, out):
    a = b.a
    with ExitStack() as ctx:
        sb, ps, sem = allocators(nc, ctx)
        w_rows = sb("w_rows", [P, HALF, D])
        wT = sb("w_turned_t", [P, HALF, D])
        bias = sb("bias1", [P, D])
        ball = sb("ball", [P, D])
        junk = sb("junk5", [P, 2, D])
        junk2 = sb("junk6", [P, 2, D])
        part = sb("part", [P, 2, D])
        u = sb("u_blk", [P, 2, D])
        ut = sb("ut_blk", [P, 2, D])
        xr = sb("xr_blk", [P, 2, D])
        tabs = {n: sb(f"t_{n}", [P, BLOCKS])[:, :] for n in
                ("n2", "xa", "u2", "m2", "mb", "h2", "t2", "a", "b", "c", "d", "e", "f", "g", "w", "v", "x2")}
        one = {n: sb(f"o_{n}", [P, 1])[:, :] for n in ("n2", "n", "th", "b2", "r")}
        p_w = ps("p_w", [P, 2, 512])
        p_ut = ps("p_ut", [P, 2, 512])
        p_m = ps("p_m", [P, 2, 512])
        V, A = nc.vector, nc.scalar
        sums = k.big1[:, 0:BLOCKS * (D + 1)].rearrange("p (b c) -> p b c", c=D + 1)
        rows_x2 = k.big2[:, :].rearrange("p (b c) -> p b c", c=D + 1)[:, :, D]

        def sums_of(r):
            return k.big1[:, bass.ds(r.at(D + 1), D)]

        def rows_of_block(r):
            return k.big2[:, bass.ds(r.at(D + 1), D)]

        def col(name, r):
            return tabs[name][:, bass.ds(r.at(1), 1)]

        def phase(name, engines):
            with ExitStack() as c:
                sems = {}

                def s(n):
                    if n not in sems:
                        sems[n] = c.enter_context(nc.semaphore(f"{name}_{n}"))
                    return sems[n]

                block = c.enter_context(nc.Block())
                for e, fn in engines.items():
                    engine = {"sync": block.sync, "vector": block.vector, "scalar": block.scalar,
                              "tensor": block.tensor}[e]
                    engine(lambda eng, fn=fn: fn(eng, s))

        def p1_dve(dve, s):
            def body(r, z):
                to = sums_of(r)
                V.scalar_tensor_tensor(out=to, in0=rows_of_block(r), scalar=k.big1[:, bass.ds(r.at(D + 1, D), 1)],
                                       in1=to, op0=ALU.mult, op1=ALU.add).then_inc(s("first"), 1)
                dve.wait_ge(s("first"), r.at(1, 1))
                if r.has(2):
                    dve.wait_ge(s("fourth"), r.at(1, -1))
                V.tensor_tensor(junk[:, z, :], to, rows_of_block(r), ALU.mult).then_inc(s("second"), 1)
            rounds(dve, BLOCKS, body)

        def p1_act(act, s):
            def body(r, z):
                act.wait_ge(s("first"), r.at(1, 1))
                if r.has(2):
                    act.wait_ge(s("third"), r.at(1, -1))
                A.activation(junk2[:, z, :], sums_of(r), ACT.Square, accum_out=col("n2", r)).then_inc(s("third"), 1)
                act.wait_ge(s("second"), r.at(1, 1))
                A.activation(junk[:, z, :], junk[:, z, :], ACT.Copy, accum_out=col("xa", r)).then_inc(s("fourth"), 1)
            rounds(act, BLOCKS, body)

        def p1_sp(sp, s):
            sp.dma_start(w_rows[:, :, :], a["L1_gnn_weight"].rearrange("(c p) n -> p c n", p=P)).then_inc(s("in0"), 16)
            sp.dma_start(bias[:, :], a["L1_gnn_bias"].partition_broadcast(P)).then_inc(s("in0"), 16)
            sp.wait_ge(s("in0"), 32)

        phase("sum_pass", {"sync": p1_sp, "vector": p1_dve, "scalar": p1_act})

        def q1_dve(dve, s):
            line = Line(dve, s("line"))
            T = tabs
            line(V.tensor_copy(T["x2"], rows_x2))
            dve.wait_ge(s("first"), 1)
            line(V.tensor_scalar(T["a"], T["a"], MIN_NORM, None, ALU.max))
            line(V.tensor_scalar(T["b"], T["x2"], -1.0, 1.0, ALU.mult, ALU.add))
            line(V.tensor_scalar(T["c"], T["b"], MIN_NORM, None, ALU.max))
            line(V.reciprocal(T["c"], T["c"]))
            line(V.tensor_scalar(T["c"], T["c"], 2.0, MIN_NORM, ALU.mult, ALU.max))
            line(V.scalar_tensor_tensor(out=T["d"], in0=T["a"], scalar=0.5, in1=T["c"], op0=ALU.mult, op1=ALU.mult))
            V.reciprocal(T["c"], T["a"]).then_inc(s("second"), 1)
            dve.wait_ge(s("third"), 1)
            dve.wait_ge(s("second"), 1)
            line(V.tensor_tensor(T["d"], T["d"], T["c"], ALU.mult))
            line(V.tensor_tensor(T["e"], T["d"], T["xa"], ALU.mult))
            line(V.tensor_tensor(T["f"], T["n2"], T["d"], ALU.mult))
            line(V.tensor_tensor(T["f"], T["f"], T["d"], ALU.mult))
            line(V.tensor_scalar(T["e"], T["e"], 2.0, 1.0, ALU.mult, ALU.add))
            line(V.tensor_tensor(T["g"], T["x2"], T["f"], ALU.mult))
            line(V.tensor_tensor(T["g"], T["g"], T["e"], ALU.add))
            line(V.tensor_scalar(T["g"], T["g"], MIN_NORM, None, ALU.max))
            line(V.reciprocal(T["g"], T["g"]))
            line(V.tensor_tensor(T["e"], T["e"], T["f"], ALU.add))
            line(V.tensor_tensor(T["v"], T["e"], T["g"], ALU.mult))
            line(V.tensor_tensor(T["b"], T["b"], T["g"], ALU.mult))
            line(V.tensor_tensor(T["w"], T["b"], T["d"], ALU.mult))
            dve.wait_ge(s("fourth"), 1)
            line(V.tensor_scalar(one["n"], one["n"], MIN_NORM, None, ALU.max))
            V.reciprocal(one["r"], one["n"]).then_inc(s("fifth"), 1)
            dve.wait_ge(s("sixth"), 1)
            dve.wait_ge(s("fifth"), 1)
            line(V.tensor_tensor(one["r"], one["r"], one["th"], ALU.mult))
            line(V.tensor_scalar(ball[:, :], bias[:, :], one["r"], None, ALU.mult))
            line(V.tensor_tensor_reduce(out=junk[:, 0, :], in0=ball[:, :], in1=ball[:, :], scale=1.0, scalar=0.0,
                                        op0=ALU.mult, op1=ALU.add, accum_out=one["b2"]))
            for c in range(HALF):
                dve.wait_ge(s("ready"), c + 1)
                line(V.tensor_copy(wT[:, c, :], p_w[:, c, 0:D]))

        def q1_act(act, s):
            line = Line(act, s("act_line"))
            line(A.activation(tabs["a"], tabs["n2"], ACT.Sqrt))
            A.activation(junk2[:, 0, :], bias[:, :], ACT.Square, accum_out=one["n2"]).then_inc(s("first"), 1)
            act.wait_ge(s("first"), 1)
            A.activation(one["n"], one["n2"], ACT.Sqrt).then_inc(s("fourth"), 1)
            act.wait_ge(s("second"), 1)
            A.activation(tabs["d"], tabs["d"], ACT.Tanh).then_inc(s("third"), 1)
            act.wait_ge(s("fifth"), 1)
            A.activation(one["th"], one["n"], ACT.Tanh).then_inc(s("sixth"), 1)

        def q1_pe(pe, s):
            for c in range(HALF):
                for o in range(HALF):
                    last = nc.tensor.transpose(p_w[:, c, o * P:(o + 1) * P], w_rows[:, o, c * P:(c + 1) * P],
                                               k.ident[:, :])
                last.then_inc(s("ready"), 1)

        phase("expmap", {"vector": q1_dve, "scalar": q1_act, "tensor": q1_pe})

        def p2_act(act, s):
            def multiply(r, z):
                if r.has(2):
                    act.wait_ge(s("second"), r.at(1, -1))
                A.activation(part[:, z, :], rows_of_block(r), ACT.Copy, scale=col("v", r)).then_inc(s("first"), 1)

            def body(r, z):
                multiply(r, z)
                act.wait_ge(s("second"), r.at(1, 1))
                if r.has(2):
                    act.wait_ge(s("act_line"), r.at(2, -2))
                A.activation(junk2[:, z, :], u[:, z, :], ACT.Square, accum_out=col("u2", r)).then_inc(s("act_line"), 1)
                act.wait_ge(s("third"), r.at(1, 1))
                A.copy(ut[:, z, :], p_ut[:, z, 0:D]).then_inc(s("fourth"), 1)
                act.wait_ge(s("sixth"), r.at(1, 1))
                act.wait_ge(s("act_line"), r.at(2, 1))
                A.activation(junk2[:, z, :], sums_of(r), ACT.Square, accum_out=col("m2", r)).then_inc(s("act_line"), 1)
                act.wait_ge(s("ready"), r.at(1, 1))
                A.activation(junk[:, z, :], junk[:, z, :], ACT.Copy, accum_out=col("mb", r)).then_inc(s("dotted"), 1)
            rounds(act, BLOCKS, body)

        def p2_dve(dve, s):
            def body(r, z):
                dve.wait_ge(s("first"), r.at(1, 1))
                if r.has(2):
                    dve.wait_ge(s("third"), r.at(1, -1))
                    dve.wait_ge(s("act_line"), r.at(2, -2))
                V.scalar_tensor_tensor(out=u[:, z, :], in0=sums_of(r), scalar=col("w", r), in1=part[:, z, :],
                                       op0=ALU.mult, op1=ALU.add).then_inc(s("second"), 1)
                dve.wait_ge(s("fifth"), r.at(1, 1))
                dve.wait_ge(s("second"), r.at(1, 1))
                V.tensor_scalar(sums_of(r), p_m[:, z, 0:D], 1.0, None, ALU.mult).then_inc(s("sixth"), 1)
                if r.has(2):
                    dve.wait_ge(s("dotted"), r.at(1, -1))
                V.tensor_tensor(junk[:, z, :], p_m[:, z, 0:D], ball[:, :], ALU.mult).then_inc(s("ready"), 1)
            rounds(dve, BLOCKS, body)

        def p2_pe(pe, s):
            def body(r, z):
                pe.wait_ge(s("second"), r.at(1, 1))
                if r.has(2):
                    pe.wait_ge(s("fourth"), r.at(1, -1))
                for c in range(HALF):
                    last = nc.tensor.transpose(p_ut[:, z, c * P:(c + 1) * P], u[:, z, c * P:(c + 1) * P], k.ident[:, :])
                last.then_inc(s("third"), 1)
                pe.wait_ge(s("fourth"), r.at(1, 1))
                if r.has(2):
                    pe.wait_ge(s("ready"), r.at(1, -1))
                for c in range(HALF):
                    last = nc.tensor.matmul(p_m[:, z, 0:D], ut[:, z, c * P:(c + 1) * P], wT[:, c, :],
                                            start=c == 0, stop=c == HALF - 1)
                last.then_inc(s("fifth"), 1)
            rounds(pe, BLOCKS, body)

        phase("matvec", {"vector": p2_dve, "scalar": p2_act, "tensor": p2_pe})

        def q2_dve(dve, s):
            line = Line(dve, s("line"))
            T = tabs
            dve.wait_ge(s("first"), 1)
            line(V.tensor_scalar(T["a"], T["a"], MIN_NORM, None, ALU.max))
            line(V.tensor_scalar(T["b"], T["b"], MIN_NORM, None, ALU.max))
            line(V.tensor_scalar(T["c"], T["a"], CLIP, None, ALU.min))
            line(V.tensor_scalar(T["d"], T["c"], -1.0, 1.0, ALU.mult, ALU.add))
            line(V.reciprocal(T["d"], T["d"]))
            V.scalar_tensor_tensor(out=T["d"], in0=T["c"], scalar=1.0, in1=T["d"], op0=ALU.add, op1=ALU.mult)\
                .then_inc(s("second"), 1)
            dve.wait_ge(s("third"), 1)
            line(V.reciprocal(T["a"], T["a"]))
            artanh_ratio_tail(nc, line, T["f"], T["d"], T["a"], T["c"], T["e"], T["g"])
            V.tensor_tensor(T["f"], T["f"], T["b"], ALU.mult).then_inc(s("fourth"), 1)
            dve.wait_ge(s("fifth"), 1)
            line(V.reciprocal(T["b"], T["b"]))
            line(V.tensor_tensor(T["f"], T["f"], T["b"], ALU.mult))
            line(V.tensor_tensor(T["c"], T["f"], T["m2"], ALU.mult))
            line(V.tensor_tensor(T["c"], T["f"], T["c"], ALU.mult))
            line(V.tensor_tensor(T["d"], T["f"], T["mb"], ALU.mult))
            line(V.tensor_scalar(T["d"], T["d"], 2.0, 1.0, ALU.mult, ALU.add))
            line(V.tensor_scalar(T["e"], T["c"], one["b2"], None, ALU.mult))
            line(V.tensor_tensor(T["e"], T["e"], T["d"], ALU.add))
            line(V.tensor_scalar(T["e"], T["e"], MIN_NORM, None, ALU.max))
            line(V.reciprocal(T["e"], T["e"]))
            line(V.tensor_scalar(T["d"], T["d"], one["b2"], None, ALU.add))
            line(V.tensor_tensor(T["d"], T["d"], T["f"], ALU.mult))
            line(V.tensor_tensor(T["v"], T["d"], T["e"], ALU.mult))
            line(V.tensor_scalar(T["c"], T["c"], -1.0, 1.0, ALU.mult, ALU.add))
            line(V.tensor_tensor(T["w"], T["c"], T["e"], ALU.mult))

        def q2_act(act, s):
            line = Line(act, s("act_line"))
            line(A.activation(tabs["a"], tabs["u2"], ACT.Sqrt))
            A.activation(tabs["b"], tabs["m2"], ACT.Sqrt).then_inc(s("first"), 1)
            act.wait_ge(s("second"), 1)
            A.activation(tabs["d"], tabs["d"], ACT.Ln).then_inc(s("third"), 1)
            act.wait_ge(s("fourth"), 1)
            A.activation(tabs["f"], tabs["f"], ACT.Tanh).then_inc(s("fifth"), 1)

        phase("matvec_norms", {"vector": q2_dve, "scalar": q2_act})

        def p3_dve(dve, s):
            def body(r, z):
                if r.has(2):
                    dve.wait_ge(s("second"), r.at(1, -1))
                V.tensor_scalar(part[:, z, :], ball[:, :], col("w", r), None, ALU.mult).then_inc(s("first"), 1)
                dve.wait_ge(s("first"), r.at(1, 1))
                V.scalar_tensor_tensor(out=sums_of(r), in0=sums_of(r), scalar=col("v", r), in1=part[:, z, :],
                                       op0=ALU.mult, op1=ALU.add).then_inc(s("second"), 1)
            rounds(dve, BLOCKS, body)

        def p3_act(act, s):
            def body(r, z):
                act.wait_ge(s("second"), r.at(1, 1))
                if r.has(2):
                    act.wait_ge(s("third"), r.at(1, -1))
                A.activation(junk2[:, z, :], sums_of(r), ACT.Square, accum_out=col("h2", r)).then_inc(s("third"), 1)
            rounds(act, BLOCKS, body)

        phase("ball_add", {"vector": p3_dve, "scalar": p3_act})

        def q3_dve(dve, s):
            line = Line(dve, s("line"))
            T = tabs
            dve.wait_ge(s("first"), 1)
            line(V.tensor_scalar(T["a"], T["a"], MIN_NORM, None, ALU.max))
            line(V.tensor_scalar(T["c"], T["a"], CLIP, None, ALU.min))
            line(V.tensor_scalar(T["d"], T["c"], -1.0, 1.0, ALU.mult, ALU.add))
            line(V.reciprocal(T["d"], T["d"]))
            V.scalar_tensor_tensor(out=T["d"], in0=T["c"], scalar=1.0, in1=T["d"], op0=ALU.add, op1=ALU.mult)\
                .then_inc(s("second"), 1)
            dve.wait_ge(s("third"), 1)
            line(V.reciprocal(T["a"], T["a"]))
            artanh_ratio_tail(nc, line, T["f"], T["d"], T["a"], T["c"], T["e"], T["g"])

        def q3_act(act, s):
            A.activation(tabs["a"], tabs["h2"], ACT.Sqrt).then_inc(s("first"), 1)
            act.wait_ge(s("second"), 1)
            A.activation(tabs["d"], tabs["d"], ACT.Ln).then_inc(s("third"), 1)

        phase("logmap", {"vector": q3_dve, "scalar": q3_act})

        def p4_act(act, s):
            def body(r, z):
                A.activation(sums_of(r), sums_of(r), ACT.Relu, scale=col("f", r)).then_inc(s("first"), 1)
                act.wait_ge(s("first"), r.at(1, 1))
                if r.has(2):
                    act.wait_ge(s("second"), r.at(1, -1))
                A.activation(junk2[:, z, :], sums_of(r), ACT.Square, accum_out=col("t2", r)).then_inc(s("second"), 1)
            rounds(act, BLOCKS, body)

        phase("tangent", {"scalar": p4_act})

        def q4_dve(dve, s):
            line = Line(dve, s("line"))
            T = tabs
            top = 1.0 - BALL_EPS
            dve.wait_ge(s("first"), 1)
            line(V.tensor_scalar(T["a"], T["a"], MIN_NORM, None, ALU.max))
            V.reciprocal(T["b"], T["a"]).then_inc(s("second"), 1)
            dve.wait_ge(s("third"), 1)
            dve.wait_ge(s("second"), 1)
            line(V.tensor_tensor(T["v"], T["c"], T["b"], ALU.mult))
            line(V.tensor_scalar(T["d"], T["t2"], 0.0, None, ALU.is_gt))
            line(V.tensor_tensor(T["c"], T["c"], T["d"], ALU.mult))
            line(V.tensor_scalar(T["c"], T["c"], top, None, ALU.max))
            line(V.reciprocal(T["c"], T["c"]))
            line(V.tensor_scalar(T["c"], T["c"], top, None, ALU.mult))
            line(V.tensor_tensor(T["v"], T["v"], T["c"], ALU.mult))

        def q4_act(act, s):
            A.activation(tabs["a"], tabs["t2"], ACT.Sqrt).then_inc(s("first"), 1)
            act.wait_ge(s("second"), 1)
            A.activation(tabs["c"], tabs["a"], ACT.Tanh).then_inc(s("third"), 1)

        phase("project", {"vector": q4_dve, "scalar": q4_act})

        def p5_sp(sp, s):
            def store(r, z):
                n = rows_of(r)
                sp.wait_ge(s("first"), r.at(1, 1))
                sp.dma_start(out[bass.ds(r.at(P), n), :], xr[0:n, z, :]).then_inc(s(f"out{z}"), 16)

            def body(r, z):
                n = rows_of(r)
                if r.has(2):
                    sp.wait_ge(s(f"out{z}"), r.half(16, 0))
                sp.dma_start(xr[0:n, z, :], b.xs[bass.ds(r.at(P), n), :]).then_inc(s(f"in{z}"), 16)
                if r.has(1):
                    store(r.before(), 1 - z)
            rounds(sp, BLOCKS, body)
            store(Round(None, BLOCKS - 1), 0)
            sp.wait_ge(s("out0"), 16 * 25)
            sp.wait_ge(s("out1"), 16 * 24)

        def p5_dve(dve, s):
            def body(r, z):
                dve.wait_ge(s(f"in{z}"), r.half(16, 16))
                V.scalar_tensor_tensor(out=xr[:, z, :], in0=sums_of(r), scalar=col("v", r), in1=xr[:, z, :],
                                       op0=ALU.mult, op1=ALU.add).then_inc(s("first"), 1)
            rounds(dve, BLOCKS, body)

        phase("result", {"sync": p5_sp, "vector": p5_dve})


class Keep:
    pass


def program(nc, a, out):
    b = Build(nc, a)
    k = Keep()
    with ExitStack() as ctx:
        sb, _, _ = allocators(nc, ctx)
        k.iota = sb("iota", [P, P])
        k.ident = sb("ident", [P, P])
        k.of_step = sb("of_step", [P, S])
        k.of_head = sb("of_head", [P, H])
        k.head_of = sb("head_of", [H, P])
        k.loc = sb("loc_tab", [P, SPAD])
        k.tile_of = sb("tile_of_i", [P, COLS], I32)
        k.src = sb("src_tab", [P, SPAD], I32)
        k.chain = sb("chain_tab", [H, BATCHES * CH])
        k.straddler = sb("straddler", [H, BATCHES])
        k.row = sb("row_tab", [1, SPAD], I32)
        k.packed = sb("packed_tab", [1, SPAD // PACK], I32)
        k.big1 = sb("node_sums", [P, BLOCKS * H * CE])
        k.big2 = sb("node_rows", [P, BLOCKS * (D + 1)])
        prep(nc, b, k)
        if PHASES >= 2:
            project_nodes(nc, b, k)
        if PHASES >= 3:
            attend(nc, b, k)
        if PHASES >= 4:
            finish_attention(nc, b, k)
        if PHASES >= 5:
            k.wt = sb("wt_tab", [P, SPAD])
            weights_by_step(nc, b, k)
            aggregate(nc, b, k)
        if PHASES >= 6:
            hyperbolic_layer(nc, b, k, out)


PHASES = 6


_INS = ["x", "src", "dst", "edge_attr_256", "edge_weight",
        "L0_gnn_Wq", "L0_gnn_bq", "L0_gnn_Wk", "L0_gnn_bk", "L0_gnn_Wv", "L0_gnn_bv", "L0_gnn_We",
        "L0_gnn_Ws", "L0_gnn_bs", "L1_gnn_weight", "L1_gnn_bias"]


def kernel(**inputs):
    import numpy as _np
    import concourse.bacc as _bacc
    from concourse import mybir as _mybir
    from concourse.bass_utils import run_bass_kernel_spmd as _run

    nc = _bacc.Bacc("TRN2", target_bir_lowering=False, num_devices=1)
    arrays, args = {}, {}
    for name in _INS:
        x = _np.ascontiguousarray(inputs[name])
        arrays[f"in_{name}"] = x
        args[name] = nc.dram_tensor(f"in_{name}", x.shape, _mybir.dt.from_np(x.dtype), kind="ExternalInput").ap()
    out = nc.dram_tensor("out_rows", (N, D), F32, kind="ExternalOutput").ap()
    program(nc, args, out)
    r = _run(nc, [arrays], core_ids=[0])
    return r.results[0]["out_rows"]
```

```python
import concourse.bass as bass
import concourse.mybir as mybir
import numpy as np
from contextlib import ExitStack

F32 = mybir.dt.float32
I32 = mybir.dt.int32
ALU = mybir.AluOpType
ACT = mybir.ActivationFunctionType
AX = mybir.AxisListType

P = 128
N, E, D = 6250, 106250, 256
H, C = 8, 32
CE = C + 1
BLOCKS = -(-N // P)
TAIL = N - (BLOCKS - 1) * P
TILES = -(-E // P)
LAST = E - (TILES - 1) * P
S = 16
BATCHES = -(-(TILES + BLOCKS - 1) // S)
STEPS = BATCHES * S
COLS = -(-STEPS // P)
SPAD = COLS * P
NFLAG = 4 * P + 1
CH = 2 * S + 2
BIG = 1.0e30
HALF = D // P
EA_SLOTS = 4
KV_SLOTS = 8
LN_EPS = 1e-5
MIN_NORM = 1e-15
BALL_EPS = 1e-5
CLIP = float(np.float32(1.0 - 1e-7))
CHUNK = 4
PACK = 4
GROUP = 7
assert BLOCKS % GROUP == 0


class Round:

    def __init__(self, m, a):
        self.m, self.a = m, a

    def at(self, per, k=0):
        return per * self.a + k if self.m is None else self.m * (2 * per) + (per * self.a + k)


    def half(self, per, k=0):
        return per * (self.a // 2) + k if self.m is None else self.m * per + (per * (self.a // 2) + k)

    def after(self):
        return Round(self.m, self.a + 1)

    def before(self):
        return Round(self.m, self.a - 1)

    def has(self, back):
        return self.m is not None or self.a >= back


def rounds(eng, total, body):
    body(Round(None, 0), 0)
    body(Round(None, 1), 1)
    pairs = (total - 2) // 2
    with eng.Fori(0, pairs) as m:
        body(Round(m, 2), 0)
        body(Round(m, 3), 1)
    if total % 2:
        body(Round(None, total - 1), 0)


def edge_rounds(eng, body):
    body(Round(None, 0), 0, True, False, False)
    body(Round(None, 1), 1, True, True, False)
    with eng.Fori(0, (BATCHES - 2) // 2) as m:
        body(Round(m, 2), 0, True, True, True)
        body(Round(m, 3), 1, True, True, True)
    body(Round(None, BATCHES - 1), 0, True, True, True)
    body(Round(None, BATCHES), 1, False, True, True)
    body(Round(None, BATCHES + 1), 0, False, False, True)


def bcast(ap, n):
    return ap.unsqueeze(2).to_broadcast([ap.shape[0], ap.shape[1], n])


class Line:

    def __init__(self, eng, sem, base=0):
        self.eng, self.sem, self.base, self.n = eng, sem, base, 0

    def __call__(self, ins):
        self.n += 1
        ins.then_inc(self.sem, 1)
        self.eng.wait_ge(self.sem, self.base + self.n)

    def wait(self):
        self.eng.wait_ge(self.sem, self.base + self.n)

    def on(self, ins):
        self.n += 1
        ins.then_inc(self.sem, 1)


class Build:
    def __init__(self, nc, a):
        self.nc, self.a = nc, a
        self.scratch()

    def scratch(self):
        nc = self.nc

        def dram(name, shape, dt=F32):
            return nc.dram_tensor(name, shape, dt, kind="Internal").ap()

        self.dstp = dram("dst_tiles", (TILES, P), I32)
        self.srcp = dram("src_tiles", (TILES, P), I32)
        self.wtp = dram("weight_tiles", (TILES, P))
        self.flags = dram("step_flags", (SPAD, H, NFLAG))
        self.ends = dram("step_ends", (SPAD, 5))
        self.kv = dram("kv_rows", (N, 2 * D))
        self.xs = dram("x_rows", (N, D))
        self.h2 = dram("h2_rows", (N, D))


def allocators(nc, ctx):
    def sb(name, shape, dt=F32):
        return ctx.enter_context(nc.sbuf_tensor(name, shape, dt))

    def ps(name, shape, dt=F32):
        return ctx.enter_context(nc.psum_tensor(name, shape, dt))

    def sem(name):
        return ctx.enter_context(nc.semaphore(name))

    return sb, ps, sem


def prep(nc, b, k):
    a = b.a
    with ExitStack() as ctx:
        sb, ps, sem = allocators(nc, ctx)
        tile_last = sb("tile_last", [1, TILES], I32)
        tile_block = sb("tile_block", [1, TILES], I32)
        tile_no = sb("tile_no", [1, TILES], I32)
        start_row = sb("start_row", [1, TILES], F32)
        block_row = sb("block_row", [1, TILES], F32)
        one_row = sb("one_row", [1, P], F32)
        starts = sb("starts", [P, TILES], F32)
        junk = sb("junk", [P, TILES], F32)
        step_no_i = sb("step_no_i", [P, COLS], I32)
        step_no = sb("step_no", [P, COLS], F32)
        tile_of = sb("tile_of", [P, COLS], F32)
        base_of = sb("base_of", [P, COLS], F32)
        dst_g = sb("dst_g", [P, COLS, P], I32)
        src_g = sb("src_g", [P, COLS, P], I32)
        loc = sb("loc", [P, COLS, P], F32)
        src_f = sb("src_f", [P, COLS, P], F32)
        seg = sb("seg", [P, COLS, P], F32)
        flag = sb("flag", [P, COLS, NFLAG], F32)
        dup_i = sb("dup_i", [P, 1], I32)
        dup = sb("dup", [P, 1])
        fill = sb("fill", [P, COLS])
        ends5 = sb("ends5", [P, COLS, 5], F32)
        ends8 = sb("ends8", [H, SPAD, 5], F32)
        neg = sb("neg", [1, P], I32)
        packf = sb("packf", [1, SPAD // PACK], F32)
        iota_i = sb("iota_i", [P, P], I32)
        part_i = sb("part_i", [P, 1], I32)
        part8_i = sb("part8_i", [P, 1], I32)
        partm_i = sb("partm_i", [P, 1], I32)
        part3 = sb("part3", [P, 3], F32)
        p_starts = ps("p_starts", [P, 1024], F32)
        p_tr = ps("p_tr", [P, 2, P], F32)
        tiles_in = sem("tiles_in")
        tables_out = sem("tables_out")
        iotas = sem("iotas")
        dve_line = sem("dve_line")
        row_ready = sem("row_ready")
        starts_up = sem("starts_up")
        tile_of_ready = sem("tile_of_ready")
        gathered = sem("gathered")
        loc_ready = sem("loc_ready")
        turned = sem("turned")
        turned_read = sem("turned_read")
        flags_ready = sem("flags_ready")
        flags_out = sem("flags_out")
        block = ctx.enter_context(nc.Block())

        @block.sync
        def _(sp):
            with nc.allow_non_contiguous_dma(reason="the last edge of each tile"):
                sp.dma_start(tile_last[0:1, 0:TILES - 1],
                             a["dst"][0:(TILES - 1) * P].rearrange("(o t e) -> o t e", o=1, e=P)[:, :, P - 1])\
                    .then_inc(tiles_in, 16)
            sp.dma_start(tile_last[0:1, TILES - 1:TILES],
                         a["dst"][E - 1:E].rearrange("(o e) -> o e", o=1)).then_inc(tiles_in, 16)
            sp.dma_start(dup_i[:, :], a["dst"][E - LAST - 1:E - LAST].partition_broadcast(P)).then_inc(tiles_in, 16)
            for table, name in ((b.dstp, "dst"), (b.srcp, "src")):
                sp.dma_start(table[0:TILES - 1, :],
                             a[name][0:(TILES - 1) * P].rearrange("(t e) -> t e", e=P)).then_inc(tables_out, 16)
            sp.dma_start(b.srcp[TILES - 1:TILES, :],
                         a["src"][E - P:E].rearrange("(o e) -> o e", o=1)).then_inc(tables_out, 16)
            sp.dma_start(b.dstp[TILES - 1:TILES, P - LAST:P],
                         a["dst"][E - LAST:E].rearrange("(o e) -> o e", o=1)).then_inc(tables_out, 16)
            sp.wait_ge(iotas, 1)
            sp.dma_start(b.dstp[TILES - 1:TILES, 0:P - LAST], neg[0:1, 0:P - LAST]).then_inc(tables_out, 16)
            sp.wait_ge(flags_ready, 1)
            for h in range(H):
                sp.dma_start(b.flags[:, h, :].rearrange("(c p) f -> p c f", p=P), flag[:, :, :])\
                    .then_inc(flags_out, 16)
            with nc.allow_non_contiguous_dma(reason="five words for each step"):
                sp.dma_start(b.ends.rearrange("(c p) f -> p c f", p=P), ends5[:, :, :]).then_inc(flags_out, 16)
            sp.wait_ge(flags_out, 16 * (H + 1))
            sp.dma_start(ends8[:, :, :], b.ends.partition_broadcast(H)).then_inc(flags_out, 16)

        @block.gpsimd
        def _(pool):
            nc.gpsimd.memset(neg[:, :], -1).then_inc(iotas, 1)
            nc.gpsimd.iota(tile_no[:, :], [[1, TILES]], base=0, channel_multiplier=0).then_inc(iotas, 1)
            nc.gpsimd.iota(step_no_i[:, :], [[P, COLS]], base=0, channel_multiplier=1).then_inc(iotas, 1)
            nc.gpsimd.iota(iota_i[:, :], [[1, P]], base=0, channel_multiplier=0).then_inc(iotas, 1)
            nc.gpsimd.iota(part_i[:, :], [[0, 1]], base=0, channel_multiplier=1).then_inc(iotas, 1)
            pool.wait_ge(tables_out, 16 * 5)
            pool.wait_ge(tile_of_ready, 1)
            for c in range(COLS):
                for table, to in ((b.dstp, dst_g), (b.srcp, src_g)):
                    pool.indirect_dma_start(
                        out=to[:, c, :], out_offset=None, in_=table,
                        in_offset=bass.IndirectOffsetOnAxis(ap=k.tile_of[:, c:c + 1], axis=0))\
                        .then_inc(gathered, 16)

        @block.vector
        def _(dve):
            line = Line(dve, dve_line)
            dve.wait_ge(iotas, 5)
            line(nc.vector.tensor_copy(k.iota[:, :], iota_i[:, :]))
            line(nc.vector.tensor_copy(part3[:, 0:1], part_i[:, :]))
            line(nc.vector.tensor_single_scalar(part8_i[:, :], part_i[:, :], 3, ALU.arith_shift_right))
            line(nc.vector.tensor_single_scalar(partm_i[:, :], part_i[:, :], H - 1, ALU.bitwise_and))
            line(nc.vector.tensor_copy(part3[:, 1:2], part8_i[:, :]))
            line(nc.vector.tensor_copy(part3[:, 2:3], partm_i[:, :]))
            line(nc.vector.tensor_scalar(k.ident[:, :], k.iota[:, :], part3[:, 0:1], None, ALU.is_equal))
            line(nc.vector.tensor_scalar(k.of_step[:, :], k.iota[:, 0:S], part3[:, 1:2], None, ALU.is_equal))
            line(nc.vector.tensor_scalar(k.of_head[:, :], k.iota[:, 0:H], part3[:, 2:3], None, ALU.is_equal))
            for s in range(S):
                line(nc.vector.tensor_copy(k.head_of[:, s * H:(s + 1) * H], k.ident[0:H, 0:H]))
            line(nc.vector.memset(one_row[:, :], 1.0))
            dve.wait_ge(tiles_in, 48)
            line(nc.vector.tensor_single_scalar(tile_block[:, :], tile_last[:, :], 7, ALU.arith_shift_right))
            line(nc.vector.tensor_copy(block_row[:, :], tile_block[:, :]))
            line(nc.vector.tensor_copy(start_row[:, :], tile_no[:, :]))
            line(nc.vector.tensor_tensor(start_row[0:1, 1:TILES], start_row[0:1, 1:TILES],
                                         block_row[0:1, 0:TILES - 1], ALU.add))
            nc.vector.tensor_copy(step_no[:, :], step_no_i[:, :]).then_inc(row_ready, 1)
            dve.wait_ge(row_ready, 1)
            dve.wait_ge(starts_up, 1)
            line(nc.vector.tensor_copy(starts[:, :], p_starts[:, 0:TILES]))
            for c in range(COLS):
                line(nc.vector.tensor_scalar(junk[:, :], starts[:, :], step_no[:, c:c + 1], 0.0,
                                             ALU.is_le, ALU.add, accum_out=tile_of[:, c:c + 1]))
            line(nc.vector.tensor_scalar(tile_of[:, :], tile_of[:, :], -1.0, float(TILES - 1), ALU.add, ALU.min))
            nc.vector.tensor_copy(k.tile_of[:, :], tile_of[:, :]).then_inc(tile_of_ready, 1)
            line(nc.vector.tensor_tensor(base_of[:, :], step_no[:, :], tile_of[:, :], ALU.subtract))
            line(nc.vector.tensor_scalar(ends5[:, :, 3], base_of[:, :], float(BLOCKS - 1), None, ALU.min))
            line(nc.vector.tensor_scalar(ends5[:, :, 4], tile_of[:, :], float(P), float(E - P), ALU.mult, ALU.min))
            line(nc.vector.tensor_scalar(base_of[:, :], base_of[:, :], float(P), None, ALU.mult))
            dve.wait_ge(gathered, 16 * 2 * COLS)
            line(nc.vector.tensor_copy(loc[:, :, :], dst_g[:, :, :]))
            for c in range(COLS):
                line(nc.vector.tensor_scalar(loc[:, c, :], loc[:, c, :], base_of[:, c:c + 1], None, ALU.subtract))
            nc.vector.tensor_copy(src_f[:, :, :], src_g[:, :, :]).then_inc(loc_ready, 1)
            line(nc.vector.memset(flag[:, :, :], 0.0))
            line(nc.vector.tensor_scalar(seg[:, :, :], loc[:, :, :], -0.5, P - 0.5, ALU.max, ALU.min))
            line(nc.vector.tensor_tensor(flag[:, :, 3 * P + 1:NFLAG], seg[:, :, :], loc[:, :, :], ALU.is_equal))
            line(nc.vector.tensor_copy(dup[:, :], dup_i[:, :]))
            line(nc.vector.tensor_scalar(fill[:, :], tile_of[:, :], float(TILES - 1), dup[:, :], ALU.is_equal, ALU.mult))
            for c in range(COLS):
                line(nc.vector.tensor_copy(seg[:, c, :], dst_g[:, c, :]))
                line(nc.vector.tensor_scalar(seg[:, c, :], seg[:, c, :], fill[:, c:c + 1], base_of[:, c:c + 1],
                                             ALU.max, ALU.subtract))
            line(nc.vector.tensor_scalar(seg[:, :, :], seg[:, :, :], -0.5, P - 0.5, ALU.max, ALU.min))
            line(nc.vector.tensor_copy(ends5[:, :, 2], seg[:, :, 0]))
            for c in range(COLS):
                line(nc.vector.tensor_scalar(seg[:, c, :], seg[:, c, :], base_of[:, c:c + 1], None, ALU.add))
            line(nc.vector.tensor_copy(ends5[:, :, 0], seg[:, :, 0]))
            line(nc.vector.tensor_copy(ends5[:, :, 1], seg[:, :, P - 1]))
            line(nc.vector.tensor_tensor(flag[:, :, 1:P], seg[:, :, 1:P], seg[:, :, 0:P - 1], ALU.is_equal))
            for c in range(COLS):
                line(nc.vector.tensor_scalar(flag[:, c, P + 1:2 * P + 1], seg[:, c, :], seg[:, c, 0:1], None,
                                             ALU.is_equal))
                line(nc.vector.tensor_scalar(flag[:, c, 2 * P + 1:3 * P + 1], seg[:, c, :], seg[:, c, P - 1:P],
                                             None, ALU.is_equal))
            nc.vector.tensor_scalar(flag[:, :, :], flag[:, :, :], BIG, -BIG, ALU.mult, ALU.add)\
                .then_inc(flags_ready, 1)
            for c in range(COLS):
                dve.wait_ge(turned, c + 1)
                line(nc.vector.tensor_copy(k.loc[:, c * P:(c + 1) * P], p_tr[:, 0, :]))
                nc.vector.tensor_copy(k.src[:, c * P:(c + 1) * P], p_tr[:, 1, :]).then_inc(turned_read, 1)
            dve.wait_ge(flags_out, 16 * (H + 2))
            chain = k.chain[:, :].rearrange("p (i c) -> p i c", c=CH)
            line(nc.vector.memset(k.chain[:, :], 0.0))
            e5 = ends8[:, 0:STEPS, :]
            line(nc.vector.tensor_tensor(
                chain[:, :, 2:CH - 1:2], e5[:, :, 0].rearrange("p (i s) -> p i s", s=S),
                e5[:, :, 1].rearrange("p (i s) -> p i s", s=S), ALU.is_equal))
            line(nc.vector.tensor_tensor(
                chain[:, :, 3:CH - 1:2], ends8[:, 1:STEPS + 1, 0].rearrange("p (i s) -> p i s", s=S)[:, :, 0:S - 1],
                e5[:, :, 1].rearrange("p (i s) -> p i s", s=S)[:, :, 0:S - 1], ALU.is_equal))
            line(nc.vector.tensor_tensor(
                chain[:, 1:BATCHES, 1], ends8[:, S:STEPS, 0].rearrange("p (i s) -> p i s", s=S)[:, :, 0],
                ends8[:, S - 1:STEPS - 1, 1].rearrange("p (i s) -> p i s", s=S)[:, :, 0], ALU.is_equal))
            line(nc.vector.tensor_scalar(k.chain[:, :], k.chain[:, :], BIG, -BIG, ALU.mult, ALU.add))
            line(nc.vector.tensor_copy(k.straddler[:, :], e5[:, :, 2].rearrange("p (i s) -> p i s", s=S)[:, :, 0]))
            line(nc.vector.tensor_copy(k.row[:, :], ends8[0:1, :, 4]))
            blocks = ends8[0:1, :, 3].rearrange("p (w j) -> p w j", j=PACK)
            line(nc.vector.tensor_copy(packf[:, :], blocks[:, :, PACK - 1]))
            for j in reversed(range(PACK - 1)):
                line(nc.vector.scalar_tensor_tensor(out=packf[:, :], in0=packf[:, :], scalar=64.0,
                                                    in1=blocks[:, :, j], op0=ALU.mult, op1=ALU.add))
            line(nc.vector.tensor_copy(k.packed[:, :], packf[:, :]))

        @block.tensor
        def _(pe):
            pe.wait_ge(row_ready, 1)
            for at in range(0, TILES, 512):
                n = min(512, TILES - at)
                last = nc.tensor.matmul(p_starts[:, at:at + n], one_row[:, :], start_row[0:1, at:at + n],
                                        start=True, stop=True)
            last.then_inc(starts_up, 1)
            pe.wait_ge(loc_ready, 1)
            for c in range(COLS):
                if c:
                    pe.wait_ge(turned_read, c)
                nc.tensor.transpose(p_tr[:, 0, :], loc[:, c, :], k.ident[:, :])
                nc.tensor.transpose(p_tr[:, 1, :], src_f[:, c, :], k.ident[:, :]).then_inc(turned, 1)


def rows_of(r):
    return TAIL if r.m is None and r.a == BLOCKS - 1 else P


def project_nodes(nc, b, k):
    a = b.a
    with ExitStack() as ctx:
        sb, ps, sem = allocators(nc, ctx)
        w = sb("w_qkvs", [P, HALF, 4 * D])
        bias = sb("bias_qkvs", [P, 4, D])
        x = sb("x_blk", [P, 2, D])
        carrier = sb("wait_carrier", [1, 2])
        six = sb("six", [P, 2, 6])
        mv = sb("mv", [P, 2, 2])
        sd = sb("sd", [P, 2, 1])
        rs = sb("rs", [P, 2, 1])
        nm = sb("nm", [P, 2, 1])
        xb = sb("x_bs", [P, 2, D])
        h = sb("h_blk", [P, 2, D])
        ht = sb("ht_blk", [P, 2, D])
        kvs = sb("kv_stage", [P, 2, 2 * D])
        xo = sb("xo_stage", [P, 2, D])
        p_ht = ps("p_ht", [P, 2, D])
        p_qk = ps("p_qk", [P, 2, 2 * D])
        p_vs = ps("p_vs", [P, 2, 2 * D])
        w_in = sem("w_in")
        x_in = [sem(f"x_in{z}") for z in range(2)]
        out_done = [sem(f"kv_out{z}") for z in range(2)]
        line_sem = sem("proj_dve_line")
        var_ready, sd_ready, norm_ready = sem("var_ready"), sem("sd_ready"), sem("norm_ready")
        h_ready, turned, ht_ready = sem("h_ready"), sem("h_turned"), sem("ht_ready")
        projected, staged, xb_ready = sem("projected"), sem("staged"), sem("xb_ready")
        block = ctx.enter_context(nc.Block())
        scale = 1.0 / float(np.sqrt(np.float32(C)))

        @block.sync
        def _(sp):
            for i, name in enumerate(("Wq", "Wk", "Wv", "Ws")):
                sp.dma_start(w[:, :, i * D:(i + 1) * D],
                             a[f"L0_gnn_{name}"].rearrange("(c p) n -> p c n", p=P)).then_inc(w_in, 16)
            for i, name in enumerate(("bq", "bk", "bv", "bs")):
                sp.dma_start(bias[:, i, :], a[f"L0_gnn_{name}"].partition_broadcast(P)).then_inc(w_in, 16)

            def store(r, z):
                n = rows_of(r)
                sp.wait_ge(staged, r.at(1, 1))
                sp.dma_start(b.kv[bass.ds(r.at(P), n), :], kvs[0:n, z, :]).then_inc(out_done[z], 16)
                sp.dma_start(b.xs[bass.ds(r.at(P), n), :], xo[0:n, z, :]).then_inc(out_done[z], 16)

            def body(r, z):
                n = rows_of(r)
                if r.has(2):
                    sp.wait_ge(h_ready, r.at(1, -1))
                    sp.wait_ge(xb_ready, r.at(1, -1))
                sp.dma_start(x[0:n, z, :], a["x"][bass.ds(r.at(P), n), :]).then_inc(x_in[z], 16)
                if r.has(2):
                    store(r.before().before(), z)

            rounds(sp, BLOCKS, body)
            store(Round(None, BLOCKS - 2), 1)
            store(Round(None, BLOCKS - 1), 0)
            sp.wait_ge(out_done[0], 32 * 25)
            sp.wait_ge(out_done[1], 32 * 24)

        @block.gpsimd
        def _(pool):
            pool.wait_ge(w_in, 16 * 8)

            def body(r, z):
                pool.wait_ge(x_in[z], r.half(16, 16))
                if r.has(2):
                    pool.wait_ge(staged, r.at(1, -1))
                nc.gpsimd.tensor_tensor(xb[:, z, :], x[:, z, :], bias[:, 3, :], ALU.add).then_inc(xb_ready, 1)

            rounds(pool, BLOCKS, body)

        @block.vector
        def _(dve):
            dve.wait_ge(w_in, 16 * 8)
            nc.vector.tensor_scalar(bias[:, 0, :], bias[:, 0, :], scale, None, ALU.mult).then_inc(line_sem, 1)
            dve.wait_ge(line_sem, 1)

            def evacuate(r, z):
                dve.wait_ge(projected, r.at(1, 1))
                q = k.big2[:, bass.ds(r.at(D + 1), D)]
                nc.vector.scalar_tensor_tensor(out=q, in0=p_qk[:, z, 0:D], scalar=scale, in1=bias[:, 0, :],
                                               op0=ALU.mult, op1=ALU.add)
                if r.has(2):
                    dve.wait_ge(out_done[z], r.half(32, 0))
                nc.vector.tensor_tensor(kvs[:, z, 0:D], p_qk[:, z, D:2 * D], bias[:, 1, :], ALU.add)
                nc.vector.tensor_tensor(kvs[:, z, D:2 * D], p_vs[:, z, 0:D], bias[:, 2, :], ALU.add)
                dve.wait_ge(xb_ready, r.at(1, 1))
                nc.vector.tensor_tensor(xo[:, z, :], p_vs[:, z, D:2 * D], xb[:, z, :], ALU.add).then_inc(staged, 1)

            def stats(r, z):
                line = Line(dve, line_sem, r.at(3, 1))
                dve.wait_ge(x_in[z], r.half(16, 16))
                line(nc.vector.bn_stats(six[:, z, :], x[:, z, :]))
                nc.vector.memset(carrier[:, z:z + 1], 0.0)
                line(nc.vector.bn_aggr(mv[:, z, :], six[:, z, :]))
                nc.vector.tensor_scalar(mv[:, z, 1:2], mv[:, z, 1:2], LN_EPS, None, ALU.add).then_inc(var_ready, 1)

            def norm(r, z):
                line = Line(dve, line_sem, r.at(3, 3))
                dve.wait_ge(sd_ready, r.at(1, 1))
                line(nc.vector.reciprocal(rs[:, z, :], sd[:, z, :]))
                nc.vector.scalar_tensor_tensor(out=nm[:, z, :], in0=mv[:, z, 0:1], scalar=-1.0, in1=rs[:, z, :],
                                               op0=ALU.mult, op1=ALU.mult).then_inc(norm_ready, 1)

            def body(r, z):
                norm(r, z)
                if r.has(1):
                    evacuate(r.before(), 1 - z)
                if r.m is not None or r.a + 1 < BLOCKS:
                    stats(r.after(), 1 - z)

            stats(Round(None, 0), 0)
            rounds(dve, BLOCKS, body)
            evacuate(Round(None, BLOCKS - 1), 0)

        @block.scalar
        def _(act):
            def deviation(r, z):
                act.wait_ge(var_ready, r.at(1, 1))
                nc.scalar.activation(sd[:, z, :], mv[:, z, 1:2], ACT.Sqrt).then_inc(sd_ready, 1)

            def body(r, z):
                act.wait_ge(norm_ready, r.at(1, 1))
                if r.has(2):
                    act.wait_ge(turned, r.at(1, -1))
                nc.scalar.activation(h[:, z, :], x[:, z, :], ACT.Relu, bias=nm[:, z, :], scale=rs[:, z, :])\
                    .then_inc(h_ready, 1)
                act.wait_ge(turned, r.at(1, 1))
                if r.has(2):
                    act.wait_ge(projected, r.at(1, -1))
                nc.scalar.copy(ht[:, z, :], p_ht[:, z, :]).then_inc(ht_ready, 1)
                if r.m is not None or r.a + 1 < BLOCKS:
                    deviation(r.after(), 1 - z)

            deviation(Round(None, 0), 0)
            rounds(act, BLOCKS, body)

        @block.tensor
        def _(pe):
            pe.wait_ge(w_in, 16 * 8)

            def body(r, z):
                pe.wait_ge(h_ready, r.at(1, 1))
                if r.has(2):
                    pe.wait_ge(ht_ready, r.at(1, -1))
                for c in range(HALF):
                    last = nc.tensor.transpose(p_ht[:, z, c * P:(c + 1) * P], h[:, z, c * P:(c + 1) * P],
                                               k.ident[:, :])
                last.then_inc(turned, 1)
                if r.has(2):
                    pe.wait_ge(staged, r.at(1, -1))
                pe.wait_ge(ht_ready, r.at(1, 1))
                for to, at in ((p_qk, 0), (p_vs, 2 * D)):
                    for c in range(HALF):
                        last = nc.tensor.matmul(to[:, z, :], ht[:, z, c * P:(c + 1) * P], w[:, c, at:at + 2 * D],
                                                start=c == 0, stop=c == HALF - 1)
                last.then_inc(projected, 1)

            rounds(pe, BLOCKS, body)


MSG_FROM = S // 2
LAG = 2
MSG_AT = {j: [2 * (j - MSG_FROM), 2 * (j - MSG_FROM) + 1] for j in range(MSG_FROM, S)}
SUM_AT = {j + LAG: m for j, m in MSG_AT.items() if j + LAG < S}
LATE_AT = {j + LAG - S: m for j, m in MSG_AT.items() if j + LAG >= S}


def block_no(eng, k, r, j, word, known=False):
    if j % PACK == 0 and not known:
        word[0] = eng.value_load(k.packed[0:1, bass.ds(r.at(S // PACK, j // PACK), 1)], min_val=0,
                                 max_val=(1 << (6 * PACK)) - 1)
    return eng.bass.s_assert_within(
        eng.snap((word[0] >> (6 * (j % PACK))) & 63), 0, BLOCKS - 1,
        skip_runtime_bounds_check_because="the table's blocks are clamped to the last one")


def attend(nc, b, k):
    a = b.a
    with ExitStack() as ctx:
        sb, ps, sem = allocators(nc, ctx)
        we = sb("we", [P, HALF, D])
        ea = sb("ea", [P, EA_SLOTS, D])
        kv = sb("kv", [P, KV_SLOTS, 2 * D])
        idx = sb("idx", [P, 2, S], I32)
        carrier = sb("wait_carrier3", [1, S])
        loc = sb("loc_b", [P, 2, S])
        oh = sb("oh", [P, 2, S, P])
        xt = sb("xt", [P, 2, D + P])
        kj = sb("kj", [P, 4, D])
        score = sb("score", [P, S * H])
        ve = sb("ve", [P, 2, S, H * CE])
        msg = sb("msg", [P, 4, H * CE])
        fl = sb("fl", [P, NFLAG])
        run = sb("run", [P, P])
        top = sb("top", [P, P])
        sc = sb("sc", [P, P])
        u = sb("u", [P, 2 * S])
        cin = sb("cin", [H, CH - 1])
        cfl = sb("chain_flags", [H, 2, CH])
        cf = sb("cf", [H, CH - 1])
        cb = sb("cb", [H, CH - 1])
        carry = sb("carry", [H, 1])
        fd = sb("fd", [H, 1])
        fe = sb("fe", [H, 1])
        sel8 = sb("sel8", [H, H])
        oh8 = top[0:H, :]
        mf = sb("mf", [P, 2])
        p_x = ps("p_x", [P, 2, 512])
        p_y = ps("p_y", [P, 2, 2 * D])
        p_ch = ps("p_ch", [P, 512])
        p_p = ps("p_p", [P, 512])
        p_sum = ps("p_sum", [P, 2, 512])
        p_st, p_top, p_f, p_u = p_ch[:, 0:P], p_ch[:, 128:128 + CH - 1], p_ch[:, 192:192 + H], p_ch[0:H, 256:256 + 2 * S]
        we_in, setup = sem("we_in"), sem("att_setup")
        ea_in = [sem(f"ea_in{i}") for i in range(EA_SLOTS)]
        kv_in = [sem(f"kv_in{i}") for i in range(KV_SLOTS)]
        fl_in = sem("fl_in")
        idx_ready, oh_ready = sem("idx_ready"), sem("oh_ready")
        turned, xt_ready, y_done = sem("turned"), sem("xt_ready"), sem("y_done")
        kj_done, ve_done, prod_done, score_done = sem("kj_done"), sem("ve_done"), sem("prod_done"), sem("score_done")
        st_done, u_ready, u_done, c_ready, fd_ready, fe_ready, sel_ready, top_done, f_done = (
            sem(n) for n in ("st_done", "u_ready", "u_done", "c_ready", "fd_ready", "fe_ready", "sel_ready", "top_done",
                             "f_done"))
        dd_ready, pt_ready, p_ready = sem("dd_ready"), sem("pt_ready"), sem("p_ready")
        msg_done, sum_done, add_done, chain_line = sem("msg_done"), sem("sum_done"), sem("add_done"), sem("chain_line")
        block = ctx.enter_context(nc.Block())
        NLINE = 15

        @block.sync
        def _(sp):
            sp.dma_start(we[:, :, :], a["L0_gnn_We"].rearrange("(c p) n -> p c n", p=P)).then_inc(we_in, 16)
            flag_rows = b.flags.rearrange("s h f -> (s h) f")

            def body(r, z, here, prev, late):
                if not here:
                    return
                for j in range(S):
                    row = sp.value_load(k.row[0:1, bass.ds(r.at(S, j), 1)], min_val=0, max_val=E - P)
                    if r.has(1) or j >= EA_SLOTS:
                        sp.wait_ge(turned, r.at(S, j + 1 - EA_SLOTS))
                    slot = j % EA_SLOTS
                    sp.dma_start(ea[:, slot, :], a["edge_attr_256"][bass.ds(row, P), :]).then_inc(ea_in[slot], 16)
                if r.has(1):
                    sp.wait_ge(dd_ready, r.at(1, 0))
                sp.dma_start(fl[:, :], flag_rows[bass.ds(r.at(S * H), S * H), :]).then_inc(fl_in, 16)

            edge_rounds(sp, body)

        @block.gpsimd
        def _(pool):
            def body(r, z, here, prev, late):
                if not here:
                    return
                nc.gpsimd.tensor_copy(idx[:, z, :], k.src[:, bass.ds(r.at(S), S)]).then_inc(idx_ready, 1)
                nc.gpsimd.tensor_copy(loc[:, z, :], k.loc[:, bass.ds(r.at(S), S)]).then_inc(idx_ready, 1)
                nc.gpsimd.tensor_copy(cfl[:, z, :], k.chain[:, bass.ds(r.at(CH), CH)]).then_inc(idx_ready, 1)
                pool.wait_ge(idx_ready, r.at(3, 3))
                for j in range(S):
                    slot = j % KV_SLOTS
                    if r.has(1) or j >= KV_SLOTS:
                        pool.wait_ge(ve_done, r.at(S, j + 1 - KV_SLOTS))
                    if r.has(2):
                        pool.wait_ge(sum_done, r.at(S, j + 1 - 2 * S))
                    nc.gpsimd.tensor_tensor(carrier[:, j:j + 1], k.iota[0:1, 0:1], k.iota[0:1, 0:1], ALU.add)
                    nc.gpsimd.tensor_scalar(oh[:, z, j, :], k.iota[:, :], loc[:, z, j:j + 1], None, ALU.is_equal)\
                        .then_inc(oh_ready, 1)
                    pool.indirect_dma_start(
                        out=kv[:, slot, :], out_offset=None, in_=b.kv,
                        in_offset=bass.IndirectOffsetOnAxis(ap=idx[:, z, j:j + 1], axis=0)).then_inc(kv_in[slot], 16)

            edge_rounds(pool, body)

        @block.tensor
        def _(pe):
            pe.wait_ge(we_in, 16)
            word = [None]

            def turn(r, z, j):
                g = j % 2
                pe.wait_ge(ea_in[j % EA_SLOTS], r.at(16 * (S // EA_SLOTS), 16 * (j // EA_SLOTS + 1)))
                for c in range(HALF):
                    nc.tensor.transpose(p_x[:, g, c * P:(c + 1) * P], ea[:, j % EA_SLOTS, c * P:(c + 1) * P],
                                        k.ident[:, :])
                pe.wait_ge(oh_ready, r.at(S, j + 1))
                nc.tensor.transpose(p_x[:, g, D:D + P], oh[:, z, j, :], k.ident[:, :]).then_inc(turned, 1)

            def product(r, z, j):
                g = j % 2
                block_of = block_no(pe, k, r, j, word)
                if r.has(1) or j >= 2:
                    pe.wait_ge(prod_done, r.at(S, j - 1))
                pe.wait_ge(xt_ready, r.at(S, j + 1))
                for c in range(HALF):
                    nc.tensor.matmul(p_y[:, g, 0:D], xt[:, g, c * P:(c + 1) * P], we[:, c, :],
                                     start=c == 0, stop=c == HALF - 1)
                nc.tensor.matmul(p_y[:, g, D:2 * D], xt[:, g, D:D + P], k.big2[:, bass.ds(block_of * (D + 1), D)],
                                 start=True, stop=True).then_inc(y_done, 1)

            def sums(p, y, i):
                if i % 2 == 0:
                    if p.has(1) or i >= 2:
                        pe.wait_ge(add_done, p.at(S, i))
                    pe.wait_ge(msg_done, p.at(S, i + 2))
                nc.tensor.matmul(p_sum[:, i % 2, 0:H * CE], oh[:, y, i, :], msg[:, i % 4, :],
                                 start=True, stop=True).then_inc(sum_done, 1)

            def chain(p, y, j):
                if j == 1:
                    pe.wait_ge(score_done, p.at(S, S))
                    nc.tensor.transpose(p_st, score[:, :], k.ident[:, :]).then_inc(st_done, 1)
                if j == 3:
                    pe.wait_ge(u_ready, p.at(1, 1))
                    nc.tensor.matmul(p_u, k.of_head[:, :], u[:, :], start=True, stop=True).then_inc(u_done, 1)
                if j == 5:
                    pe.wait_ge(c_ready, p.at(1, 1))
                    nc.tensor.matmul(p_top, k.head_of[:, :], cb[:, :], start=True, stop=True).then_inc(top_done, 1)
                if j == 7:
                    pe.wait_ge(pt_ready, p.at(1, 1))
                    nc.tensor.transpose(p_p[:, 0:P], run[:, :], k.ident[:, :]).then_inc(p_ready, 1)
                if j == 8:
                    pe.wait_ge(sel_ready, p.at(1, 1))
                    nc.tensor.matmul(p_f, oh8, sel8[:, :], start=True, stop=True).then_inc(f_done, 1)

            def body(r, z, here, prev, late):
                p, y = r.before(), 1 - z
                for j in range(S):
                    if here and j == 0:
                        turn(r, z, 0)
                    if here and j + 1 < S:
                        turn(r, z, j + 1)
                    if here:
                        product(r, z, j)
                    if late:
                        for i in LATE_AT.get(j, ()):
                            sums(p.before(), z, i)
                    if prev:
                        chain(p, y, j)
                        for i in SUM_AT.get(j, ()):
                            sums(p, y, i)

            edge_rounds(pe, body)

        @block.scalar
        def _(act):
            def body(r, z, here, prev, late):
                p = r.before()
                for j in range(S):
                    g = j % 2
                    for i in ([0, 1] if j == 0 else [j + 1] if j + 1 < S else []):
                        if not here:
                            break
                        g = i % 2
                        act.wait_ge(kv_in[i % KV_SLOTS], r.at(16 * (S // KV_SLOTS), 16 * (i // KV_SLOTS + 1)))
                        act.wait_ge(turned, r.at(S, i + 1))
                        if r.has(1) or i >= 2:
                            act.wait_ge(y_done, r.at(S, i - 1))
                        nc.scalar.copy(xt[:, g, :], p_x[:, g, 0:D + P]).then_inc(xt_ready, 1)
                    if prev and j == 5:
                        act.wait_ge(fd_ready, p.at(1, 1))
                        nc.scalar.activation(fe[:, :], fd[:, :], ACT.Exp).then_inc(fe_ready, 1)
                    if prev and j == 7:
                        act.wait_ge(dd_ready, p.at(1, 1))
                        nc.scalar.activation(run[:, :], run[:, :], ACT.Exp).then_inc(pt_ready, 1)

            edge_rounds(act, body)

        @block.vector
        def _(dve):
            nc.vector.memset(k.big1[:, :], 0.0).then_inc(setup, 1)
            nc.vector.memset(ve[:, :, :, :], 1.0).then_inc(setup, 1)
            nc.vector.memset(carry[:, :], -BIG).then_inc(setup, 1)
            dve.wait_ge(setup, 3)
            word = [None]

            def keys(r, z, j):
                g, slot = j % 2, j % KV_SLOTS
                dve.wait_ge(y_done, r.at(S, j + 1))
                nc.vector.tensor_tensor(kj[:, j % 4, :], p_y[:, g, 0:D], kv[:, slot, 0:D], ALU.add).then_inc(kj_done, 1)

            def values(r, z, j):
                g, slot = j % 2, j % KV_SLOTS
                nc.vector.tensor_tensor(
                    ve[:, z, j, :].rearrange("p (h c) -> p h c", c=CE)[:, :, 0:C],
                    p_y[:, g, 0:D].rearrange("p (h c) -> p h c", c=C),
                    kv[:, slot, D:2 * D].rearrange("p (h c) -> p h c", c=C), ALU.add).then_inc(ve_done, 1)

            def multiply(r, z, j):
                dve.wait_ge(kj_done, r.at(S, j + 1))
                nc.vector.tensor_tensor(kj[:, j % 4, :], p_y[:, j % 2, D:2 * D], kj[:, j % 4, :], ALU.mult)\
                    .then_inc(prod_done, 1)

            def reduce(r, z, j, waits=False):
                if j == 0 and r.has(1):
                    dve.wait_ge(st_done, r.at(1, 0))
                if waits:
                    dve.wait_ge(prod_done, r.at(S, j + 1))
                nc.vector.tensor_reduce(score[:, j * H:(j + 1) * H],
                                        kj[:, j % 4, :].rearrange("p (h c) -> p h c", c=C), AX.X, ALU.add)\
                    .then_inc(score_done, 1)

            def add(p, i):
                block_of = block_no(dve, k, p, i, word, known=i == 0)
                to = k.big1[:, bass.ds(block_of * (H * CE), H * CE)]
                dve.wait_ge(sum_done, p.at(S, i + 1))
                if i:
                    dve.wait_ge(add_done, p.at(S, i))
                nc.vector.tensor_tensor(to, p_sum[:, i % 2, 0:H * CE], to, ALU.add).then_inc(add_done, 1)

            def message(p, y, i):
                if i == 0:
                    dve.wait_ge(p_ready, p.at(1, 1))
                nc.vector.tensor_tensor(msg[:, i % 4, :].rearrange("p (h c) -> p h c", c=CE),
                                        ve[:, y, i, :].rearrange("p (h c) -> p h c", c=CE),
                                        bcast(p_p[:, i * H:(i + 1) * H], CE), ALU.mult).then_inc(msg_done, 1)

            def chain(p, y, j, line):
                if j == 1:
                    dve.wait_ge(st_done, p.at(1, 1))
                    dve.wait_ge(fl_in, p.at(16, 16))
                    if p.has(1):
                        dve.wait_ge(p_ready, p.at(1, 0))
                    line(nc.vector.tensor_tensor(sc[:, :], p_st, fl[:, 3 * P + 1:NFLAG], ALU.add))
                    line(nc.vector.tensor_tensor_scan(run[:, :], fl[:, 0:P], sc[:, :], -BIG, ALU.add, ALU.max))
                    line(nc.vector.tensor_tensor_scan(top[:, ::-1], fl[:, 1:P + 1][:, ::-1], run[:, ::-1], -BIG,
                                                      ALU.add, ALU.max))
                    line.on(nc.vector.tensor_scalar(u[:, 0:2 * S:2], k.of_step[:, :], top[:, 0:1], None, ALU.mult))
                    nc.vector.tensor_scalar(u[:, 1:2 * S:2], k.of_step[:, :], top[:, P - 1:P], None, ALU.mult)\
                        .then_inc(u_ready, 1)
                if j == 3:
                    dve.wait_ge(u_done, p.at(1, 1))
                    line.on(nc.vector.tensor_copy(cin[:, 0:1], carry[:, :]))
                    line(nc.vector.tensor_copy(cin[:, 1:CH - 1], p_u))
                    flags = cfl[:, y, :]
                    line(nc.vector.tensor_tensor_scan(cf[:, :], flags[:, 0:CH - 1], cin[:, :], -BIG, ALU.add, ALU.max))
                    nc.vector.tensor_tensor_scan(cb[:, ::-1], flags[:, 1:CH][:, ::-1], cf[:, ::-1], -BIG,
                                                 ALU.add, ALU.max).then_inc(c_ready, 1)
                    dve.wait_ge(c_ready, p.at(1, 1))
                    line.on(nc.vector.tensor_copy(carry[:, :], cb[:, CH - 2:CH - 1]))
                    nc.vector.tensor_tensor(fd[:, :], cin[:, 0:1], cb[:, 0:1], ALU.subtract).then_inc(fd_ready, 1)
                if j == 6:
                    dve.wait_ge(fe_ready, p.at(1, 1))
                    dve.wait_ge(dd_ready, p.at(1, 1))
                    line.on(nc.vector.tensor_scalar(oh8, k.iota[0:H, :], k.straddler[:, bass.ds(p.at(1), 1)], None,
                                                 ALU.is_equal))
                    line(nc.vector.tensor_scalar(fe[:, :], fe[:, :], -1.0, None, ALU.add))
                    nc.vector.tensor_scalar(sel8[:, :], k.ident[0:H, 0:H], fe[:, :], None, ALU.mult).then_inc(sel_ready, 1)
                if j == 5:
                    dve.wait_ge(top_done, p.at(1, 1))
                    for c, step in enumerate((line.on, line)):
                        step(nc.vector.tensor_tensor_reduce(
                            out=u[:, c * S:(c + 1) * S], in0=p_top[:, 1 + c:CH - 1:2], in1=k.of_step[:, :],
                            scale=1.0, scalar=0.0, op0=ALU.mult, op1=ALU.add, accum_out=mf[:, c:c + 1]))
                    for c in range(2):
                        line(nc.vector.scalar_tensor_tensor(
                            out=top[:, :], in0=fl[:, (c + 1) * P + 1:(c + 2) * P + 1], scalar=mf[:, c:c + 1],
                            in1=top[:, :], op0=ALU.add, op1=ALU.max))
                    nc.vector.tensor_tensor(run[:, :], sc[:, :], top[:, :], ALU.subtract).then_inc(dd_ready, 1)
                if j == 9:
                    dve.wait_ge(f_done, p.at(1, 1))
                    to = k.big1[:, bass.ds(block_no(dve, k, p, 0, word) * (H * CE), H * CE)]\
                        .rearrange("p (h c) -> p h c", c=CE)
                    if p.has(1):
                        dve.wait_ge(add_done, p.at(S, 0))
                    line(nc.vector.scalar_tensor_tensor(out=to, in0=bcast(p_f, CE), scalar=1.0, in1=to, op0=ALU.add,
                                                        op1=ALU.mult))

            def body(r, z, here, prev, late):
                p, y = r.before(), 1 - z
                line = Line(dve, chain_line, p.at(NLINE) if prev else 0)
                for j in range(S):
                    adds = [(p.before(), i) for i in LATE_AT.get(j, ()) if late] + \
                        [(p, i) for i in SUM_AT.get(j, ()) if prev]
                    for q, i in adds[:1]:
                        add(q, i)
                    if here:
                        keys(r, z, j)
                    for q, i in adds[1:]:
                        add(q, i)
                    if here:
                        values(r, z, j)
                        multiply(r, z, j)
                    if here and j:
                        reduce(r, z, j - 1)
                    if prev:
                        chain(p, y, j, line)
                        for i in MSG_AT.get(j, ()):
                            message(p, y, i)
                if here:
                    reduce(r, z, S - 1, waits=True)
                assert not prev or line.n == NLINE, line.n

            edge_rounds(dve, body)


def finish_attention(nc, b, k):
    with ExitStack() as ctx:
        sb, ps, sem = allocators(nc, ctx)
        xr = sb("x_skip_blk", [P, 2, D])
        x = sb("x1_blk", [P, 2, D])
        carrier = sb("wait_carrier2", [1, 2])
        den = sb("den", [P, 2, H])
        out = sb("att_out", [P, 2, D])
        six = sb("six2", [P, 2, 6])
        mv = sb("mv2", [P, 2, 2])
        sd = sb("sd2", [P, 2, 1])
        rs = sb("rs2", [P, 2, 1])
        nm = sb("nm2", [P, 2, 1])
        junk = sb("sq_junk", [P, 2, D])
        x_in = [sem(f"xr_in{z}") for z in range(2)]
        out_done = [sem(f"x1_out{z}") for z in range(2)]
        x1_ready, var_ready, sd_ready, norm_ready = sem("x1_ready"), sem("var2_ready"), sem("sd2_ready"), sem("norm2_ready")
        h_ready, sq_ready, line_sem = sem("h2_ready"), sem("sq_ready"), sem("fin_dve_line")
        norm_line, h2_out = sem("fin_norm_line"), sem("h2_out")
        block = ctx.enter_context(nc.Block())

        @block.sync
        def _(sp):
            def store(r, z):
                n = rows_of(r)
                sp.wait_ge(x1_ready, r.at(1, 1))
                sp.dma_start(b.xs[bass.ds(r.at(P), n), :], x[0:n, z, :]).then_inc(out_done[z], 16)

            def store_h2(r):
                n = rows_of(r)
                sp.wait_ge(h_ready, r.at(1, 1))
                sp.dma_start(b.h2[bass.ds(r.at(P), n), :], k.big2[0:n, bass.ds(r.at(D + 1), D)])\
                    .then_inc(h2_out, 16)

            def body(r, z):
                n = rows_of(r)
                if r.has(2):
                    sp.wait_ge(x1_ready, r.at(1, -1))
                sp.dma_start(xr[0:n, z, :], b.xs[bass.ds(r.at(P), n), :]).then_inc(x_in[z], 16)
                if r.has(1):
                    store(r.before(), 1 - z)
                if r.has(2):
                    store_h2(r.before().before())

            rounds(sp, BLOCKS, body)
            store(Round(None, BLOCKS - 1), 0)
            store_h2(Round(None, BLOCKS - 2))
            store_h2(Round(None, BLOCKS - 1))
            sp.wait_ge(out_done[0], 16 * 25)
            sp.wait_ge(out_done[1], 16 * 24)
            sp.wait_ge(h2_out, 16 * BLOCKS)

        @block.vector
        def _(dve):
            per = 5

            def front(r, z):
                line = Line(dve, line_sem, r.at(per))
                sums = k.big1[:, bass.ds(r.at(H * CE), H * CE)].rearrange("p (h c) -> p h c", c=CE)
                line(nc.vector.tensor_scalar(den[:, z, :], sums[:, :, C], 1e-16, None, ALU.add))
                line(nc.vector.reciprocal(den[:, z, :], den[:, z, :]))
                line(nc.vector.tensor_tensor(out[:, z, :].rearrange("p (h c) -> p h c", c=C), sums[:, :, 0:C],
                                             bcast(den[:, z, :], C), ALU.mult))
                dve.wait_ge(x_in[z], r.half(16, 16))
                if r.has(2):
                    dve.wait_ge(out_done[z], r.half(16, 0))
                    dve.wait_ge(h_ready, r.at(1, -1))
                nc.vector.tensor_tensor(x[:, z, :], out[:, z, :], xr[:, z, :], ALU.add).then_inc(x1_ready, 1)
                dve.wait_ge(x1_ready, r.at(1, 1))
                line(nc.vector.bn_stats(six[:, z, :], x[:, z, :]))
                nc.vector.memset(carrier[:, z:z + 1], 0.0)
                line(nc.vector.bn_aggr(mv[:, z, :], six[:, z, :]))
                nc.vector.tensor_scalar(mv[:, z, 1:2], mv[:, z, 1:2], LN_EPS, None, ALU.add).then_inc(var_ready, 1)

            def norm(r, z):
                line = Line(dve, norm_line, r.at(1))
                dve.wait_ge(sd_ready, r.at(1, 1))
                line(nc.vector.reciprocal(rs[:, z, :], sd[:, z, :]))
                nc.vector.scalar_tensor_tensor(out=nm[:, z, :], in0=mv[:, z, 0:1], scalar=-1.0, in1=rs[:, z, :],
                                               op0=ALU.mult, op1=ALU.mult).then_inc(norm_ready, 1)

            def body(r, z):
                if r.m is not None or r.a + 1 < BLOCKS:
                    front(r.after(), 1 - z)
                norm(r, z)

            front(Round(None, 0), 0)
            rounds(dve, BLOCKS, body)

        @block.scalar
        def _(act):
            def deviation(r, z):
                act.wait_ge(var_ready, r.at(1, 1))
                nc.scalar.activation(sd[:, z, :], mv[:, z, 1:2], ACT.Sqrt).then_inc(sd_ready, 1)

            def body(r, z):
                if r.m is not None or r.a + 1 < BLOCKS:
                    deviation(r.after(), 1 - z)
                act.wait_ge(norm_ready, r.at(1, 1))
                rows = k.big2[:, bass.ds(r.at(D + 1), D)]
                nc.scalar.activation(rows, x[:, z, :], ACT.Relu, bias=nm[:, z, :], scale=rs[:, z, :]).then_inc(h_ready, 1)
                act.wait_ge(h_ready, r.at(1, 1))
                if r.has(2):
                    act.wait_ge(sq_ready, r.at(1, -1))
                nc.scalar.activation(junk[:, z, :], rows, ACT.Square,
                                     accum_out=k.big2[:, bass.ds(r.at(D + 1, D), 1)]).then_inc(sq_ready, 1)

            deviation(Round(None, 0), 0)
            rounds(act, BLOCKS, body)


def weights_by_step(nc, b, k):
    a = b.a
    with ExitStack() as ctx:
        sb, ps, sem = allocators(nc, ctx)
        wg = sb("w_gathered", [P, COLS, P])
        p_tr = ps("p_wtr", [P, P])
        table_out, gathered, turned, copied = sem("w_table_out"), sem("w_gathered_sem"), sem("w_turned"), sem("w_copied")
        block = ctx.enter_context(nc.Block())

        @block.sync
        def _(sp):
            sp.dma_start(b.wtp[0:TILES - 1, :],
                         a["edge_weight"][0:(TILES - 1) * P].rearrange("(t e) -> t e", e=P)).then_inc(table_out, 16)
            sp.dma_start(b.wtp[TILES - 1:TILES, :],
                         a["edge_weight"][E - P:E].rearrange("(o e) -> o e", o=1)).then_inc(table_out, 16)

        @block.gpsimd
        def _(pool):
            pool.wait_ge(table_out, 32)
            for c in range(COLS):
                pool.indirect_dma_start(out=wg[:, c, :], out_offset=None, in_=b.wtp,
                                        in_offset=bass.IndirectOffsetOnAxis(ap=k.tile_of[:, c:c + 1], axis=0))\
                    .then_inc(gathered, 16)

        @block.tensor
        def _(pe):
            pe.wait_ge(gathered, 16 * COLS)
            for c in range(COLS):
                if c:
                    pe.wait_ge(copied, c)
                nc.tensor.transpose(p_tr[:, :], wg[:, c, :], k.ident[:, :]).then_inc(turned, 1)

        @block.vector
        def _(dve):
            nc.vector.memset(k.big1[:, :], 0.0)
            for c in range(COLS):
                dve.wait_ge(turned, c + 1)
                nc.vector.tensor_copy(k.wt[:, c * P:(c + 1) * P], p_tr[:, :]).then_inc(copied, 1)


PAIRS = S // 2 - LAG
SCALED = {S // 2 + n: [2 * n, 2 * n + 1] for n in range(PAIRS)} | \
    {S // 2 + PAIRS + n: [2 * PAIRS + n] for n in range(S - 2 * PAIRS)}
SCALE_AT = {j: m for j, m in SCALED.items() if j < S}
LATE_SCALE_AT = {j - S: m for j, m in SCALED.items() if j >= S}
ROW_AT = {j + LAG: m for j, m in SCALED.items() if j + LAG < S}
LATE_ROW_AT = {j + LAG - S: m for j, m in SCALED.items() if j + LAG >= S}


def artanh_ratio_tail(nc, line, out, ln, isn, z, t, mask):
    V = nc.vector
    line.on(V.scalar_tensor_tensor(out=out, in0=ln, scalar=0.5, in1=isn, op0=ALU.mult, op1=ALU.mult))
    line(V.tensor_tensor(z, z, z, ALU.mult))
    line.on(V.tensor_scalar(mask, z, 1e-3, None, ALU.is_lt))
    line(V.tensor_scalar(t, z, 1.0 / 7, 1.0 / 5, ALU.mult, ALU.add))
    line(V.tensor_tensor(t, t, z, ALU.mult))
    line(V.scalar_tensor_tensor(out=t, in0=t, scalar=1.0 / 3, in1=z, op0=ALU.add, op1=ALU.mult))
    line(V.scalar_tensor_tensor(out=t, in0=t, scalar=1.0, in1=out, op0=ALU.add, op1=ALU.subtract))
    line(V.tensor_tensor(t, t, mask, ALU.mult))
    line(V.tensor_tensor(out, out, t, ALU.add))


def aggregate(nc, b, k):
    with ExitStack() as ctx:
        sb, ps, sem = allocators(nc, ctx)
        xs = sb("xs", [P, 2, S, D + 1])
        idx = sb("idx2", [P, 2, S], I32)
        carrier = sb("wait_carrier4", [1, S])
        wt = sb("wt_b", [P, 2, S])
        oh = sb("oh2", [P, 2, S, P])
        oht = sb("oht2", [P, 2, P])
        junk = sb("dot_junk", [P, 2, D])
        sqj = sb("sqj", [P, 2, D])
        xy = sb("xy", [P, 2, S])
        x2 = sb("x2", [P, 2, S])
        y2 = sb("y2", [P, 2, S])
        tmp = [sb(f"edge_t{i}", [P, S]) for i in range(18)]
        c2 = sb("c2_tab", [P, 2, S])
        ca, cb_, dn, bc, sn, zc, rat, ln, t, mask, lam, isn, bb, dd, zz, po, k1, k2 = [v[:, :] for v in tmp]
        p_x = ps("p_x2", [P, 2, 512])
        p_y = ps("p_y2", [P, 2, 512])
        p_sum = ps("p_sum2", [P, 4, 512])
        xs_in = [sem(f"xs_in{i}") for i in range(KV_SLOTS)]
        idx_ready, oh_ready = sem("idx2_ready"), sem("oh2_ready")
        turned, oht_ready, y_done, x2_done, y2_done = (
            sem(n) for n in ("turned2", "oht2_ready", "y2_mm", "x2_done", "y2_done"))
        sq_ready, sn_ready, rat_ready, ln_ready, c_ready = (
            sem(n) for n in ("n2_ready", "sn_ready", "rat_ready", "ln_ready", "c12_ready"))
        scaled_done, sum_done, add_done, line_sem = sem("rows_scaled"), sem("sum2_done"), sem("add2_done"), sem("edge_line")
        block = ctx.enter_context(nc.Block())
        NLINE = 37

        @block.gpsimd
        def _(pool):
            def body(r, z, here, prev, late):
                if not here:
                    return
                nc.gpsimd.tensor_copy(idx[:, z, :], k.src[:, bass.ds(r.at(S), S)]).then_inc(idx_ready, 1)
                nc.gpsimd.tensor_copy(wt[:, z, :], k.wt[:, bass.ds(r.at(S), S)]).then_inc(idx_ready, 1)
                pool.wait_ge(idx_ready, r.at(2, 2))
                for j in range(S):
                    slot = j % KV_SLOTS
                    if r.has(1) or j >= KV_SLOTS:
                        pool.wait_ge(x2_done, r.at(S, j + 1 - KV_SLOTS))
                        pool.wait_ge(y2_done, r.at(S, j + 1 - KV_SLOTS))
                    if r.has(2):
                        pool.wait_ge(sum_done, r.at(S, j + 1 - 2 * S))
                    nc.gpsimd.tensor_tensor(carrier[:, j:j + 1], k.iota[0:1, 0:1], k.iota[0:1, 0:1], ALU.add)
                    pool.indirect_dma_start(
                        out=xs[:, z, j, 0:D], out_offset=None, in_=b.h2,
                        in_offset=bass.IndirectOffsetOnAxis(ap=idx[:, z, j:j + 1], axis=0)).then_inc(xs_in[slot], 16)

            edge_rounds(pool, body)

        @block.tensor
        def _(pe):
            word = [None]

            def turn(r, z, j):
                if j % CHUNK == 0:
                    pe.wait_ge(oh_ready, r.at(S // CHUNK, j // CHUNK + 1))
                nc.tensor.transpose(p_x[:, j % 2, 0:P], oh[:, z, j, :], k.ident[:, :]).then_inc(turned, 1)

            def product(r, z, j):
                block_of = block_no(pe, k, r, j, word)
                if r.has(1) or j >= 2:
                    pe.wait_ge(x2_done, r.at(S, j - 1))
                pe.wait_ge(oht_ready, r.at(S, j + 1))
                nc.tensor.matmul(p_y[:, j % 2, 0:D + 1], oht[:, j % 2, :], k.big2[:, bass.ds(block_of * (D + 1), D + 1)],
                                 start=True, stop=True).then_inc(y_done, 1)

            def sums(p, y, i):
                if p.has(1) or i >= 4:
                    pe.wait_ge(add_done, p.at(S, i - 3))
                pe.wait_ge(scaled_done, p.at(S, i + 1))
                nc.tensor.matmul(p_sum[:, i % 4, 0:D + 1], oh[:, y, i, :], xs[:, y, i, :],
                                 start=True, stop=True).then_inc(sum_done, 1)

            def body(r, z, here, prev, late):
                p, y = r.before(), 1 - z
                for j in range(S):
                    if here and j == 0:
                        turn(r, z, 0)
                    if here and j + 1 < S:
                        turn(r, z, j + 1)
                    if here:
                        product(r, z, j)
                    for i in LATE_ROW_AT.get(j, ()) if late else ():
                        sums(p.before(), z, i)
                    for i in ROW_AT.get(j, ()) if prev else ():
                        sums(p, y, i)

            edge_rounds(pe, body)

        @block.scalar
        def _(act):
            def scale_row(p, y, i):
                if i == 0:
                    act.wait_ge(c_ready, p.at(2, 2))
                nc.scalar.activation(xs[:, y, i, 0:D], xs[:, y, i, 0:D], ACT.Copy, scale=c2[:, y, i:i + 1])\
                    .then_inc(scaled_done, 1)

            def body(r, z, here, prev, late):
                p, y = r.before(), 1 - z
                for j in range(S):
                    for i in ([0, 1] if j == 0 else [j + 1] if j + 1 < S else []) if here else ():
                        act.wait_ge(turned, r.at(S, i + 1))
                        if r.has(1) or i >= 2:
                            act.wait_ge(y_done, r.at(S, i - 1))
                        nc.scalar.copy(oht[:, i % 2, :], p_x[:, i % 2, 0:P]).then_inc(oht_ready, 1)
                    if here:
                        if r.has(1) or j >= 2:
                            act.wait_ge(y2_done, r.at(S, j - 1))
                        if j == 0 and r.has(2):
                            act.wait_ge(c_ready, r.at(2, -2))
                        act.wait_ge(xs_in[j % KV_SLOTS], r.at(16 * (S // KV_SLOTS), 16 * (j // KV_SLOTS + 1)))
                        nc.scalar.activation(sqj[:, j % 2, :], xs[:, z, j, 0:D], ACT.Square,
                                             accum_out=y2[:, z, j:j + 1]).then_inc(y2_done, 1)
                    if prev and j == 3:
                        act.wait_ge(sq_ready, p.at(1, 1))
                        nc.scalar.activation(sn, sn, ACT.Sqrt).then_inc(sn_ready, 1)
                    if prev and j == 5:
                        act.wait_ge(rat_ready, p.at(1, 1))
                        nc.scalar.activation(ln, rat, ACT.Ln).then_inc(ln_ready, 1)
                    for i in LATE_SCALE_AT.get(j, ()) if late else ():
                        scale_row(p.before(), z, i)
                    for i in SCALE_AT.get(j, ()) if prev else ():
                        scale_row(p, y, i)

            edge_rounds(act, body)

        @block.vector
        def _(dve):
            word = [None]
            V = nc.vector

            def dot(r, z, j):
                dve.wait_ge(xs_in[j % KV_SLOTS], r.at(16 * (S // KV_SLOTS), 16 * (j // KV_SLOTS + 1)))
                dve.wait_ge(y_done, r.at(S, j + 1))
                V.tensor_tensor_reduce(out=junk[:, j % 2, :], in0=p_y[:, j % 2, 0:D], in1=xs[:, z, j, 0:D], scale=1.0,
                                       scalar=0.0, op0=ALU.mult, op1=ALU.add, accum_out=xy[:, z, j:j + 1])
                V.tensor_copy(x2[:, z, j:j + 1], p_y[:, j % 2, D:D + 1]).then_inc(x2_done, 1)

            def coefficients(p, y, tick, line):
                w = wt[:, y, :]
                X2, Y2, XY = x2[:, y, :], y2[:, y, :], xy[:, y, :]
                on = line.on
                if tick == 0:
                    dve.wait_ge(x2_done, p.at(S, S))
                    dve.wait_ge(y2_done, p.at(S, S))
                    if p.has(1):
                        line.wait()
                    on(V.tensor_scalar(t, XY, -2.0, 1.0, ALU.mult, ALU.add))
                    on(V.tensor_scalar(bc, X2, -1.0, 1.0, ALU.mult, ALU.add))
                    on(V.tensor_tensor(dn, X2, Y2, ALU.mult))
                if tick == 1:
                    line.wait()
                    on(V.tensor_tensor(ca, t, Y2, ALU.add))
                    on(V.tensor_tensor(cb_, bc, XY, ALU.mult))
                    on(V.tensor_tensor(dn, dn, t, ALU.add))
                    on(V.tensor_scalar(lam, bc, MIN_NORM, None, ALU.max))
                    on(V.tensor_tensor(bb, bc, Y2, ALU.mult))
                if tick == 2:
                    line.wait()
                    on(V.tensor_tensor(sn, ca, X2, ALU.mult))
                    on(V.tensor_scalar(dn, dn, MIN_NORM, None, ALU.max))
                    on(V.reciprocal(lam, lam))
                    on(V.tensor_tensor(bb, bc, bb, ALU.mult))
                if tick == 3:
                    line.wait()
                    on(V.scalar_tensor_tensor(out=sn, in0=cb_, scalar=-2.0, in1=sn, op0=ALU.mult, op1=ALU.add))
                    on(V.reciprocal(dn, dn))
                    on(V.tensor_scalar(lam, lam, 2.0, MIN_NORM, ALU.mult, ALU.max))
                if tick == 4:
                    line.wait()
                    on(V.tensor_tensor(sn, sn, ca, ALU.mult))
                    on(V.tensor_tensor(dd, dn, dn, ALU.mult))
                    on(V.reciprocal(lam, lam))
                if tick == 5:
                    line.wait()
                    on(V.tensor_tensor(sn, sn, bb, ALU.add))
                    on(V.scalar_tensor_tensor(out=lam, in0=lam, scalar=2.0, in1=w, op0=ALU.mult, op1=ALU.mult))
                if tick == 6:
                    line.wait()
                    V.scalar_tensor_tensor(out=sn, in0=sn, scalar=0.0, in1=dd, op0=ALU.max, op1=ALU.mult)\
                        .then_inc(sq_ready, 1)
                    on(V.tensor_tensor(lam, lam, dn, ALU.mult))
                if tick == 7:
                    line.wait()
                    on(V.scalar_tensor_tensor(out=k1, in0=lam, scalar=-1.0, in1=ca, op0=ALU.mult, op1=ALU.mult))
                    on(V.tensor_tensor(k2, lam, bc, ALU.mult))
                if tick == 10:
                    dve.wait_ge(sn_ready, p.at(1, 1))
                    on(V.tensor_scalar(zc, sn, MIN_NORM, CLIP, ALU.max, ALU.min))
                    on(V.tensor_scalar(isn, sn, MIN_NORM, None, ALU.max))
                if tick == 11:
                    line.wait()
                    on(V.tensor_scalar(t, zc, -1.0, 1.0, ALU.mult, ALU.add))
                    on(V.reciprocal(isn, isn))
                    on(V.tensor_tensor(zz, zc, zc, ALU.mult))
                if tick == 12:
                    line.wait()
                    on(V.reciprocal(t, t))
                    on(V.tensor_scalar(po, zz, 1.0 / 7, 1.0 / 5, ALU.mult, ALU.add))
                    on(V.tensor_scalar(mask, zz, 1e-3, None, ALU.is_lt))
                if tick == 13:
                    line.wait()
                    V.scalar_tensor_tensor(out=rat, in0=zc, scalar=1.0, in1=t, op0=ALU.add, op1=ALU.mult)\
                        .then_inc(rat_ready, 1)
                    on(V.tensor_tensor(po, po, zz, ALU.mult))
                if tick == 14:
                    line.wait()
                    on(V.scalar_tensor_tensor(out=po, in0=po, scalar=1.0 / 3, in1=zz, op0=ALU.add, op1=ALU.mult))
                if tick == 16:
                    dve.wait_ge(ln_ready, p.at(1, 1))
                    line.wait()
                    on(V.scalar_tensor_tensor(out=rat, in0=ln, scalar=0.5, in1=isn, op0=ALU.mult, op1=ALU.mult))
                if tick == 17:
                    line.wait()
                    on(V.scalar_tensor_tensor(out=po, in0=po, scalar=1.0, in1=rat, op0=ALU.add, op1=ALU.subtract))
                if tick == 18:
                    line.wait()
                    on(V.tensor_tensor(po, po, mask, ALU.mult))
                if tick == 19:
                    line.wait()
                    on(V.tensor_tensor(rat, rat, po, ALU.add))
                if tick == 20:
                    line.wait()
                    V.tensor_tensor(xs[:, y, :, D], k1, rat, ALU.mult).then_inc(c_ready, 1)
                    V.tensor_tensor(c2[:, y, :], k2, rat, ALU.mult).then_inc(c_ready, 1)

            def one_hots(r, z, c):
                V.tensor_tensor(oh[:, z, c * CHUNK:(c + 1) * CHUNK, :],
                                k.iota[:, :].unsqueeze(1).to_broadcast([P, CHUNK, P]),
                                bcast(k.loc[:, bass.ds(r.at(S, c * CHUNK), CHUNK)], P), ALU.is_equal).then_inc(oh_ready, 1)

            def add(p, i):
                block_of = block_no(dve, k, p, i, word)
                to = k.big1[:, bass.ds(block_of * (D + 1), D + 1)]
                dve.wait_ge(sum_done, p.at(S, i + 1))
                if p.has(1) or i:
                    dve.wait_ge(add_done, p.at(S, i))
                V.tensor_tensor(to, p_sum[:, i % 4, 0:D + 1], to, ALU.add).then_inc(add_done, 1)

            def body(r, z, here, prev, late):
                p, y = r.before(), 1 - z
                line = Line(dve, line_sem, p.at(NLINE) if prev else 0)
                if here and not r.has(1):
                    one_hots(r, z, 0)
                for j in range(S):
                    adds = [(p.before(), i) for i in LATE_ROW_AT.get(j, ()) if late] + \
                        [(p, i) for i in ROW_AT.get(j, ()) if prev]
                    for q, i in adds[:1]:
                        add(q, i)
                    if prev:
                        coefficients(p, y, 3 * j, line)
                    if here:
                        dot(r, z, j)
                    for q, i in adds[1:]:
                        add(q, i)
                    if prev:
                        coefficients(p, y, 3 * j + 1, line)
                    c = j // CHUNK + 1
                    if here and j % CHUNK == 0 and c < S // CHUNK:
                        one_hots(r, z, c)
                    if here and j % CHUNK == 0 and c == S // CHUNK and (r.m is not None or r.a + 1 < BATCHES):
                        one_hots(r.after(), 1 - z, 0)
                    if prev:
                        coefficients(p, y, 3 * j + 2, line)
                assert not prev or line.n == NLINE, line.n

            edge_rounds(dve, body)


def hyperbolic_layer(nc, b, k, out):
    a = b.a
    with ExitStack() as ctx:
        sb, ps, sem = allocators(nc, ctx)
        w_rows = sb("w_rows", [P, HALF, D])
        wT = sb("w_turned_t", [P, HALF, D + 1])
        bias_col = sb("bias_col", [P, HALF])
        bias = sb("bias1", [P, D])
        ball = sb("ball", [P, D])
        junk = sb("junk5", [P, 2, D])
        junk2 = sb("junk6", [P, 2, D])
        part = sb("part", [P, 2, D])
        u = sb("u_blk", [P, 2, D])
        ut = sb("ut_blk", [P, 2, D])
        x1 = sb("x1_rows", [P, BLOCKS, D])
        tabs = {n: sb(f"t_{n}", [P, BLOCKS])[:, :] for n in
                ("n2", "xa", "u2", "m2", "h2", "t2", "a", "b", "c", "d", "e", "f", "g", "w", "v", "x2")}
        one = {n: sb(f"o_{n}", [P, 1])[:, :] for n in ("n2", "n", "th", "b2", "r")}
        p_w = ps("p_w", [P, 2, 512])
        p_wb = ps("p_wb", [P, HALF])
        p_ut = ps("p_ut", [P, 2, 512])
        p_m = ps("p_m", [P, 2, 512])
        V, A = nc.vector, nc.scalar
        x1_rows = x1[:, :, :].rearrange("p b d -> p (b d)")
        sums = k.big1[:, 0:BLOCKS * (D + 1)].rearrange("p (b c) -> p b c", c=D + 1)
        products = sums[:, :, D]
        rows_x2 = k.big2[:, :].rearrange("p (b c) -> p b c", c=D + 1)[:, :, D]

        def sums_of(r):
            return k.big1[:, bass.ds(r.at(D + 1), D)]

        def rows_of_block(r):
            return k.big2[:, bass.ds(r.at(D + 1), D)]

        def col(name, r):
            return tabs[name][:, bass.ds(r.at(1), 1)]

        def phase(name, engines):
            with ExitStack() as c:
                sems = {}

                def s(n):
                    if n not in sems:
                        sems[n] = c.enter_context(nc.semaphore(f"{name}_{n}"))
                    return sems[n]

                block = c.enter_context(nc.Block())
                for e, fn in engines.items():
                    engine = {"sync": block.sync, "vector": block.vector, "scalar": block.scalar,
                              "tensor": block.tensor}[e]
                    engine(lambda eng, fn=fn: fn(eng, s))

        def p1_dve(dve, s):
            def body(r, z):
                to = sums_of(r)
                V.scalar_tensor_tensor(out=to, in0=rows_of_block(r), scalar=k.big1[:, bass.ds(r.at(D + 1, D), 1)],
                                       in1=to, op0=ALU.mult, op1=ALU.add).then_inc(s("sum_whole"), 1)
                dve.wait_ge(s("sum_whole"), r.at(1, 1))
                if r.has(2):
                    dve.wait_ge(s("dotted"), r.at(1, -1))
                V.tensor_tensor(junk[:, z, :], to, rows_of_block(r), ALU.mult).then_inc(s("multiplied"), 1)
            rounds(dve, BLOCKS, body)

        def p1_act(act, s):
            def body(r, z):
                act.wait_ge(s("sum_whole"), r.at(1, 1))
                if r.has(2):
                    act.wait_ge(s("squared"), r.at(1, -1))
                A.activation(junk2[:, z, :], sums_of(r), ACT.Square, accum_out=col("n2", r)).then_inc(s("squared"), 1)
                act.wait_ge(s("multiplied"), r.at(1, 1))
                A.activation(junk[:, z, :], junk[:, z, :], ACT.Copy, accum_out=col("xa", r)).then_inc(s("dotted"), 1)
            rounds(act, BLOCKS, body)

        def p1_sp(sp, s):
            sp.dma_start(w_rows[:, :, :], a["L1_gnn_weight"].rearrange("(c p) n -> p c n", p=P)).then_inc(s("loads"), 16)
            sp.dma_start(bias[:, :], a["L1_gnn_bias"].partition_broadcast(P)).then_inc(s("loads"), 16)
            with nc.allow_non_contiguous_dma(reason="a bias value for each partition, once"):
                sp.dma_start(bias_col[:, :], a["L1_gnn_bias"].rearrange("(c p) -> p c", p=P)).then_inc(s("loads"), 16)
            full = (BLOCKS - 1) * P
            sp.dma_start(x1[:, 0:BLOCKS - 1, :], b.xs[0:full, :].rearrange("(b p) d -> p b d", p=P)).then_inc(s("loads"), 16)
            sp.dma_start(x1[0:TAIL, BLOCKS - 1, :], b.xs[full:N, :]).then_inc(s("loads"), 16)
            sp.wait_ge(s("loads"), 16 * 5)

        phase("sum_pass", {"sync": p1_sp, "vector": p1_dve, "scalar": p1_act})

        def q1_dve(dve, s):
            line = Line(dve, s("line"))
            T = tabs
            line(V.tensor_copy(T["x2"], rows_x2))
            dve.wait_ge(s("roots"), 1)
            line(V.tensor_scalar(T["a"], T["a"], MIN_NORM, None, ALU.max))
            line(V.tensor_scalar(T["b"], T["x2"], -1.0, 1.0, ALU.mult, ALU.add))
            line(V.tensor_scalar(T["c"], T["b"], MIN_NORM, None, ALU.max))
            line(V.reciprocal(T["c"], T["c"]))
            line(V.tensor_scalar(T["c"], T["c"], 2.0, MIN_NORM, ALU.mult, ALU.max))
            line(V.scalar_tensor_tensor(out=T["d"], in0=T["a"], scalar=0.5, in1=T["c"], op0=ALU.mult, op1=ALU.mult))
            V.reciprocal(T["c"], T["a"]).then_inc(s("tanh_arguments"), 1)
            dve.wait_ge(s("tanhs"), 1)
            dve.wait_ge(s("tanh_arguments"), 1)
            line(V.tensor_tensor(T["d"], T["d"], T["c"], ALU.mult))
            line(V.tensor_tensor(T["e"], T["d"], T["xa"], ALU.mult))
            line(V.tensor_tensor(T["f"], T["n2"], T["d"], ALU.mult))
            line(V.tensor_tensor(T["f"], T["f"], T["d"], ALU.mult))
            line(V.tensor_scalar(T["e"], T["e"], 2.0, 1.0, ALU.mult, ALU.add))
            line(V.tensor_tensor(T["g"], T["x2"], T["f"], ALU.mult))
            line(V.tensor_tensor(T["g"], T["g"], T["e"], ALU.add))
            line(V.tensor_scalar(T["g"], T["g"], MIN_NORM, None, ALU.max))
            line(V.reciprocal(T["g"], T["g"]))
            line(V.tensor_tensor(T["e"], T["e"], T["f"], ALU.add))
            line(V.tensor_tensor(T["v"], T["e"], T["g"], ALU.mult))
            line(V.tensor_tensor(T["b"], T["b"], T["g"], ALU.mult))
            line(V.tensor_tensor(T["w"], T["b"], T["d"], ALU.mult))
            dve.wait_ge(s("bias_norm"), 1)
            line(V.tensor_scalar(one["n"], one["n"], MIN_NORM, None, ALU.max))
            V.reciprocal(one["r"], one["n"]).then_inc(s("bias_norm_kept"), 1)
            dve.wait_ge(s("bias_tanh"), 1)
            dve.wait_ge(s("bias_norm_kept"), 1)
            line(V.tensor_tensor(one["r"], one["r"], one["th"], ALU.mult))
            line(V.tensor_scalar(ball[:, :], bias[:, :], one["r"], None, ALU.mult))
            line(V.tensor_tensor_reduce(out=junk[:, 0, :], in0=ball[:, :], in1=ball[:, :], scale=1.0, scalar=0.0,
                                        op0=ALU.mult, op1=ALU.add, accum_out=one["b2"]))
            V.tensor_scalar(bias_col[:, :], bias_col[:, :], one["r"], None, ALU.mult).then_inc(s("ball_col"), 1)
            for c in range(HALF):
                dve.wait_ge(s("weight_turned"), c + 1)
                line(V.tensor_copy(wT[:, c, 0:D], p_w[:, c, 0:D]))
            dve.wait_ge(s("weight_turned"), HALF + 1)
            line(V.tensor_copy(wT[:, :, D], p_wb[:, :]))

        def q1_act(act, s):
            line = Line(act, s("act_line"))
            line(A.activation(tabs["a"], tabs["n2"], ACT.Sqrt))
            A.activation(junk2[:, 0, :], bias[:, :], ACT.Square, accum_out=one["n2"]).then_inc(s("roots"), 1)
            act.wait_ge(s("roots"), 1)
            A.activation(one["n"], one["n2"], ACT.Sqrt).then_inc(s("bias_norm"), 1)
            act.wait_ge(s("tanh_arguments"), 1)
            A.activation(tabs["d"], tabs["d"], ACT.Tanh).then_inc(s("tanhs"), 1)
            act.wait_ge(s("bias_norm_kept"), 1)
            A.activation(one["th"], one["n"], ACT.Tanh).then_inc(s("bias_tanh"), 1)

        def q1_pe(pe, s):
            for c in range(HALF):
                for o in range(HALF):
                    last = nc.tensor.transpose(p_w[:, c, o * P:(o + 1) * P], w_rows[:, o, c * P:(c + 1) * P],
                                               k.ident[:, :])
                last.then_inc(s("weight_turned"), 1)
            pe.wait_ge(s("ball_col"), 1)
            for c in range(HALF):
                for o in range(HALF):
                    last = nc.tensor.matmul(p_wb[:, c:c + 1], w_rows[:, o, c * P:(c + 1) * P], bias_col[:, o:o + 1],
                                            start=o == 0, stop=o == HALF - 1)
            last.then_inc(s("weight_turned"), 1)

        phase("expmap", {"vector": q1_dve, "scalar": q1_act, "tensor": q1_pe})

        def p2_act(act, s):
            def scaled_row(r, z):
                if r.has(2):
                    act.wait_ge(s("u_ready"), r.at(1, -1))
                A.activation(part[:, z, :], rows_of_block(r), ACT.Copy, scale=col("v", r)).then_inc(s("part_ready"), 1)

            def product_norm(r, z):
                act.wait_ge(s("m_kept"), r.at(1, 1))
                act.wait_ge(s("squares"), r.at(2, 1))
                A.activation(junk2[:, 1, :], sums_of(r), ACT.Square, accum_out=col("m2", r)).then_inc(s("squares"), 1)

            def body(r, z):
                if r.m is not None or r.a + 1 < BLOCKS:
                    scaled_row(r.after(), 1 - z)
                act.wait_ge(s("u_ready"), r.at(1, 1))
                if r.has(1):
                    act.wait_ge(s("squares"), r.at(2, -1))
                A.activation(junk2[:, 0, :], u[:, z, :], ACT.Square, accum_out=col("u2", r)).then_inc(s("squares"), 1)
                if r.has(1):
                    product_norm(r.before(), 1 - z)

            scaled_row(Round(None, 0), 0)
            rounds(act, BLOCKS, body)
            product_norm(Round(None, BLOCKS - 1), 0)

        def p2_dve(dve, s):
            def keep_product(r, z):
                dve.wait_ge(s("m_ready"), r.at(1, 1))
                V.tensor_scalar(k.big1[:, bass.ds(r.at(D + 1), D + 1)], p_m[:, z, 0:D + 1], 1.0, None, ALU.mult)\
                    .then_inc(s("m_kept"), 1)

            def body(r, z):
                dve.wait_ge(s("part_ready"), r.at(1, 1))
                if r.has(2):
                    dve.wait_ge(s("u_turned"), r.at(1, -1))
                    dve.wait_ge(s("squares"), r.at(2, -3))
                V.scalar_tensor_tensor(out=u[:, z, :], in0=sums_of(r), scalar=col("w", r), in1=part[:, z, :],
                                       op0=ALU.mult, op1=ALU.add).then_inc(s("u_ready"), 1)
                if r.has(1):
                    keep_product(r.before(), 1 - z)
                dve.wait_ge(s("u_turned"), r.at(1, 1))
                V.tensor_scalar(ut[:, z, :], p_ut[:, z, 0:D], 1.0, None, ALU.mult).then_inc(s("ut_ready"), 1)

            rounds(dve, BLOCKS, body)
            keep_product(Round(None, BLOCKS - 1), 0)

        def p2_pe(pe, s):
            def turn(r, z):
                pe.wait_ge(s("u_ready"), r.at(1, 1))
                for c in range(HALF):
                    last = nc.tensor.transpose(p_ut[:, z, c * P:(c + 1) * P], u[:, z, c * P:(c + 1) * P], k.ident[:, :])
                last.then_inc(s("u_turned"), 1)

            def product(r, z):
                pe.wait_ge(s("ut_ready"), r.at(1, 1))
                if r.has(2):
                    pe.wait_ge(s("m_kept"), r.at(1, -1))
                for c in range(HALF):
                    last = nc.tensor.matmul(p_m[:, z, 0:D + 1], ut[:, z, c * P:(c + 1) * P], wT[:, c, :],
                                            start=c == 0, stop=c == HALF - 1)
                last.then_inc(s("m_ready"), 1)

            def body(r, z):
                turn(r, z)
                if r.has(1):
                    product(r.before(), 1 - z)

            rounds(pe, BLOCKS, body)
            product(Round(None, BLOCKS - 1), 0)

        phase("matvec", {"vector": p2_dve, "scalar": p2_act, "tensor": p2_pe})

        def q2_dve(dve, s):
            line = Line(dve, s("line"))
            T = tabs
            dve.wait_ge(s("roots"), 1)
            line(V.tensor_scalar(T["a"], T["a"], MIN_NORM, None, ALU.max))
            line(V.tensor_scalar(T["b"], T["b"], MIN_NORM, None, ALU.max))
            line(V.tensor_scalar(T["c"], T["a"], CLIP, None, ALU.min))
            line(V.tensor_scalar(T["d"], T["c"], -1.0, 1.0, ALU.mult, ALU.add))
            line(V.reciprocal(T["d"], T["d"]))
            V.scalar_tensor_tensor(out=T["d"], in0=T["c"], scalar=1.0, in1=T["d"], op0=ALU.add, op1=ALU.mult)\
                .then_inc(s("log_arguments"), 1)
            dve.wait_ge(s("logs"), 1)
            line(V.reciprocal(T["a"], T["a"]))
            artanh_ratio_tail(nc, line, T["f"], T["d"], T["a"], T["c"], T["e"], T["g"])
            V.tensor_tensor(T["f"], T["f"], T["b"], ALU.mult).then_inc(s("tanh_arguments"), 1)
            dve.wait_ge(s("tanhs"), 1)
            line(V.reciprocal(T["b"], T["b"]))
            line(V.tensor_tensor(T["f"], T["f"], T["b"], ALU.mult))
            line(V.tensor_tensor(T["c"], T["f"], T["m2"], ALU.mult))
            line(V.tensor_tensor(T["c"], T["f"], T["c"], ALU.mult))
            line(V.tensor_tensor(T["d"], T["f"], products, ALU.mult))
            line(V.tensor_scalar(T["d"], T["d"], 2.0, 1.0, ALU.mult, ALU.add))
            line(V.tensor_scalar(T["e"], T["c"], one["b2"], None, ALU.mult))
            line(V.tensor_tensor(T["e"], T["e"], T["d"], ALU.add))
            line(V.tensor_scalar(T["e"], T["e"], MIN_NORM, None, ALU.max))
            line(V.reciprocal(T["e"], T["e"]))
            line(V.tensor_scalar(T["d"], T["d"], one["b2"], None, ALU.add))
            line(V.tensor_tensor(T["d"], T["d"], T["f"], ALU.mult))
            line(V.tensor_tensor(T["v"], T["d"], T["e"], ALU.mult))
            line(V.tensor_scalar(T["c"], T["c"], -1.0, 1.0, ALU.mult, ALU.add))
            line(V.tensor_tensor(T["w"], T["c"], T["e"], ALU.mult))

        def q2_act(act, s):
            line = Line(act, s("act_line"))
            line(A.activation(tabs["a"], tabs["u2"], ACT.Sqrt))
            A.activation(tabs["b"], tabs["m2"], ACT.Sqrt).then_inc(s("roots"), 1)
            act.wait_ge(s("log_arguments"), 1)
            A.activation(tabs["d"], tabs["d"], ACT.Ln).then_inc(s("logs"), 1)
            act.wait_ge(s("tanh_arguments"), 1)
            A.activation(tabs["f"], tabs["f"], ACT.Tanh).then_inc(s("tanhs"), 1)

        phase("matvec_norms", {"vector": q2_dve, "scalar": q2_act})

        def p3_dve(dve, s):
            def body(r, z):
                if r.has(2):
                    dve.wait_ge(s("h_ready"), r.at(1, -1))
                V.tensor_scalar(part[:, z, :], ball[:, :], col("w", r), None, ALU.mult).then_inc(s("ball_part"), 1)
                dve.wait_ge(s("ball_part"), r.at(1, 1))
                V.scalar_tensor_tensor(out=sums_of(r), in0=sums_of(r), scalar=col("v", r), in1=part[:, z, :],
                                       op0=ALU.mult, op1=ALU.add).then_inc(s("h_ready"), 1)
            rounds(dve, BLOCKS, body)

        def p3_act(act, s):
            def body(r, z):
                act.wait_ge(s("h_ready"), r.at(1, 1))
                if r.has(2):
                    act.wait_ge(s("h_squared"), r.at(1, -1))
                A.activation(junk2[:, z, :], sums_of(r), ACT.Square, accum_out=col("h2", r)).then_inc(s("h_squared"), 1)
            rounds(act, BLOCKS, body)

        phase("ball_add", {"vector": p3_dve, "scalar": p3_act})

        def q3_dve(dve, s):
            line = Line(dve, s("line"))
            T = tabs
            dve.wait_ge(s("roots"), 1)
            line(V.tensor_scalar(T["a"], T["a"], MIN_NORM, None, ALU.max))
            line(V.tensor_scalar(T["c"], T["a"], CLIP, None, ALU.min))
            line(V.tensor_scalar(T["d"], T["c"], -1.0, 1.0, ALU.mult, ALU.add))
            line(V.reciprocal(T["d"], T["d"]))
            V.scalar_tensor_tensor(out=T["d"], in0=T["c"], scalar=1.0, in1=T["d"], op0=ALU.add, op1=ALU.mult)\
                .then_inc(s("log_arguments"), 1)
            dve.wait_ge(s("logs"), 1)
            line(V.reciprocal(T["a"], T["a"]))
            artanh_ratio_tail(nc, line, T["f"], T["d"], T["a"], T["c"], T["e"], T["g"])

        def q3_act(act, s):
            A.activation(tabs["a"], tabs["h2"], ACT.Sqrt).then_inc(s("roots"), 1)
            act.wait_ge(s("log_arguments"), 1)
            A.activation(tabs["d"], tabs["d"], ACT.Ln).then_inc(s("logs"), 1)

        phase("logmap", {"vector": q3_dve, "scalar": q3_act})

        def p4_dve(dve, s):
            def body(r, z):
                V.tensor_scalar(sums_of(r), sums_of(r), col("f", r), 0.0, ALU.mult, ALU.max).then_inc(s("t_ready"), 1)
            rounds(dve, BLOCKS, body)

        def p4_act(act, s):
            def body(r, z):
                act.wait_ge(s("t_ready"), r.at(1, 1))
                if r.has(2):
                    act.wait_ge(s("t_squared"), r.at(1, -1))
                A.activation(junk2[:, z, :], sums_of(r), ACT.Square, accum_out=col("t2", r)).then_inc(s("t_squared"), 1)
            rounds(act, BLOCKS, body)

        phase("tangent", {"vector": p4_dve, "scalar": p4_act})

        def q4_dve(dve, s):
            line = Line(dve, s("line"))
            T = tabs
            top = 1.0 - BALL_EPS
            dve.wait_ge(s("roots"), 1)
            line(V.tensor_scalar(T["a"], T["a"], MIN_NORM, None, ALU.max))
            V.reciprocal(T["b"], T["a"]).then_inc(s("norms_inverted"), 1)
            dve.wait_ge(s("tanhs"), 1)
            dve.wait_ge(s("norms_inverted"), 1)
            line(V.tensor_tensor(T["v"], T["c"], T["b"], ALU.mult))
            line(V.tensor_scalar(T["d"], T["t2"], 0.0, None, ALU.is_gt))
            line(V.tensor_tensor(T["c"], T["c"], T["d"], ALU.mult))
            line(V.tensor_scalar(T["c"], T["c"], top, None, ALU.max))
            line(V.reciprocal(T["c"], T["c"]))
            line(V.tensor_scalar(T["c"], T["c"], top, None, ALU.mult))
            line(V.tensor_tensor(T["v"], T["v"], T["c"], ALU.mult))

        def q4_act(act, s):
            A.activation(tabs["a"], tabs["t2"], ACT.Sqrt).then_inc(s("roots"), 1)
            act.wait_ge(s("norms_inverted"), 1)
            A.activation(tabs["c"], tabs["a"], ACT.Tanh).then_inc(s("tanhs"), 1)

        phase("project", {"vector": q4_dve, "scalar": q4_act})

        def p5_sp(sp, s):
            for g in range(BLOCKS // GROUP):
                at, to = g * GROUP, min((g + 1) * GROUP, BLOCKS - 1)
                sp.wait_ge(s("done"), (g + 1) * GROUP)
                sp.dma_start(out[at * P:to * P, :].rearrange("(b p) d -> p b d", p=P), x1[:, at:to, :])\
                    .then_inc(s("out"), 16)
            sp.dma_start(out[(BLOCKS - 1) * P:N, :], x1[0:TAIL, BLOCKS - 1, :]).then_inc(s("out"), 16)
            sp.wait_ge(s("out"), 16 * (BLOCKS // GROUP + 1))

        def p5_dve(dve, s):
            def body(r, z):
                n = rows_of(r)
                rows = x1_rows[0:n, bass.ds(r.at(D), D)]
                V.scalar_tensor_tensor(out=rows, in0=sums_of(r)[0:n, :], scalar=col("v", r)[0:n, :], in1=rows,
                                       op0=ALU.mult, op1=ALU.add).then_inc(s("done"), 1)
            rounds(dve, BLOCKS, body)

        phase("result", {"sync": p5_sp, "vector": p5_dve})


class Keep:
    pass


def program(nc, a, out):
    b = Build(nc, a)
    k = Keep()
    with ExitStack() as ctx:
        sb, _, _ = allocators(nc, ctx)
        k.iota = sb("iota", [P, P])
        k.ident = sb("ident", [P, P])
        k.of_step = sb("of_step", [P, S])
        k.of_head = sb("of_head", [P, H])
        k.head_of = sb("head_of", [H, P])
        k.loc = sb("loc_tab", [P, SPAD])
        k.tile_of = sb("tile_of_i", [P, COLS], I32)
        k.src = sb("src_tab", [P, SPAD], I32)
        k.chain = sb("chain_tab", [H, BATCHES * CH])
        k.straddler = sb("straddler", [H, BATCHES])
        k.row = sb("row_tab", [1, SPAD], I32)
        k.packed = sb("packed_tab", [1, SPAD // PACK], I32)
        k.big1 = sb("node_sums", [P, BLOCKS * H * CE])
        k.big2 = sb("node_rows", [P, BLOCKS * (D + 1)])
        prep(nc, b, k)
        project_nodes(nc, b, k)
        attend(nc, b, k)
        finish_attention(nc, b, k)
        k.wt = sb("wt_tab", [P, SPAD])
        weights_by_step(nc, b, k)
        aggregate(nc, b, k)
        hyperbolic_layer(nc, b, k, out)


_INS = ["x", "src", "dst", "edge_attr_256", "edge_weight",
        "L0_gnn_Wq", "L0_gnn_bq", "L0_gnn_Wk", "L0_gnn_bk", "L0_gnn_Wv", "L0_gnn_bv", "L0_gnn_We",
        "L0_gnn_Ws", "L0_gnn_bs", "L1_gnn_weight", "L1_gnn_bias"]


def kernel(**inputs):
    import numpy as _np
    import concourse.bacc as _bacc
    from concourse import mybir as _mybir
    from concourse.bass_utils import run_bass_kernel_spmd as _run

    nc = _bacc.Bacc("TRN2", target_bir_lowering=False, num_devices=1)
    arrays, args = {}, {}
    for name in _INS:
        x = _np.ascontiguousarray(inputs[name])
        arrays[f"in_{name}"] = x
        args[name] = nc.dram_tensor(f"in_{name}", x.shape, _mybir.dt.from_np(x.dtype), kind="ExternalInput").ap()
    out = nc.dram_tensor("out_rows", (N, D), F32, kind="ExternalOutput").ap()
    program(nc, args, out)
    r = _run(nc, [arrays], core_ids=[0])
    return r.results[0]["out_rows"]
```
